# Optimizing a Trainium2 kernel written in Bass

```python
import numpy as np
import jax
import jax.numpy as jnp

def _softmax(x, axis=-1):
    return jax.nn.softmax(x, axis=axis)

def _gelu(x):
    return jax.nn.gelu(x, approximate=True)

def _silu(x):
    return jax.nn.silu(x)

def _sigmoid(x):
    return jax.nn.sigmoid(x)

def _layernorm(x, axis=-1, eps=1e-05):
    m = jnp.mean(x, axis=axis, keepdims=True)
    v = jnp.var(x, axis=axis, keepdims=True)
    return (x - m) / jnp.sqrt(v + eps)

def _scatter_add(tgt, idx, src, axis=0):
    return tgt.at[idx].add(src)

def _segment_sum(src, seg, n):
    return jax.ops.segment_sum(src, seg, n)
kernel_name = 'mk_gps_d1_gnn_r32_5451c4'

def setup_inputs(seed: int=0):
    np.random.seed(seed)
    _w = jnp.asarray

    def _rec_inputs():
        import jax
        import jax.numpy as jnp
        _gk = jax.random.key(seed)
        x = -6.415e-05 + 1 * jax.random.normal(jax.random.fold_in(_gk, 1), (625, 512), jnp.float32)
        _s = jax.random.randint(jax.random.fold_in(_gk, 2), (5000,), 0, 625, jnp.int32)
        _d = jax.random.randint(jax.random.fold_in(_gk, 3), (5000,), 0, 625, jnp.int32)
        _loop = jnp.arange(625, dtype=jnp.int32)
        src = jnp.concatenate([_s, _d, _loop])
        dst = jnp.concatenate([_d, _s, _loop])
        _o = jnp.argsort(dst, stable=True)
        src = src[_o]
        dst = dst[_o]
        return (x, src, dst)
    x, src, dst = _rec_inputs()

    def _L0_gnn_setup():
        import jax, jax.numpy as jnp
        import numpy as np
        N_NODES = 625
        N_EDGES = 10000
        D_IN = 512
        D_HID = 512
        EPS = 1e-05

        def _xavier(key, shape):
            fan_in, fan_out = (shape[1], shape[0])
            limit = np.sqrt(6.0 / (fan_in + fan_out)).astype(np.float32)
            return jax.random.uniform(key, shape, jnp.float32, -limit, limit)

        def _sage_conv(h, src, dst, Wl, bl, Wr):
            msg = h[src]
            s = jax.ops.segment_sum(msg, dst, num_segments=N_NODES)
            cnt = jax.ops.segment_sum(jnp.ones((src.shape[0], 1), h.dtype), dst, num_segments=N_NODES)
            agg = s / jnp.maximum(cnt, 1.0)
            return agg @ Wl.T + bl + h @ Wr.T

        def _layer_norm(h, g, b):
            mu = jnp.mean(h, axis=-1, keepdims=True)
            var = jnp.mean((h - mu) ** 2, axis=-1, keepdims=True)
            return (h - mu) * jax.lax.rsqrt(var + EPS) * g + b

        def _prelu(h, a):
            return jnp.where(h >= 0, h, a * h)
        key = jax.random.key(seed)
        ks = jax.random.split(key, 16)
        x = jax.random.normal(ks[0], (N_NODES, D_IN), jnp.float32)
        edge_index = jax.random.randint(ks[1], (2, N_EDGES), 0, N_NODES, jnp.int64)
        dims = [(D_IN, D_HID), (D_HID, D_HID), (D_HID, D_HID)]
        inp = {'x': x, 'edge_index': edge_index}
        for i, (din, dout) in enumerate(dims):
            inp[f'Wl{i}'] = _xavier(ks[2 + 3 * i], (dout, din))
            inp[f'bl{i}'] = jnp.zeros((dout,), jnp.float32)
            inp[f'Wr{i}'] = _xavier(ks[3 + 3 * i], (dout, din))
            inp[f'g{i}'] = jnp.ones((dout,), jnp.float32)
            inp[f'b{i}'] = jnp.zeros((dout,), jnp.float32)
        inp['a_prelu'] = jnp.full((1,), 0.25, jnp.float32)
        return inp
    _L0_gnn_all = _L0_gnn_setup()
    _L0_gnn_in = {k: v for k, v in _L0_gnn_all.items() if k in ('Wl0', 'bl0', 'Wr0', 'g0', 'b0', 'Wl1', 'bl1', 'Wr1', 'g1', 'b1', 'Wl2', 'bl2', 'Wr2', 'g2', 'b2', 'a_prelu')}
    del _L0_gnn_all

    def _L0_mix_setup():
        import jax, jax.numpy as jnp
        import numpy as np
        DIM = 512
        H = 8
        C = 64
        HID = H * C
        NMEM = H

        def _rmsnorm_seq(x, w):
            n = jnp.sqrt(jnp.sum(x * x, axis=2, keepdims=True))
            return x / jnp.maximum(n, 1e-12) * w * jnp.asarray(DIM ** 0.5, x.dtype)
        key = jax.random.key(seed)
        ks = jax.random.split(key, 7)
        b, n = (4, 128)
        x = jax.random.normal(ks[0], (b, n, DIM), dtype=jnp.float32)
        norm_w = jnp.ones((1, 1, DIM), dtype=jnp.float32)
        w_qkv = jax.random.normal(ks[1], (DIM, 3 * HID), dtype=jnp.float32) / np.sqrt(DIM)
        mem_kv = jax.random.normal(ks[2], (2, H, C, NMEM), dtype=jnp.float32)
        w_out = jax.random.normal(ks[3], (HID, DIM), dtype=jnp.float32) / np.sqrt(HID)
        b_out = jax.random.normal(ks[4], (DIM,), dtype=jnp.float32) * 0.01
        out_norm_w = jnp.ones((1, 1, DIM), dtype=jnp.float32)
        return {'x': x, 'norm_w': norm_w, 'w_qkv': w_qkv, 'mem_kv': mem_kv, 'w_out': w_out, 'b_out': b_out, 'out_norm_w': out_norm_w}
    _L0_mix_all = _L0_mix_setup()
    _L0_mix_in = {k: v for k, v in _L0_mix_all.items() if k in ('norm_w', 'w_qkv', 'mem_kv', 'w_out', 'b_out', 'out_norm_w')}
    del _L0_mix_all

    def _L0_ffn_setup():
        import jax, jax.numpy as jnp
        import numpy as np
        B, T, D = (4, 512, 512)
        N = 128
        key = jax.random.key(seed)
        ks = jax.random.split(key, 6)
        x = jax.random.normal(ks[0], (B, T, D), dtype=jnp.float32)
        positions = jax.random.normal(ks[1], (N, D), dtype=jnp.float32) * 0.1
        scales = jnp.ones((N,), dtype=jnp.float32) * 10.0
        value_weight = jax.random.normal(ks[2], (N, D, D), dtype=jnp.float32) * 0.02
        out_W = jax.random.normal(ks[3], (D, D), dtype=jnp.float32) * (1.0 / np.sqrt(D))
        out_b = jax.random.normal(ks[4], (D,), dtype=jnp.float32) * 0.01
        return {'x': x, 'positions': positions, 'scales': scales, 'value_weight': value_weight, 'out_W': out_W, 'out_b': out_b}
    _L0_ffn_all = _L0_ffn_setup()
    _L0_ffn_in = {k: v for k, v in _L0_ffn_all.items() if k in ('positions', 'scales', 'value_weight', 'out_W', 'out_b')}
    del _L0_ffn_all
    return {'x': x, 'src': src, 'dst': dst, 'L0_gnn_Wl0': _L0_gnn_in['Wl0'], 'L0_gnn_bl0': _L0_gnn_in['bl0'], 'L0_gnn_Wr0': _L0_gnn_in['Wr0'], 'L0_gnn_g0': _L0_gnn_in['g0'], 'L0_gnn_b0': _L0_gnn_in['b0'], 'L0_gnn_Wl1': _L0_gnn_in['Wl1'], 'L0_gnn_bl1': _L0_gnn_in['bl1'], 'L0_gnn_Wr1': _L0_gnn_in['Wr1'], 'L0_gnn_g1': _L0_gnn_in['g1'], 'L0_gnn_b1': _L0_gnn_in['b1'], 'L0_gnn_Wl2': _L0_gnn_in['Wl2'], 'L0_gnn_bl2': _L0_gnn_in['bl2'], 'L0_gnn_Wr2': _L0_gnn_in['Wr2'], 'L0_gnn_g2': _L0_gnn_in['g2'], 'L0_gnn_b2': _L0_gnn_in['b2'], 'L0_gnn_a_prelu': _L0_gnn_in['a_prelu'], 'L0_mix_norm_w': _L0_mix_in['norm_w'], 'L0_mix_w_qkv': _L0_mix_in['w_qkv'], 'L0_mix_mem_kv': _L0_mix_in['mem_kv'], 'L0_mix_w_out': _L0_mix_in['w_out'], 'L0_mix_b_out': _L0_mix_in['b_out'], 'L0_mix_out_norm_w': _L0_mix_in['out_norm_w'], 'L0_ffn_positions': _L0_ffn_in['positions'], 'L0_ffn_scales': _L0_ffn_in['scales'], 'L0_ffn_value_weight': _L0_ffn_in['value_weight'], 'L0_ffn_out_W': _L0_ffn_in['out_W'], 'L0_ffn_out_b': _L0_ffn_in['out_b']}

def reference(x, src, dst, L0_gnn_Wl0, L0_gnn_bl0, L0_gnn_Wr0, L0_gnn_g0, L0_gnn_b0, L0_gnn_Wl1, L0_gnn_bl1, L0_gnn_Wr1, L0_gnn_g1, L0_gnn_b1, L0_gnn_Wl2, L0_gnn_bl2, L0_gnn_Wr2, L0_gnn_g2, L0_gnn_b2, L0_gnn_a_prelu, L0_mix_norm_w, L0_mix_w_qkv, L0_mix_mem_kv, L0_mix_w_out, L0_mix_b_out, L0_mix_out_norm_w, L0_ffn_positions, L0_ffn_scales, L0_ffn_value_weight, L0_ffn_out_W, L0_ffn_out_b):
    import jax
    import jax.numpy as jnp

    def _L0_gnn_ref(x, edge_index, Wl0, bl0, Wr0, g0, b0, Wl1, bl1, Wr1, g1, b1, Wl2, bl2, Wr2, g2, b2, a_prelu):
        import jax, jax.numpy as jnp
        import numpy as np
        N_NODES = 625
        N_EDGES = 10000
        D_IN = 512
        D_HID = 512
        EPS = 1e-05

        def _xavier(key, shape):
            fan_in, fan_out = (shape[1], shape[0])
            limit = np.sqrt(6.0 / (fan_in + fan_out)).astype(np.float32)
            return jax.random.uniform(key, shape, jnp.float32, -limit, limit)

        def _sage_conv(h, src, dst, Wl, bl, Wr):
            msg = h[src]
            s = jax.ops.segment_sum(msg, dst, num_segments=N_NODES)
            cnt = jax.ops.segment_sum(jnp.ones((src.shape[0], 1), h.dtype), dst, num_segments=N_NODES)
            agg = s / jnp.maximum(cnt, 1.0)
            return agg @ Wl.T + bl + h @ Wr.T

        def _layer_norm(h, g, b):
            mu = jnp.mean(h, axis=-1, keepdims=True)
            var = jnp.mean((h - mu) ** 2, axis=-1, keepdims=True)
            return (h - mu) * jax.lax.rsqrt(var + EPS) * g + b

        def _prelu(h, a):
            return jnp.where(h >= 0, h, a * h)
        src, dst = (edge_index[0], edge_index[1])
        params = [(Wl0, bl0, Wr0, g0, b0), (Wl1, bl1, Wr1, g1, b1), (Wl2, bl2, Wr2, g2, b2)]
        h = x
        residual = 0.0
        for Wl, bl, Wr, g, b in params:
            h = residual + _sage_conv(h, src, dst, Wl, bl, Wr)
            h = _layer_norm(h, g, b)
            h = _prelu(h, a_prelu)
            residual = h
        return h

    def _L0_mix_ref(x, norm_w, w_qkv, mem_kv, w_out, b_out, out_norm_w):
        import jax, jax.numpy as jnp
        import numpy as np
        DIM = 512
        H = 8
        C = 64
        HID = H * C
        NMEM = H

        def _rmsnorm_seq(x, w):
            n = jnp.sqrt(jnp.sum(x * x, axis=2, keepdims=True))
            return x / jnp.maximum(n, 1e-12) * w * jnp.asarray(DIM ** 0.5, x.dtype)
        b, n, _ = x.shape
        scale = jnp.asarray(C ** (-0.5), x.dtype)
        xn = _rmsnorm_seq(x, norm_w)
        qkv = xn @ w_qkv
        q, k, v = jnp.split(qkv, 3, axis=2)

        def to_heads(t):
            return t.reshape(b, n, H, C).transpose(0, 2, 3, 1)
        q, k, v = map(to_heads, (q, k, v))
        mk = jnp.broadcast_to(mem_kv[0], (b, H, C, NMEM))
        mv = jnp.broadcast_to(mem_kv[1], (b, H, C, NMEM))
        k = jnp.concatenate([mk, k], axis=-1)
        v = jnp.concatenate([mv, v], axis=-1)
        q = jax.nn.softmax(q, axis=-2) * scale
        k = jax.nn.softmax(k, axis=-1)
        context = jnp.einsum('bhdn,bhen->bhde', k, v)
        out = jnp.einsum('bhde,bhdn->bhen', context, q)
        out = out.transpose(0, 3, 1, 2).reshape(b, n, HID)
        out = out @ w_out + b_out
        return _rmsnorm_seq(out, out_norm_w)

    def _L0_ffn_ref(x, positions, scales, value_weight, out_W, out_b):
        import jax, jax.numpy as jnp
        import numpy as np
        B, T, D = (4, 512, 512)
        N = 128
        diff = x[:, :, None, :] - positions[None, None, :, :]
        distances = jnp.linalg.norm(diff, axis=-1)
        interactions = scales / (distances + 0.1)
        attn = jax.nn.softmax(interactions, axis=-1)
        out = jnp.einsum('btn,btd,nde->bte', attn, x, value_weight)
        return out @ out_W.T + out_b
    edge_index = jnp.stack([src, dst])
    xn = _layernorm(x, axis=-1)
    x = x + _L0_gnn_ref(xn, edge_index, L0_gnn_Wl0, L0_gnn_bl0, L0_gnn_Wr0, L0_gnn_g0, L0_gnn_b0, L0_gnn_Wl1, L0_gnn_bl1, L0_gnn_Wr1, L0_gnn_g1, L0_gnn_b1, L0_gnn_Wl2, L0_gnn_bl2, L0_gnn_Wr2, L0_gnn_g2, L0_gnn_b2, L0_gnn_a_prelu) + _L0_mix_ref(xn[None], L0_mix_norm_w, L0_mix_w_qkv, L0_mix_mem_kv, L0_mix_w_out, L0_mix_b_out, L0_mix_out_norm_w)[0]
    x = x + _L0_ffn_ref(_layernorm(x, axis=-1)[None], L0_ffn_positions, L0_ffn_scales, L0_ffn_value_weight, L0_ffn_out_W, L0_ffn_out_b)[0]
    return x

_drawn_inputs = setup_inputs


def setup_inputs(seed=0):
    import zlib

    import numpy as np

    out = dict(_drawn_inputs(seed))
    spreads = {'L0_gnn_bl0': (0.0, 0.1),
     'L0_gnn_g0': (1.0, 0.2),
     'L0_gnn_b0': (0.0, 0.1),
     'L0_gnn_bl1': (0.0, 0.1),
     'L0_gnn_g1': (1.0, 0.2),
     'L0_gnn_b1': (0.0, 0.1),
     'L0_gnn_bl2': (0.0, 0.1),
     'L0_gnn_g2': (1.0, 0.2),
     'L0_gnn_b2': (0.0, 0.1),
     'L0_mix_norm_w': (1.0, 0.2),
     'L0_mix_out_norm_w': (1.0, 0.2),
     'L0_ffn_scales': (10.0, 0.6)}
    factors = {'L0_ffn_positions': 8.0, 'L0_ffn_out_b': 8.0}
    for name, (base, spread) in spreads.items():
        noise = np.random.default_rng([zlib.crc32(name.encode()), seed]).standard_normal(out[name].shape)
        drawn = base * np.exp(spread * noise) if base else spread * noise
        out[name] = jnp.asarray(drawn.astype(out[name].dtype))
    for name, factor in factors.items():
        out[name] = (out[name] * factor).astype(out[name].dtype)
    return out
```

```python
from contextlib import ExitStack

import concourse.bass as bass
from concourse import mybir

F32 = mybir.dt.float32
F32R = mybir.dt.float32r
BF16 = mybir.dt.bfloat16
I16 = mybir.dt.int16
I32 = mybir.dt.int32
ALU = mybir.AluOpType
ACT = mybir.ActivationFunctionType
AX = mybir.AxisListType


def gps_kernel(nc, x, src, dst, gnn_w, gnn_rows, a_prelu, norm_w, w_qkv, mem_k, mem_v, w_out, b_out,
               out_norm_w, pos_t, scales, value_w, out_wt, out_b, out):
    NODES, D = x.shape
    TP = 125
    T = NODES // TP
    TW = TP + 1
    TT = T * TW
    SA = 3 * TW
    SB = TT - SA
    K = D // 128
    EDGES = src.shape[0]
    EC = EDGES // TP
    OHW = 128
    OHR = 5
    HEADS, C = 8, 64
    J = HEADS // 2
    NMEM = mem_v.shape[0]
    LAYERS = len(gnn_rows)
    EXPERTS = value_w.shape[0]
    U = 4
    LN_EPS = 1e-5
    RMS_EPS = 1e-12
    ROOT_D = float(D) ** 0.5
    Q_SCALE = float(C) ** -0.5

    stage_k, stage_v, stage_q, stage_o = range(4)

    def stage_r(l):
        return 4 + 2 * l

    def stage_l(l):
        return 5 + 2 * l

    PRE = 4 + 2 * LAYERS
    stage_out = PRE + EXPERTS
    kp = "(p k) n -> p k n"
    stage_src = {
        stage_k: w_qkv[:, D:2 * D].rearrange(kp, k=K),
        stage_v: w_qkv[:, 2 * D:3 * D].rearrange(kp, k=K),
        stage_q: w_qkv[:, 0:D].rearrange(kp, k=K),
        stage_o: w_out.rearrange("(j p) n -> p j n", p=128),
        stage_out: out_wt.rearrange(kp, k=K),
    }
    for l in range(LAYERS):
        stage_l_t, stage_r_t = gnn_w[l]
        stage_src[stage_r(l)] = stage_r_t.rearrange(kp, k=K)
        stage_src[stage_l(l)] = stage_l_t.rearrange(kp, k=K)

    def raw_slot(s):
        return s % 2 if s < PRE else (s - PRE) % U

    def raw_loads(s):
        if s < PRE:
            return s // 2 + 1
        return (PRE // 2 if raw_slot(s) < 2 else 0) + (s - PRE) // U + 1

    JOBS = [("xrT", i) for i in range(T)]
    for j in range(J):
        JOBS += [("kTa", j), ("kTb", j)]
    JOBS += [("v", i) for i in range(T)]
    JOBS += [("kN", i) for i in range(T)] + [("kM", 0)]
    JOBS += [("q", 0), ("q", 1), ("ctx", 0)] + [("q", i) for i in range(2, T)]
    JOBS += [("qT", i) for i in range(T)]
    for j in range(J):
        JOBS += [("oTa", j), ("oTb", j)]
    JOBS += [("mo", i) for i in range(T)] + [("p2", 0)]
    JOBS += [("hT", 0, i) for i in range(T)]
    for l in range(LAYERS):
        JOBS += [("sT", l, b) for b in range(K + K // 2)]
        if l > 0:
            JOBS += [("hT", l, T - 1)]
        nxt = [("hT", l + 1, i) if l + 1 < LAYERS else ("x2T", i) for i in range(T)]
        for i in range(T):
            JOBS += [("z", l, i)]
            if i >= 1:
                JOBS += [nxt[i - 1]]
    JOBS += [("d", 0), ("x2T", T - 1), ("d", 1)]
    NJ = len(JOBS)
    JOB = {name: n for n, name in enumerate(JOBS)}
    BANKS = 8
    BW = 512

    def after(*name):
        return JOB[name] + 1

    SPLIT = [n for n in JOBS if n[0] in ("xrT", "v", "kN", "qT", "oTa", "oTb", "hT", "sT", "x2T")]

    def hi_after(*name):
        return SPLIT.index(name) + 1

    def ln_index(group, i):
        if group < LAYERS:
            return group * T + i
        return LAYERS * T + 2 * i + group - LAYERS

    NLN = (LAYERS + 2) * T

    ctx = ExitStack()
    with ctx:
        def sb(name, shape, dt=F32, stack=ctx):
            return stack.enter_context(nc.sbuf_tensor(name, shape, dt))

        def sem(name):
            return ctx.enter_context(nc.semaphore(name))

        ident = sb("ident", [128, 128])
        ones = sb("ones", [128, 128])
        iota = sb("iota", [128, T * OHW], I16)
        zeros = sb("zeros", [128, BW], BF16)
        src_i = sb("src_i", [TP, EC], I32)
        dst_i = sb("dst_i", [TP, EC], I32)
        src_f = sb("src_f", [TP, EC])
        dst_f = sb("dst_f", [TP, EC])
        work = sb("work", [128, OHR * 2 * T * OHW], BF16)
        onehot = work[:, :].rearrange("p (u s n) -> p u s n", u=OHR, s=2)
        workf = work[:, :].bitcast(F32)
        counts = workf.rearrange("p (t n) -> p t n", t=T)

        def scratch(n):
            return workf[:, n * BW:(n + 1) * BW]

        ctx_f = scratch(2).rearrange("p (j e) -> p j e", j=J)
        act_dump = scratch(3)
        pos_sq = scratch(4).rearrange("p (k n) -> p k n", k=K)
        recip_cnt = sb("recip_cnt", [128, TT])
        attn_t = sb("attn", [TP, T, EXPERTS])
        h = sb("h", [TP, T, D])
        xm_t = sb("xm", [128, T * BW])
        xm = xm_t[0:TP, :].rearrange("p (t n) -> p t n", t=T)
        k_exp = xm_t[:, 0:J * TT].rearrange("p (j n) -> p j n", j=J)
        R = [[sb(f"r{n}_{part}", [128, T * BW], F32R) for part in ("hi", "lo")] for n in range(3)]

        def cols(n):
            return [a[:, 0:K * TT].rearrange("p (k n) -> p k n", k=K) for a in R[n]]

        def rows(n):
            return [a[0:TP, :].rearrange("p (t n) -> p t n", t=T) for a in R[n]]

        xr_c, s_c, x2_c = cols(0), cols(0), cols(0)
        kn_r, q_c, h_r = rows(1), cols(1), rows(1)
        v_r, o_c, h_c = rows(2), cols(2), cols(2)
        acc_c = cols(1)
        pos_hl = [a[:, 0:K * EXPERTS].rearrange("p (k n) -> p k n", k=K) for a in R[2]]
        split_w = [[sb(f"w{n}_{part}", [128, K, D], F32R) for part in ("hi", "lo")] for n in range(2)]
        layer_rows = sb("layer_rows", [TP, 2, 3, D])
        b_out_row = sb("b_out_row", [TP, D])
        out_norm_row = sb("out_norm_row", [TP, D])
        out_b_row = sb("out_b_row", [TP, D])
        scales_row = sb("scales_row", [TP, EXPERTS])
        p2_row = sb("p2_row", [TP, EXPERTS])
        a_col = sb("a_col", [128, 1])
        nw_col = sb("nw_col", [128, K])
        memk = sb("memk", [128, J, NMEM])
        memk_exp = sb("memk_exp", [128, J, NMEM])
        memk_n = sb("memk_n", [NMEM, D])
        memv = sb("memv", [NMEM, D])
        pos = sb("pos", [128, K, EXPERTS])
        ctx_hl = [sb(f"ctx_{part}", [128, J, 128], F32R) for part in ("hi", "lo")]
        bn6 = sb("bn6", [TP, NLN, 6])
        mean_var = sb("mean_var", [TP, NLN, 2])
        ln_std = sb("ln_std", [TP, NLN])
        ln_rstd = sb("ln_rstd", [TP, NLN])
        xr_norm = sb("xr_norm", [TP, 3, T])
        mo_norm = sb("mo_norm", [TP, 3, T])
        k_max = sb("k_max", [128, J, 3])
        k_neg = sb("k_neg", [128, J])
        k_sum = sb("k_sum", [128, J, 3])
        k_rsum = sb("k_rsum", [128, J])
        q_max = sb("q_max", [TP, T, HEADS])
        q_sum = sb("q_sum", [TP, T, HEADS])
        x2_sq = sb("x2_sq", [TP, T])
        a_max = sb("a_max", [TP, T])
        a_sum = sb("a_sum", [TP, T])
        raw = [sb(f"raw{n}", [128, K, D]) for n in range(2)]
        graph = ExitStack()
        adj = [sb(f"adj_{part}", [TP, T, TT], F32R, graph) for part in ("hi", "lo")]
        graph.close()
        raw += [sb(f"raw{n}", [128, K, D]) for n in range(2, U)]

        psum = ctx.enter_context(nc.psum_tensor("psum", [128, BANKS * BW], F32))

        def bank_at(n):
            return psum[:, (n % BANKS) * BW:(n % BANKS + 1) * BW]

        def bank(*name):
            return bank_at(JOB[name])

        def transposed(b):
            return b[:, 0:K * TW].rearrange("p (k n) -> p k n", k=K)

        def expert_bank(t):
            return bank_at(NJ + t)

        count_psum = psum[0:TP, 0:T * T * OHW].rearrange("p (t n) -> p t n", t=T)
        colsum_a = psum[:, 7 * BW:7 * BW + SA]
        colsum_b = psum[:, 6 * BW + 256:6 * BW + 256 + SB]

        TAIL = [("aT", 0)]
        for i in range(1, T):
            TAIL += [("aT", i), ("fo", i - 1)]
        TAIL += [("fo", T - 1)]

        def tail_after(*name):
            return TAIL.index(name) + 1

        def tail_bank(*name):
            return bank_at(NJ + T + TAIL.index(name))

        edges_loaded = sem("edges_loaded")
        x_loaded = sem("x_loaded")
        x_again = sem("x_again")
        rows_loaded = sem("rows_loaded")
        layer_rows_loaded = [sem(f"layer_rows_loaded{n}") for n in range(2)]
        mem_loaded = sem("mem_loaded")
        pos_loaded = sem("pos_loaded")
        raw_loaded = [sem(f"raw_loaded{n}") for n in range(U)]
        stage_hi = sem("stage_hi")
        stage_split = sem("stage_split")
        iota_ready = sem("iota_ready")
        const_ready = sem("const_ready")
        pads_ready = sem("pads_ready")
        onehots_ready = sem("onehots_ready")
        onehots_used = sem("onehots_used")
        counted = sem("counted")
        counts_copied = sem("counts_copied")
        colsum_ready = sem("colsum_ready")
        adj_scaled = sem("adj_scaled")
        adj_hi = sem("adj_hi")
        adj_split = sem("adj_split")
        var_ready = sem("var_ready")
        std_ready = sem("std_ready")
        xn_ready = sem("xn_ready")
        xr_norm_ready = sem("xr_norm_ready")
        xr_ready = sem("xr_ready")
        bank_full = sem("bank_full")
        bank_free = sem("bank_free")
        hi_ready = sem("hi_ready")
        k_max_ready = sem("k_max_ready")
        k_exp_ready = sem("k_exp_ready")
        ctx_hi_ready = sem("ctx_hi_ready")
        ctx_split = sem("ctx_split")
        q_exp_ready = sem("q_exp_ready")
        q_ready = sem("q_ready")
        mo_norm_ready = sem("mo_norm_ready")
        h_ready = sem("h_ready")
        h_hi_ready = sem("h_hi_ready")
        h_split = sem("h_split")
        h_biased = sem("h_biased")
        pos_sq_ready = sem("pos_sq_ready")
        pos_hi_ready = sem("pos_hi_ready")
        pos_split = sem("pos_split")
        x2n_ready = sem("x2n_ready")
        x2_sq_ready = sem("x2_sq_ready")
        dist_sq_ready = sem("dist_sq_ready")
        dist_ready = sem("dist_ready")
        logits_ready = sem("logits_ready")
        exps_ready = sem("exps_ready")
        tile_full = sem("tile_full")
        tile_free = sem("tile_free")
        tail_full = sem("tail_full")
        tail_hi = sem("tail_hi")
        tail_free = sem("tail_free")
        out_ready = sem("out_ready")
        stored = sem("stored")
        dve_step = sem("dve_step")
        act_step = sem("act_step")
        pool_step = sem("pool_step")

        block = ctx.enter_context(nc.Block())

        @block.sync
        def _(sp):
            def load_stage(s):
                if s < PRE:
                    if s >= 2:
                        sp.wait_ge(stage_split, s - 1)
                elif s < PRE + 2:
                    sp.wait_ge(stage_split, s - 1)
                elif s < PRE + U:
                    sp.wait_ge(bank_full, after("sT", LAYERS - 1, K + K // 2 - 1))
                else:
                    sp.wait_ge(stage_split, s - U + 1)
                source = stage_src[s] if s in stage_src else value_w[s - PRE].rearrange(kp, k=K)
                sp.dma_start(raw[raw_slot(s)][:, :, :], source).then_inc(raw_loaded[raw_slot(s)], 16)

            sp.dma_start(src_i[:, :], src.rearrange("(p c) -> p c", p=TP)).then_inc(edges_loaded, 16)
            sp.dma_start(dst_i[:, :], dst.rearrange("(p c) -> p c", p=TP)).then_inc(edges_loaded, 16)
            sp.dma_start(h[:, :, :], x.rearrange("(t p) n -> p t n", p=TP)).then_inc(x_loaded, 16)
            load_stage(0)
            load_stage(1)
            sp.dma_start(nw_col[:, :], norm_w.rearrange("(p k) -> p k", k=K)).then_inc(mem_loaded, 16)
            sp.dma_start(memk[:, :, :], mem_k.rearrange("(j p) m -> p j m", p=128)).then_inc(mem_loaded, 16)
            sp.dma_start(memv[:, :], mem_v).then_inc(mem_loaded, 16)

            def row(dest, source, done):
                sp.dma_start(dest, source.partition_broadcast(TP)).then_inc(done, 16)

            row(b_out_row[:, :], b_out, rows_loaded)
            row(out_norm_row[:, :], out_norm_w, rows_loaded)
            row(out_b_row[:, :], out_b, rows_loaded)
            row(scales_row[:, :], scales, rows_loaded)
            sp.dma_start(a_col[:, :], a_prelu.partition_broadcast(128)).then_inc(rows_loaded, 16)
            for l in range(2):
                for n, source in enumerate(gnn_rows[l]):
                    row(layer_rows[:, l, n, :], source, layer_rows_loaded[l])
            sp.dma_start(pos[:, :, :], pos_t.rearrange(kp, k=K)).then_inc(pos_loaded, 16)
            load_stage(2)
            load_stage(3)
            sp.wait_ge(bank_full, after("qT", T - 1))
            sp.dma_start(xm, x.rearrange("(t p) n -> p t n", p=TP)).then_inc(x_again, 16)
            for s in range(4, 8):
                load_stage(s)
            for l in range(2, LAYERS):
                sp.wait_ge(h_ready, T * (l - 1))
                for n, source in enumerate(gnn_rows[l]):
                    row(layer_rows[:, l % 2, n, :], source, layer_rows_loaded[l % 2])
            for s in range(8, PRE + U):
                load_stage(s)
            with sp.Fori(1, EXPERTS // U) as i:
                for u in range(U):
                    sp.wait_ge(stage_split, i * U + (PRE + u - U + 1))
                    sp.dma_start(raw[u][:, :, :],
                                 value_w[bass.ds(i * U + u, 1)].rearrange("o (p k) n -> p (o k) n", k=K))\
                      .then_inc(raw_loaded[u], 16)
            load_stage(stage_out)
            for i in range(T):
                sp.wait_ge(out_ready, i + 1)
                sp.dma_start(out[i * TP:(i + 1) * TP, :], xm[:, i, :]).then_inc(stored, 16)
            sp.wait_ge(stored, 16 * T)

        @block.gpsimd
        def _(pool):
            steps = [0]

            def link(ins):
                steps[0] += 1
                ins.then_inc(pool_step, 1)
                pool.wait_ge(pool_step, steps[0])

            tiles = iota[:, :].rearrange("p (t n) -> p t n", t=T)
            link(pool.iota(tiles, [[TP, T], [1, OHW]], base=0, channel_multiplier=0))
            pool.memset(tiles[:, :, TP:OHW], -1).then_inc(iota_ready, 1)
            pool.memset(zeros[:, :], 0.0).then_inc(const_ready, 1)
            pool.memset(ones[:, :], 1.0).then_inc(const_ready, 1)
            link(pool.memset(ident[:, :], 0.0))
            pool.affine_select(out=ident[:, :], in_=ident[:, :], compare_op=ALU.not_equal, fill=1.0,
                               base=0, pattern=[[-1, 128]], channel_multiplier=1).then_inc(const_ready, 1)
            for n in range(2):
                for a in R[n]:
                    pool.memset(a[:, :].bitcast(F32), 0.0).then_inc(pads_ready, 1)
            for l in range(1, LAYERS):
                pool.wait_ge(layer_rows_loaded[l % 2], 48 * (l // 2 + 1))
                for i in range(T):
                    pool.wait_ge(bank_full, after("hT", l, i))
                    pool.wait_ge(h_split, T * l + i + 1)
                    pool.tensor_tensor(h[:, i, :], h[:, i, :], layer_rows[:, l % 2, 0, :], ALU.add)\
                        .then_inc(h_biased, 1)

        @block.scalar
        def _(act):
            steps = [0]

            def link(ins):
                steps[0] += 1
                ins.then_inc(act_step, 1)
                act.wait_ge(act_step, steps[0])

            def wait_stage_used(s):
                if s < PRE:
                    last = {stage_k: ("kTb", J - 1), stage_v: ("v", T - 1), stage_q: ("q", T - 1),
                            stage_o: ("mo", T - 1)}
                    act.wait_ge(bank_full, after(*last.get(s, ("z", (s - 4) // 2, T - 1))))
                else:
                    act.wait_ge(tile_full, T * (s - PRE + 1))

            def split_stage(s):
                act.wait_ge(raw_loaded[raw_slot(s)], 16 * raw_loads(s))
                if s >= 2:
                    wait_stage_used(s - 2)
                act.activation(split_w[s % 2][0][:, :, :], raw[raw_slot(s)][:, :, :], ACT.Copy)\
                   .then_inc(stage_hi, 1)

            def ln_std_of(n):
                act.wait_ge(var_ready, n + 1)
                act.activation(ln_std[:, n:n + 1], mean_var[:, n, 1:2], ACT.Sqrt).then_inc(std_ready, 1)

            def hi_of(job, dest, source):
                act.wait_ge(bank_full, after(*job))
                act.activation(dest, source, ACT.Copy).then_inc(hi_ready, 1)

            def hi_of_tile(job, i, dest):
                hi_of(job, dest[0][:, :, i * TW:i * TW + TP], transposed(bank(*job))[:, :, 0:TP])

            def h_hi(l, i):
                if l == 0:
                    act.wait_ge(xn_ready, i + 1)
                else:
                    act.wait_ge(h_ready, T * (l - 1) + i + 1)
                act.activation(h_r[0][:, i, :], h[:, i, :], ACT.Copy).then_inc(h_hi_ready, 1)

            for i in range(T):
                ln_std_of(ln_index(0, i))
                act.wait_ge(xn_ready, i + 1)
                link(act.activation(xm[:, i, :], h[:, i, :], ACT.Square, accum_out=xr_norm[:, 0, i:i + 1]))
                act.activation(xr_norm[:, 1, i:i + 1], xr_norm[:, 0, i:i + 1], ACT.Sqrt)\
                   .then_inc(xr_norm_ready, 1)
            act.wait_ge(pads_ready, 4)
            split_stage(stage_k)
            split_stage(stage_v)
            for i in range(T):
                act.wait_ge(adj_scaled, i + 1)
                act.activation(adj[0][:, i, :], counts[0:TP, i, 0:TT], ACT.Copy).then_inc(adj_hi, 1)
            act.wait_ge(mem_loaded, 48)
            for i in range(T):
                act.wait_ge(bank_full, after("xrT", i))
                for k in range(K):
                    ins = act.activation(xr_c[0][:, k, i * TW:i * TW + TP], transposed(bank("xrT", i))[:, k, 0:TP],
                                         ACT.Copy, scale=nw_col[:, k:k + 1])
                ins.then_inc(hi_ready, 1)
            for j in range(J):
                act.wait_ge(k_max_ready, j + 1)
                if j == 0:
                    act.wait_ge(bank_full, after("xrT", T - 1))
                for n, (name, at, width) in enumerate((("kTa", 0, SA), ("kTb", SA, SB))):
                    act.activation(k_exp[:, j, at:at + width].rearrange("p (t n) -> p t n", n=TW)[:, :, 0:TP],
                                   bank(name, j)[:, 0:width].rearrange("p (t n) -> p t n", n=TW)[:, :, 0:TP],
                                   ACT.Exp, bias=k_neg[:, j:j + 1], accum_out=k_sum[:, j, n:n + 1])
                act.activation(memk_exp[:, j, :], memk[:, j, :], ACT.Exp, bias=k_neg[:, j:j + 1],
                               accum_out=k_sum[:, j, 2:3]).then_inc(k_exp_ready, 1)
            split_stage(stage_q)
            for i in range(T):
                hi_of(("v", i), v_r[0][:, i, :], bank("v", i)[0:TP, :])
            split_stage(stage_o)
            for i in range(T):
                hi_of(("kN", i), kn_r[0][:, i, :], bank("kN", i)[0:TP, :])

            def q_exp(i):
                act.wait_ge(bank_free, after("q", i))
                act.activation(xm[:, i, :], xm[:, i, :], ACT.Exp).then_inc(q_exp_ready, 1)

            q_exp(0)
            q_exp(1)
            act.wait_ge(bank_free, after("ctx", 0))
            act.activation(ctx_hl[0][:, :, :], ctx_f, ACT.Copy).then_inc(ctx_hi_ready, 1)
            for i in range(2, T):
                q_exp(i)
            for i in range(T):
                hi_of_tile(("qT", i), i, q_c)
            for j in range(J):
                hi_of(("oTa", j), o_c[0][:, j, 0:SA], bank("oTa", j)[:, 0:SA])
                hi_of(("oTb", j), o_c[0][:, j, SA:TT], bank("oTb", j)[:, 0:SB])
            split_stage(stage_r(0))
            for i in range(T):
                act.wait_ge(bank_free, after("mo", i))
                link(act.activation(act_dump[0:TP, :], scratch(i % 2)[0:TP, :], ACT.Square,
                                    accum_out=mo_norm[:, 0, i:i + 1]))
                act.activation(mo_norm[:, 1, i:i + 1], mo_norm[:, 0, i:i + 1], ACT.Sqrt)\
                   .then_inc(mo_norm_ready, 1)
            split_stage(stage_l(0))
            for i in range(T):
                h_hi(0, i)
                hi_of_tile(("hT", 0, i), i, h_c)

            def s_hi(l):
                for m in range(K):
                    hi_of(("sT", l, m), s_c[0][:, m, 0:SA], bank("sT", l, m)[:, 0:SA])
                for m in range(0, K, 2):
                    b = ("sT", l, K + m // 2)
                    hi_of(b, s_c[0][:, m:m + 2, SA:TT], bank(*b)[:, 0:2 * SB].rearrange("p (m n) -> p m n", m=2))

            for l in range(LAYERS):
                s_hi(l)
                if l > 0:
                    hi_of_tile(("hT", l, T - 1), T - 1, h_c)
                for i in range(T):
                    ln_std_of(ln_index(1 + l, i))
                    if l + 1 < LAYERS:
                        h_hi(l + 1, i)
                        if i >= 1:
                            hi_of_tile(("hT", l + 1, i - 1), i - 1, h_c)
                    else:
                        ln_std_of(ln_index(1 + LAYERS, i))
                        act.wait_ge(x2n_ready, i + 1)
                        act.activation(act_dump[0:TP, :], h[:, i, :], ACT.Square,
                                       accum_out=x2_sq[:, i:i + 1]).then_inc(x2_sq_ready, 1)
                        if i >= 1:
                            hi_of_tile(("x2T", i - 1), i - 1, x2_c)
                if l + 1 < LAYERS:
                    split_stage(stage_r(l + 1))
                    split_stage(stage_l(l + 1))
                else:
                    act.wait_ge(pos_loaded, 16)
                    act.wait_ge(bank_full, after("z", l, T - 1))
                    act.activation(pos_hl[0], pos[:, :, :], ACT.Copy).then_inc(pos_hi_ready, 1)
                    split_stage(PRE)
                    hi_of_tile(("x2T", T - 1), T - 1, x2_c)
                    split_stage(PRE + 1)
            act.wait_ge(dist_sq_ready, 1)
            act.activation(attn_t[:, :, :], attn_t[:, :, :], ACT.Sqrt).then_inc(dist_ready, 1)
            for t in range(T):
                act.wait_ge(logits_ready, t + 1)
                act.activation(attn_t[:, t, :], attn_t[:, t, :], ACT.Exp, bias=a_max[:, t:t + 1],
                               accum_out=a_sum[:, t:t + 1]).then_inc(exps_ready, 1)
            with act.Fori(0, EXPERTS // U - 1) as i:
                for u in range(U):
                    m = u + 2
                    slot = m % U
                    act.wait_ge(raw_loaded[slot], i * 16 + 16 * raw_loads(PRE + m))
                    act.wait_ge(tile_full, i * (U * T) + (m - 1) * T)
                    act.activation(split_w[u % 2][0][:, :, :], raw[slot][:, :, :], ACT.Copy).then_inc(stage_hi, 1)
            for s in range(PRE + EXPERTS - U + 2, stage_out + 1):
                split_stage(s)
            for i in range(T):
                act.wait_ge(tail_full, tail_after("aT", i))
                act.activation(acc_c[0][:, :, i * TW:i * TW + TP], transposed(tail_bank("aT", i))[:, :, 0:TP],
                               ACT.Copy).then_inc(tail_hi, 1)

        @block.vector
        def _(dve):
            steps = [0]

            def link(ins):
                steps[0] += 1
                ins.then_inc(dve_step, 1)
                dve.wait_ge(dve_step, steps[0])

            def minus_hi(dest, source, hi):
                return dve.tensor_tensor(dest, source, hi.bitcast(F32), ALU.subtract)

            def split_stage(s):
                dve.wait_ge(stage_hi, s + 1)
                minus_hi(split_w[s % 2][1][:, :, :], raw[raw_slot(s)][:, :, :], split_w[s % 2][0][:, :, :])\
                    .then_inc(stage_split, 1)

            def lo_of(job, pair, source, at):
                dve.wait_ge(hi_ready, hi_after(*job))
                minus_hi(at(pair[1]), source, at(pair[0])).then_inc(bank_free, 1)

            def lo_of_tile(job, i, pair):
                lo_of(job, pair, transposed(bank(*job))[:, :, 0:TP], lambda a: a[:, :, i * TW:i * TW + TP])

            def onehots(chunk, slot):
                dve.tensor_scalar(onehot[0:TP, slot, 0, :], iota[0:TP, :], src_f[:, bass.ds(chunk, 1)], None,
                                  ALU.is_equal)
                dve.tensor_scalar(onehot[0:TP, slot, 1, :], iota[0:TP, :], dst_f[:, bass.ds(chunk, 1)], None,
                                  ALU.is_equal).then_inc(onehots_ready, 1)

            def onehot_loop(first, end):
                with dve.Fori(first, end) as i:
                    for u in range(OHR):
                        dve.wait_ge(onehots_used, i * OHR + (u + 1 - OHR))
                        onehots(i * OHR + u, u)

            def ln_stats(n, source):
                link(dve.bn_stats(bn6[:, n, :], source))
                link(dve.bn_aggr(mean_var[:, n, :], bn6[:, n, :]))
                dve.tensor_scalar(mean_var[:, n, 1:2], mean_var[:, n, 1:2], LN_EPS, None, ALU.add)\
                   .then_inc(var_ready, 1)
                dve.wait_ge(std_ready, n + 1)
                link(dve.reciprocal(ln_rstd[:, n:n + 1], ln_std[:, n:n + 1]))

            def ln_apply(n, dest, source):
                return dve.tensor_scalar(dest, source, mean_var[:, n, 0:1], ln_rstd[:, n:n + 1],
                                         ALU.subtract, ALU.mult)

            def root_d_over(norms, i):
                link(dve.tensor_scalar(norms[:, 1, i:i + 1], norms[:, 1, i:i + 1], RMS_EPS, None, ALU.max))
                link(dve.reciprocal(norms[:, 2, i:i + 1], norms[:, 1, i:i + 1]))
                link(dve.tensor_scalar(norms[:, 2, i:i + 1], norms[:, 2, i:i + 1], ROOT_D, None, ALU.mult))

            def xn_tile(i):
                n = ln_index(0, i)
                ln_stats(n, h[:, i, :])
                ln_apply(n, h[:, i, :], h[:, i, :]).then_inc(xn_ready, 1)
                dve.wait_ge(xr_norm_ready, i + 1)
                root_d_over(xr_norm, i)
                dve.tensor_scalar(xm[:, i, :], h[:, i, :], xr_norm[:, 2, i:i + 1], None, ALU.mult)\
                   .then_inc(xr_ready, 1)

            dve.wait_ge(edges_loaded, 32)
            dve.tensor_copy(src_f[:, :], src_i[:, :])
            link(dve.tensor_copy(dst_f[:, :], dst_i[:, :]))
            dve.wait_ge(iota_ready, 1)
            for u in range(OHR):
                onehots(u, u)
            dve.wait_ge(x_loaded, 16)
            loops = EC // OHR
            xn_tile(0)
            onehot_loop(1, 2)
            xn_tile(1)
            onehot_loop(2, 3)
            xn_tile(2)
            onehot_loop(3, 4)
            xn_tile(3)
            onehot_loop(4, 5)
            xn_tile(4)
            onehot_loop(5, 6)
            split_stage(stage_k)
            onehot_loop(6, 7)
            split_stage(stage_v)
            onehot_loop(7, loops)

            dve.wait_ge(counted, 1)
            for i in range(T):
                dve.tensor_copy(counts[0:TP, i, 0:TT].rearrange("p (t n) -> p t n", t=T),
                                count_psum[:, i, :].rearrange("p (t n) -> p t n", t=T)[:, :, 0:TW])\
                   .then_inc(counts_copied, 1)
            dve.wait_ge(colsum_ready, 1)
            dve.tensor_scalar(recip_cnt[:, 0:SA], colsum_a, 1.0, None, ALU.max)
            link(dve.tensor_scalar(recip_cnt[:, SA:TT], colsum_b, 1.0, None, ALU.max))
            link(dve.reciprocal(recip_cnt[:, :], recip_cnt[:, :]))
            for i in range(T):
                dve.wait_ge(counts_copied, i + 1)
                dve.tensor_tensor(counts[0:TP, i, 0:TT], counts[0:TP, i, 0:TT], recip_cnt[0:TP, :], ALU.mult)\
                   .then_inc(adj_scaled, 1)
            for i in range(T):
                dve.wait_ge(adj_hi, i + 1)
                minus_hi(adj[1][:, i, :], counts[0:TP, i, 0:TT], adj[0][:, i, :]).then_inc(adj_split, 1)

            for i in range(T):
                dve.wait_ge(hi_ready, hi_after("xrT", i))
                for k in range(K):
                    at = slice(i * TW, i * TW + TP)
                    ins = dve.scalar_tensor_tensor(out=xr_c[1][:, k, at], in0=transposed(bank("xrT", i))[:, k, 0:TP],
                                                   scalar=nw_col[:, k:k + 1], in1=xr_c[0][:, k, at].bitcast(F32),
                                                   op0=ALU.mult, op1=ALU.subtract)
                ins.then_inc(bank_free, 1)
            for j in range(J):
                for n, (name, width) in enumerate((("kTa", SA), ("kTb", SB))):
                    dve.wait_ge(bank_full, after(name, j))
                    dve.tensor_reduce(k_max[:, j, n:n + 1],
                                      bank(name, j)[:, 0:width].rearrange("p (t n) -> p t n", n=TW)[:, :, 0:TP],
                                      AX.XY, ALU.max)
                link(dve.tensor_reduce(k_max[:, j, 2:3], memk[:, j, :], AX.X, ALU.max))
                dve.tensor_reduce(k_neg[:, j:j + 1], k_max[:, j, :], AX.X, ALU.max, negate=True)\
                   .then_inc(k_max_ready, 1)
            for j in range(J):
                dve.wait_ge(k_exp_ready, j + 1)
                link(dve.tensor_reduce(k_rsum[:, j:j + 1], k_sum[:, j, :], AX.X, ALU.add))
                dve.reciprocal(k_rsum[:, j:j + 1], k_rsum[:, j:j + 1]).then_inc(bank_free, 2)
            split_stage(stage_q)
            link(dve.memset(ctx_f, 0.0))
            for i in range(T):
                lo_of(("v", i), v_r, bank("v", i)[0:TP, :], lambda a: a[:, i, :])
            split_stage(stage_o)
            for i in range(T):
                lo_of(("kN", i), kn_r, bank("kN", i)[0:TP, :], lambda a: a[:, i, :])
            dve.wait_ge(bank_full, after("kM", 0))
            dve.tensor_copy(memk_n[:, :], bank("kM", 0)[0:NMEM, :]).then_inc(bank_free, 1)

            def per_head(a):
                return a.rearrange("p (h c) -> p h c", c=C)

            def q_shift(i):
                dve.wait_ge(bank_full, after("q", i))
                link(dve.tensor_reduce(q_max[:, i, :], per_head(bank("q", i)[0:TP, :]), AX.X, ALU.max))
                dve.tensor_tensor(per_head(xm[:, i, :]), per_head(bank("q", i)[0:TP, :]),
                                  q_max[:, i, :].unsqueeze(2).to_broadcast([TP, HEADS, C]), ALU.subtract)\
                   .then_inc(bank_free, 1)

            def q_softmax(i):
                dve.wait_ge(q_exp_ready, i + 1)
                link(dve.tensor_reduce(q_sum[:, i, :], per_head(xm[:, i, :]), AX.X, ALU.add))
                link(dve.reciprocal(q_sum[:, i, :], q_sum[:, i, :]))
                link(dve.tensor_scalar(q_sum[:, i, :], q_sum[:, i, :], Q_SCALE, None, ALU.mult))
                dve.tensor_tensor(per_head(xm[:, i, :]), per_head(xm[:, i, :]),
                                  q_sum[:, i, :].unsqueeze(2).to_broadcast([TP, HEADS, C]), ALU.mult)\
                   .then_inc(q_ready, 1)

            q_shift(0)
            q_shift(1)
            dve.wait_ge(bank_full, after("ctx", 0))
            ctx_psum = bank("ctx", 0).rearrange("p (j e) -> p j e", j=J)
            for half in range(2):
                at = slice(C * half, C * half + C)
                ins = dve.tensor_tensor(ctx_f[at, :, at], ctx_psum[at, :, at],
                                        k_rsum[at, :].unsqueeze(2).to_broadcast([C, J, C]), ALU.mult)
                if half == 0:
                    link(ins)
            ins.then_inc(bank_free, 1)
            dve.wait_ge(ctx_hi_ready, 1)
            minus_hi(ctx_hl[1][:, :, :], ctx_f, ctx_hl[0][:, :, :]).then_inc(ctx_split, 1)
            q_softmax(0)
            q_softmax(1)
            for i in range(2, T):
                q_shift(i)
            for i in range(2, T):
                q_softmax(i)
            for i in range(T):
                lo_of_tile(("qT", i), i, q_c)
            for j in range(J):
                lo_of(("oTa", j), o_c, bank("oTa", j)[:, 0:SA], lambda a: a[:, j, 0:SA])
                lo_of(("oTb", j), o_c, bank("oTb", j)[:, 0:SB], lambda a: a[:, j, SA:TT])
            split_stage(stage_r(0))
            dve.wait_ge(rows_loaded, 80)
            dve.wait_ge(x_again, 16)
            dve.wait_ge(pos_loaded, 16)
            dve.tensor_tensor(pos_sq, pos[:, :, :], pos[:, :, :], ALU.mult).then_inc(pos_sq_ready, 1)
            for i in range(T):
                tmp = scratch(i % 2)[0:TP, :]
                dve.wait_ge(bank_full, after("mo", i))
                dve.tensor_tensor(tmp, bank("mo", i)[0:TP, :], b_out_row[:, :], ALU.add)\
                   .then_inc(bank_free, 1)
                dve.wait_ge(mo_norm_ready, i + 1)
                root_d_over(mo_norm, i)
                link(dve.scalar_tensor_tensor(out=tmp, in0=tmp, scalar=mo_norm[:, 2, i:i + 1],
                                              in1=out_norm_row[:, :], op0=ALU.mult, op1=ALU.mult))
                link(dve.tensor_tensor(xm[:, i, :], xm[:, i, :], tmp, ALU.add))
            dve.wait_ge(bank_full, after("p2", 0))
            dve.tensor_copy(p2_row[:, :], bank("p2", 0)[0:TP, 0:EXPERTS]).then_inc(bank_free, 1)
            split_stage(stage_l(0))

            def h_lo(l, i):
                dve.wait_ge(h_hi_ready, T * l + i + 1)
                minus_hi(h_r[1][:, i, :], h[:, i, :], h_r[0][:, i, :]).then_inc(h_split, 1)

            for i in range(T):
                h_lo(0, i)
                lo_of_tile(("hT", 0, i), i, h_c)

            def s_lo(l):
                for m in range(K):
                    lo_of(("sT", l, m), s_c, bank("sT", l, m)[:, 0:SA], lambda a: a[:, m, 0:SA])
                for m in range(0, K, 2):
                    b = ("sT", l, K + m // 2)
                    lo_of(b, s_c, bank(*b)[:, 0:2 * SB].rearrange("p (m n) -> p m n", m=2),
                          lambda a: a[:, m:m + 2, SA:TT])

            for l in range(LAYERS):
                s_lo(l)
                if l > 0:
                    lo_of_tile(("hT", l, T - 1), T - 1, h_c)
                bias_row, gain_row, shift_row = (layer_rows[:, l % 2, n, :] for n in range(3))
                dve.wait_ge(layer_rows_loaded[l % 2], 48 * (l // 2 + 1))
                for i in range(T):
                    n = ln_index(1 + l, i)
                    tmp = scratch(i % 2)[0:TP, :]
                    dve.wait_ge(bank_full, after("z", l, i))
                    if l > 0:
                        dve.wait_ge(h_biased, T * (l - 1) + i + 1)
                    dve.tensor_tensor(tmp, bank("z", l, i)[0:TP, :], h[:, i, :] if l > 0 else bias_row, ALU.add)\
                       .then_inc(bank_free, 1)
                    dve.wait_ge(bank_free, after("z", l, i))
                    ln_stats(n, tmp)
                    link(ln_apply(n, tmp, tmp))
                    link(dve.tensor_tensor(tmp, tmp, gain_row, ALU.mult))
                    link(dve.tensor_tensor(tmp, tmp, shift_row, ALU.add))
                    link(dve.tensor_scalar(h[:, i, :], tmp, 0.0, a_col[0:TP, 0:1], ALU.min, ALU.mult))
                    dve.scalar_tensor_tensor(out=h[:, i, :], in0=tmp, scalar=0.0, in1=h[:, i, :],
                                             op0=ALU.max, op1=ALU.add).then_inc(h_ready, 1)
                    if l + 1 < LAYERS:
                        h_lo(l + 1, i)
                        if i >= 1:
                            lo_of_tile(("hT", l + 1, i - 1), i - 1, h_c)
                    else:
                        dve.wait_ge(h_ready, T * l + i + 1)
                        link(dve.tensor_tensor(xm[:, i, :], xm[:, i, :], h[:, i, :], ALU.add))
                        n = ln_index(1 + LAYERS, i)
                        ln_stats(n, xm[:, i, :])
                        ln_apply(n, h[:, i, :], xm[:, i, :]).then_inc(x2n_ready, 1)
                        if i >= 1:
                            lo_of_tile(("x2T", i - 1), i - 1, x2_c)
                if l + 1 < LAYERS:
                    split_stage(stage_r(l + 1))
                    split_stage(stage_l(l + 1))
                else:
                    dve.wait_ge(pos_hi_ready, 1)
                    minus_hi(pos_hl[1], pos[:, :, :], pos_hl[0]).then_inc(pos_split, 1)
                    split_stage(PRE)

            dve.wait_ge(x2_sq_ready, T)

            def squares(t):
                return dve.tensor_scalar(attn_t[:, t, :], p2_row[:, :], x2_sq[:, t:t + 1], None, ALU.add)

            for t in range(T):
                link(squares(t))
            dve.wait_ge(bank_full, after("d", 0))
            dots = bank("d", 0)[0:TP, :].rearrange("p (t n) -> p t n", n=EXPERTS)
            dve.scalar_tensor_tensor(out=attn_t[:, 0:4, :], in0=dots, scalar=-2.0, in1=attn_t[:, 0:4, :],
                                     op0=ALU.mult, op1=ALU.add).then_inc(bank_free, 1)
            lo_of_tile(("x2T", T - 1), T - 1, x2_c)
            split_stage(PRE + 1)
            dve.wait_ge(bank_full, after("x2T", T - 1))
            for t in range(T):
                dve.memset(h[:, t, :], 0.0).then_inc(tile_free, 1)
            dve.wait_ge(bank_full, after("d", 1))
            dve.scalar_tensor_tensor(out=attn_t[:, 4, :], in0=bank("d", 1)[0:TP, 0:EXPERTS], scalar=-2.0,
                                     in1=attn_t[:, 4, :], op0=ALU.mult, op1=ALU.add).then_inc(bank_free, 1)
            dve.wait_ge(bank_free, NJ)
            dve.tensor_scalar(attn_t[:, :, :], attn_t[:, :, :], 0.0, None, ALU.max).then_inc(dist_sq_ready, 1)
            dve.wait_ge(dist_ready, 1)
            link(dve.tensor_scalar(attn_t[:, :, :], attn_t[:, :, :], 0.1, None, ALU.add))
            link(dve.reciprocal(attn_t[:, :, :], attn_t[:, :, :]))
            link(dve.tensor_tensor(attn_t[:, :, :], attn_t[:, :, :],
                                   scales_row[:, :].unsqueeze(1).to_broadcast([TP, T, EXPERTS]), ALU.mult))
            for t in range(T):
                dve.tensor_reduce(a_max[:, t:t + 1], attn_t[:, t, :], AX.X, ALU.max, negate=True)\
                   .then_inc(logits_ready, 1)
            dve.wait_ge(exps_ready, T)
            link(dve.reciprocal(a_sum[:, :], a_sum[:, :]))
            for t in range(T):
                ins = dve.tensor_scalar(attn_t[:, t, :], attn_t[:, t, :], a_sum[:, t:t + 1], None, ALU.mult)
            link(ins)

            def gather(full, expert):
                for t in range(T):
                    dve.wait_ge(tile_full, full + (t + 1))
                    dve.wait_ge(tile_free, full + (t + 1))
                    dve.scalar_tensor_tensor(out=h[:, t, :], in0=expert_bank(t)[0:TP, :],
                                             scalar=attn_t[:, t, bass.ds(expert, 1)], in1=h[:, t, :],
                                             op0=ALU.mult, op1=ALU.add).then_inc(tile_free, 1)

            with dve.Fori(0, EXPERTS // U - 1) as i:
                for u in range(U):
                    gather(i * (U * T) + u * T, i * U + u)
                    m = u + 2
                    dve.wait_ge(stage_hi, i * U + (PRE + m + 1))
                    minus_hi(split_w[u % 2][1][:, :, :], raw[m % U][:, :, :], split_w[u % 2][0][:, :, :])\
                        .then_inc(stage_split, 1)
            for n in range(EXPERTS - U, EXPERTS):
                gather(n * T, n)
                if PRE + n + 2 <= stage_out:
                    split_stage(PRE + n + 2)

            def tail_lo(i):
                dve.wait_ge(tail_hi, i + 1)
                minus_hi(acc_c[1][:, :, i * TW:i * TW + TP], transposed(tail_bank("aT", i))[:, :, 0:TP],
                         acc_c[0][:, :, i * TW:i * TW + TP]).then_inc(tail_free, 1)

            tail_lo(0)
            for i in range(T):
                if i + 1 < T:
                    tail_lo(i + 1)
                link(dve.tensor_tensor(scratch(i % 2)[0:TP, :], xm[:, i, :], out_b_row[:, :], ALU.add))
                dve.wait_ge(tail_full, tail_after("fo", i))
                dve.tensor_tensor(xm[:, i, :], tail_bank("fo", i)[0:TP, :], scratch(i % 2)[0:TP, :], ALU.add)\
                   .then_inc(out_ready, 1)

        @block.tensor
        def _(pe):
            def start_job(name):
                n = JOB[name]
                if n >= BANKS:
                    pe.wait_ge(bank_free, n - BANKS + 1)
                return bank(*name)

            def three_pass(dest, lhs, rhs, start, stop, **more):
                pe.matmul(dest, lhs[0], rhs[0], start=start, stop=False, **more)
                pe.matmul(dest, lhs[1], rhs[0], start=False, stop=False, **more)
                return pe.matmul(dest, lhs[0], rhs[1], start=False, stop=stop, **more)

            def pair(p, *at):
                return [a[at] for a in p]

            def weights(s):
                return split_w[s % 2]

            def tile_product(dest, lhs_cols, i, w, start=True, stop=True):
                at = slice(i * TW, i * TW + TP)
                for k in range(K):
                    ins = three_pass(dest, pair(lhs_cols, slice(None), k, at), pair(w, slice(None), k),
                                     start and k == 0, stop and k == K - 1)
                return ins

            def transposes(job, source):
                b = transposed(start_job(job))
                for k in range(K):
                    ins = pe.transpose(b[:, k, 0:TP], source(k), ident[0:TP, 0:TP])
                ins.then_inc(bank_full, 1)

            pe.wait_ge(const_ready, 1)
            for b in range(7):
                pe.matmul(psum[0:TP, b * BW:(b + 1) * BW], zeros[:, 0:TP], zeros[:, :], start=True, stop=False,
                          skip_group_check=True)

            def count_chunk(slot, last=False):
                for i in range(T):
                    first = i * T * OHW
                    cut = (first // BW + 1) * BW
                    for a, b in ((first, cut), (cut, first + T * OHW)):
                        ins = pe.matmul(psum[0:TP, a:b], onehot[0:TP, slot, 0, i * OHW:i * OHW + TP],
                                        onehot[0:TP, slot, 1, a - first:b - first], start=False, stop=last,
                                        skip_group_check=True)
                return ins

            with pe.Fori(0, EC // OHR - 1) as it:
                for u in range(OHR):
                    pe.wait_ge(onehots_ready, it * OHR + (u + 1))
                    count_chunk(u).then_inc(onehots_used, 1)
            for u in range(OHR):
                pe.wait_ge(onehots_ready, EC - OHR + u + 1)
                ins = count_chunk(u, last=u == OHR - 1)
                ins.then_inc(onehots_used, 1) if u < OHR - 1 else ins.then_inc(counted, 1)
            pe.wait_ge(const_ready, 3)
            pe.wait_ge(counts_copied, T)
            for at, dest in ((slice(0, SA), colsum_a), (slice(SA, TT), colsum_b)):
                for i in range(T):
                    ins = pe.matmul(dest, ones[0:TP, :], counts[0:TP, i, at], start=i == 0, stop=i == T - 1)
            ins.then_inc(colsum_ready, 1)

            for i in range(T):
                pe.wait_ge(xr_ready, i + 1)
                transposes(("xrT", i), lambda k: xm[:, i, k::K])
            pe.wait_ge(stage_split, stage_k + 1)
            pe.wait_ge(bank_free, after("xrT", T - 1))
            pe.wait_ge(adj_scaled, 1)
            for j in range(J):
                for name, at in (("kTa", slice(0, SA)), ("kTb", slice(SA, TT))):
                    b = start_job((name, j))
                    for k in range(K):
                        ins = three_pass(b[:, 0:at.stop - at.start],
                                         pair(weights(stage_k), slice(None), k, slice(128 * j, 128 * j + 128)),
                                         pair(xr_c, slice(None), k, at), k == 0, k == K - 1)
                    ins.then_inc(bank_full, 1)

            def project(job, i, s, lhs):
                ins = tile_product(start_job(job)[0:TP, :], lhs, i, weights(s))
                ins.then_inc(bank_full, 1)

            pe.wait_ge(stage_split, stage_v + 1)
            for i in range(T):
                project(("v", i), i, stage_v, xr_c)
            for i in range(T):
                pe.wait_ge(k_exp_ready, J)
                b = start_job(("kN", i))
                for j in range(J):
                    ins = pe.transpose(b[0:TP, 128 * j:128 * j + 128], k_exp[:, j, i * TW:i * TW + TP], ident[:, :])
                ins.then_inc(bank_full, 1)
            b = start_job(("kM", 0))
            for j in range(J):
                ins = pe.transpose(b[0:NMEM, 128 * j:128 * j + 128], memk_exp[:, j, :], ident[:, :])
            ins.then_inc(bank_full, 1)
            pe.wait_ge(stage_split, stage_q + 1)
            for i in range(2):
                project(("q", i), i, stage_q, xr_c)
            pe.wait_ge(bank_free, after("kM", 0))
            pe.wait_ge(mem_loaded, 48)
            b = start_job(("ctx", 0))
            for j in range(J):
                at = slice(128 * j, 128 * j + 128)
                for i in range(T):
                    three_pass(b[:, at], pair(kn_r, slice(None), i, at), pair(v_r, slice(None), i, at), i == 0, False)
                ins = pe.matmul(b[:, at], memk_n[:, at], memv[:, at], start=False, stop=True)
            ins.then_inc(bank_full, 1)
            for i in range(2, T):
                project(("q", i), i, stage_q, xr_c)
            for i in range(T):
                pe.wait_ge(q_ready, i + 1)
                if i == 0:
                    pe.wait_ge(ctx_split, 1)
                b = transposed(start_job(("qT", i)))
                for j in range(J):
                    ins = pe.transpose(b[:, j, 0:TP], xm[:, i, 128 * j:128 * j + 128], ident[0:TP, 0:TP])
                ins.then_inc(bank_full, 1)
            pe.wait_ge(bank_free, after("qT", T - 1))
            for j in range(J):
                for name, at in (("oTa", slice(0, SA)), ("oTb", slice(SA, TT))):
                    b = start_job((name, j))
                    three_pass(b[:, 0:at.stop - at.start], pair(ctx_hl, slice(None), j), pair(q_c, slice(None), j, at),
                               True, True).then_inc(bank_full, 1)
            pe.wait_ge(bank_free, after("oTb", J - 1))
            pe.wait_ge(stage_split, stage_o + 1)
            for i in range(T):
                project(("mo", i), i, stage_o, o_c)
            pe.wait_ge(pos_sq_ready, 1)
            b = start_job(("p2", 0))
            for k in range(K):
                ins = pe.matmul(b[0:TP, 0:EXPERTS], ones[:, 0:TP], pos_sq[:, k, :], start=k == 0, stop=k == K - 1)
            ins.then_inc(bank_full, 1)

            for i in range(T):
                transposes(("hT", 0, i), lambda k: h[:, i, k::K])
            pe.wait_ge(adj_split, T)
            for l in range(LAYERS):
                banks = [start_job(("sT", l, b)) for b in range(K + K // 2)]
                for i in range(T):
                    pe.wait_ge(h_split, T * l + i + 1)
                    for m in range(K):
                        for dest, at, first, done in (
                                (banks[m][:, 0:SA], slice(0, SA), True, ("sT", l, m)),
                                (banks[K + m // 2][:, m % 2 * SB:m % 2 * SB + SB], slice(SA, TT), m % 2 == 0, None)):
                            ins = three_pass(dest, pair(h_r, slice(None), i, slice(m, None, K)),
                                             pair(adj, slice(None), i, at), i == 0 and first, i == T - 1,
                                             skip_group_check=True)
                            if i == T - 1 and done is None and m == K - 1:
                                ins.then_inc(bank_full, K + K // 2)
                if l > 0:
                    transposes(("hT", l, T - 1), lambda k: h[:, T - 1, k::K])
                pe.wait_ge(stage_split, stage_r(l) + 1)
                for i in range(T):
                    dest = start_job(("z", l, i))[0:TP, :]
                    pe.wait_ge(bank_free, after("hT", l, i))
                    tile_product(dest, h_c, i, weights(stage_r(l)), stop=False)
                    if i == 0:
                        pe.wait_ge(stage_split, stage_l(l) + 1)
                        pe.wait_ge(bank_free, after("sT", l, K + K // 2 - 1))
                    tile_product(dest, s_c, i, weights(stage_l(l)), start=False).then_inc(bank_full, 1)
                    if i >= 1 and l + 1 < LAYERS:
                        pe.wait_ge(h_ready, T * l + i)
                        transposes(("hT", l + 1, i - 1), lambda k: h[:, i - 1, k::K])
                    elif i >= 1:
                        pe.wait_ge(x2n_ready, i)
                        transposes(("x2T", i - 1), lambda k: h[:, i - 1, k::K])

            def dots(b, i):
                at = slice(i * TW, i * TW + TP)
                for k in range(K):
                    ins = three_pass(b, pair(x2_c, slice(None), k, at), pair(pos_hl, slice(None), k),
                                     k == 0, k == K - 1)
                return ins

            pe.wait_ge(pos_split, 1)
            pe.wait_ge(bank_free, after("x2T", T - 2))
            b = start_job(("d", 0))
            for i in range(T - 1):
                ins = dots(b[0:TP, i * EXPERTS:(i + 1) * EXPERTS], i)
            ins.then_inc(bank_full, 1)
            pe.wait_ge(x2n_ready, T)
            transposes(("x2T", T - 1), lambda k: h[:, T - 1, k::K])
            pe.wait_ge(bank_free, after("x2T", T - 1))
            dots(start_job(("d", 1))[0:TP, 0:EXPERTS], T - 1).then_inc(bank_full, 1)

            pe.wait_ge(bank_free, NJ + T - BANKS)
            with pe.Fori(0, EXPERTS // U) as it:
                for u in range(U):
                    pe.wait_ge(stage_split, it * U + (PRE + u + 1))
                    for t in range(T):
                        pe.wait_ge(tile_free, it * (U * T) + (u * T + t + 1))
                        ins = tile_product(expert_bank(t)[0:TP, :], x2_c, t, weights(u))
                        ins.then_inc(tile_full, 1)

            def tail_transposes(i):
                b = transposed(tail_bank("aT", i))
                for k in range(K):
                    ins = pe.transpose(b[:, k, 0:TP], h[:, i, k::K], ident[0:TP, 0:TP])
                ins.then_inc(tail_full, 1)

            pe.wait_ge(tile_free, T * EXPERTS + T)
            tail_transposes(0)
            pe.wait_ge(stage_split, stage_out + 1)
            for i in range(T):
                if i + 1 < T:
                    tail_transposes(i + 1)
                pe.wait_ge(tail_free, i + 1)
                tile_product(tail_bank("fo", i)[0:TP, :], acc_c, i, weights(stage_out)).then_inc(tail_full, 1)


def kernel(**inputs):
    import numpy as np
    import concourse.bacc as bacc
    from concourse.bass_utils import run_bass_kernel_spmd

    nc = bacc.Bacc("TRN2", target_bir_lowering=False, num_devices=1)
    arrays = {}

    def dram(name, array):
        array = np.ascontiguousarray(array)
        arrays[name] = array
        return nc.dram_tensor(name, array.shape, mybir.dt.from_np(array.dtype), kind="ExternalInput").ap()

    def given(name):
        return dram(name, inputs[name])

    def turned(name):
        return dram(name + "_t", np.asarray(inputs[name]).T)

    layers = range(3)
    heads, dim, slots = inputs["L0_mix_mem_kv"].shape[1:]
    mem_kv = np.asarray(inputs["L0_mix_mem_kv"]).reshape(2, heads * dim, slots)
    nodes, features = inputs["x"].shape
    out = nc.dram_tensor("out", (nodes, features), F32, kind="ExternalOutput").ap()
    gps_kernel(
        nc, given("x"), given("src"), given("dst"),
        [(turned(f"L0_gnn_Wl{l}"), turned(f"L0_gnn_Wr{l}")) for l in layers],
        [[given(f"L0_gnn_{row}{l}") for row in ("bl", "g", "b")] for l in layers],
        given("L0_gnn_a_prelu"),
        dram("norm_w", np.asarray(inputs["L0_mix_norm_w"]).reshape(-1)),
        given("L0_mix_w_qkv"), dram("mem_k", mem_kv[0]), dram("mem_v", mem_kv[1].T),
        given("L0_mix_w_out"), given("L0_mix_b_out"),
        dram("out_norm_w", np.asarray(inputs["L0_mix_out_norm_w"]).reshape(-1)),
        turned("L0_ffn_positions"), given("L0_ffn_scales"), given("L0_ffn_value_weight"),
        turned("L0_ffn_out_W"), given("L0_ffn_out_b"), out)
    result = run_bass_kernel_spmd(nc, [arrays], core_ids=[0])
    return result.results[0]["out"]
```

```python
from contextlib import ExitStack

import concourse.bass as bass
from concourse import mybir

F32 = mybir.dt.float32
F32R = mybir.dt.float32r
BF16 = mybir.dt.bfloat16
I16 = mybir.dt.int16
I32 = mybir.dt.int32
ALU = mybir.AluOpType
ACT = mybir.ActivationFunctionType
AX = mybir.AxisListType


def gps_kernel(nc, x, src, dst, gnn_w, gnn_rows, a_prelu, norm_w, w_qkv, mem_k, mem_v, w_out, b_out,
               out_norm_w, pos_t, scales, value_w, out_wt, out_b, out):
    NODES, D = x.shape
    TP = 125
    T = NODES // TP
    TW = TP + 1
    TT = T * TW
    SA = 3 * TW
    SB = TT - SA
    K = D // 128
    EDGES = src.shape[0]
    EC = EDGES // TP
    OHW = 128
    OHR = 5
    EG = EC // OHR
    HEADS, C = 8, 64
    J = HEADS // 2
    NMEM = mem_v.shape[0]
    LAYERS = len(gnn_rows)
    EXPERTS = value_w.shape[0]
    U = 4
    LN_EPS = 1e-5
    RMS_EPS = 1e-12
    EXACT = 4096.0
    ROOT_D = float(D) ** 0.5
    Q_SCALE = float(C) ** -0.5

    stage_k, stage_v, stage_q, stage_o = range(4)

    def stage_r(l):
        return 4 + 2 * l

    def stage_l(l):
        return 5 + 2 * l

    PRE = 4 + 2 * LAYERS
    stage_out = PRE + EXPERTS
    kp = "(p k) n -> p k n"
    stage_src = {
        stage_k: w_qkv[:, D:2 * D].rearrange(kp, k=K),
        stage_v: w_qkv[:, 2 * D:3 * D].rearrange(kp, k=K),
        stage_q: w_qkv[:, 0:D].rearrange(kp, k=K),
        stage_o: w_out.rearrange("(j p) n -> p j n", p=128),
        stage_out: out_wt.rearrange(kp, k=K),
    }
    for l in range(LAYERS):
        stage_l_t, stage_r_t = gnn_w[l]
        stage_src[stage_r(l)] = stage_r_t.rearrange(kp, k=K)
        stage_src[stage_l(l)] = stage_l_t.rearrange(kp, k=K)

    def raw_slot(s):
        return s % 2 if s < PRE else (s - PRE) % U

    def raw_loads(s):
        if s < PRE:
            return s // 2 + 1
        return (PRE // 2 if raw_slot(s) < 2 else 0) + (s - PRE) // U + 1

    BANKS = 8
    BW = 512
    JOBS, BANK = [], []

    def take(names, banks):
        for n, name in enumerate(names):
            JOBS.append(name)
            BANK.append(banks[n % len(banks)])

    kt = [[("kTa", j), ("kTb", j)] for j in range(J)]
    take([("range", 0), ("edgeT", 0), ("range", 1)] + [("xrT", i) for i in range(T)]
         + kt[0] + kt[1] + kt[2] + kt[3] + [("v", i) for i in range(T)] + [("cnt", 0), ("flag", 0)], range(4))
    mix = [("kN", i) for i in range(T)] + [("kM", 0)]
    mix += [("q", 0), ("q", 1), ("ctx", 0)] + [("q", i) for i in range(2, T)]
    mix += [("qT", i) for i in range(T)]
    for j in range(J):
        mix += [("oTa", j), ("oTb", j)]
    mix += [("mo", 0), ("mo", 1)]
    for i in range(2, T):
        mix += [("hT", 0, i - 2), ("mo", i)]
    mix += [("hT", 0, T - 2), ("p2", 0), ("hT", 0, T - 1)]
    take(mix, [(n + 3) % BANKS for n in range(BANKS)])
    graph_jobs = [("zR", 0, i) for i in range(T)]
    for l in range(1, LAYERS):
        graph_jobs += [("hT", l, 0), ("hT", l, 1), ("zR", l, 0), ("zR", l, 1), ("hT", l, 2), ("zR", l, 2),
                       ("hT", l, 3), ("hT", l, 4), ("zR", l, 3), ("zR", l, 4)]
    graph_jobs += [("x2T", i) for i in range(T)] + [("d", 1)]
    take(graph_jobs, (6, 7))
    NJ = len(JOBS)
    JOB = {name: n for n, name in enumerate(JOBS)}

    def after(*name):
        return JOB[name] + 1

    SPLIT = [n for n in JOBS if n[0] in ("xrT", "v", "kN", "qT", "oTa", "oTb", "hT", "x2T")]

    def hi_after(*name):
        return SPLIT.index(name) + 1

    SUMS = [((0,), slice(0, SA)), ((1,), slice(0, SA)), ((0, 1), slice(SA, TT)),
            ((2,), slice(0, SA)), ((3,), slice(0, SA)), ((2, 3), slice(SA, TT))]

    LAYER_STEPS = [("add", 0), ("norm", 0), ("add", 1), ("add", 2), ("norm", 1), ("add", 3), ("add", 4),
                   ("hT", 0), ("hT", 1), ("norm", 2), ("zR", 0), ("norm", 3), ("zR", 1), ("hT", 2),
                   ("norm", 4), ("zR", 2), ("hT", 3), ("hT", 4)]
    LAST_STEPS = [("add", 0), ("norm", 0), ("add", 1), ("add", 2), ("norm", 1), ("add", 3), ("add", 4),
                  ("x2T", 0), ("x2T", 1), ("norm", 2), ("x2T", 2), ("norm", 3), ("x2T", 3), ("norm", 4),
                  ("x2T", 4)]

    def ln_index(group, i):
        if group < LAYERS:
            return group * T + i
        return LAYERS * T + 2 * i + group - LAYERS

    NLN = (LAYERS + 2) * T

    ctx = ExitStack()
    with ctx:
        def sb(name, shape, dt=F32, stack=ctx):
            return stack.enter_context(nc.sbuf_tensor(name, shape, dt))

        def sem(name):
            return ctx.enter_context(nc.semaphore(name))

        ident = sb("ident", [128, 128])
        ones = sb("ones", [128, 128])
        iota = sb("iota", [128, T * OHW], I16)
        zeros = sb("zeros", [128, BW], BF16)
        edges_i = sb("edges_i", [EC, 2, TP], I32)
        edges_f = sb("edges_f", [EC, 2, TP])
        groups_i = sb("groups_i", [EG, OHR * TP], I32)
        edge = sb("edge", [TP, 2, EC])
        group_no = sb("group_no", [EG, 2])
        block_no = sb("block_no", [EG, 2, T])
        extent = sb("extent", [EG, 2])
        cand = sb("cand", [EG, 2, T])
        cand_max = sb("cand_max", [2 * T, 1])
        bounds_f = sb("bounds_f", [1, 2, T])
        bounds = sb("bounds", [1, 2, T], I32)
        ones_r = sb("ones_r", [TP, 2], F32R)
        rcnt = sb("rcnt", [TP, T])
        cnt_max = sb("cnt_max", [TP, 1])
        flag_f = sb("flag_f", [1, 1])
        flag = sb("flag", [1, 1], I32)
        work = sb("work", [128, OHR * 2 * T * OHW], BF16)
        onehot = work[:, :].rearrange("p (u s n) -> p u s n", u=OHR, s=2)
        workf = work[:, :].bitcast(F32)

        def scratch(n):
            return workf[:, n * BW:(n + 1) * BW]

        ctx_f = scratch(2).rearrange("p (j e) -> p j e", j=J)
        act_dump = scratch(3)
        pos_sq = scratch(4).rearrange("p (k n) -> p k n", k=K)
        attn_t = sb("attn", [TP, T, EXPERTS])
        h = sb("h", [TP, T, D])
        xm_t = sb("xm", [128, T * BW])
        xm = xm_t[0:TP, :].rearrange("p (t n) -> p t n", t=T)
        k_exp = xm_t[:, 0:J * TT].rearrange("p (j n) -> p j n", j=J)
        R = [[sb(f"r{n}_{part}", [128, T * BW], F32R) for part in ("hi", "lo")] for n in range(3)]

        def cols(n):
            return [a[:, 0:K * TT].rearrange("p (k n) -> p k n", k=K) for a in R[n]]

        def rows(n):
            return [a[0:TP, :].rearrange("p (t n) -> p t n", t=T) for a in R[n]]

        xr_c, s_c, x2_c = cols(0), cols(0), cols(0)
        kn_r, q_c, h_r = rows(1), cols(1), rows(1)
        v_r, o_c, h_c = rows(2), cols(2), cols(2)
        acc_c = cols(1)

        def sum_part(a, n):
            chunks, at = SUMS[n]
            return a[:, chunks[0]:chunks[-1] + 1, at]

        pos_hl = [a[:, 0:K * EXPERTS].rearrange("p (k n) -> p k n", k=K) for a in R[2]]
        split_w = [[sb(f"w{n}_{part}", [128, K, D], F32R) for part in ("hi", "lo")] for n in range(2)]
        layer_rows = sb("layer_rows", [TP, 2, 3, D])
        b_out_row = sb("b_out_row", [TP, D])
        out_norm_row = sb("out_norm_row", [TP, D])
        out_b_row = sb("out_b_row", [TP, D])
        scales_row = sb("scales_row", [TP, EXPERTS])
        p2_row = sb("p2_row", [TP, EXPERTS])
        a_col = sb("a_col", [128, 1])
        nw_col = sb("nw_col", [128, K])
        memk = sb("memk", [128, J, NMEM])
        memk_exp = sb("memk_exp", [128, J, NMEM])
        memk_n = sb("memk_n", [NMEM, D])
        memv = sb("memv", [NMEM, D])
        pos = sb("pos", [128, K, EXPERTS])
        ctx_hl = [sb(f"ctx_{part}", [128, J, 128], F32R) for part in ("hi", "lo")]
        bn6 = sb("bn6", [TP, NLN, 6])
        mean_var = sb("mean_var", [TP, NLN, 2])
        ln_std = sb("ln_std", [TP, NLN])
        ln_rstd = sb("ln_rstd", [TP, NLN])
        xr_norm = sb("xr_norm", [TP, 3, T])
        mo_norm = sb("mo_norm", [TP, 3, T])
        k_max = sb("k_max", [128, J, 3])
        k_neg = sb("k_neg", [128, J])
        k_sum = sb("k_sum", [128, J, 3])
        k_rsum = sb("k_rsum", [128, J])
        q_max = sb("q_max", [TP, T, HEADS])
        q_sum = sb("q_sum", [TP, T, HEADS])
        x2_sq = sb("x2_sq", [TP, T])
        a_max = sb("a_max", [TP, T])
        a_sum = sb("a_sum", [TP, T])
        raw = [sb(f"raw{n}", [128, K, D]) for n in range(2)]
        graph = ExitStack()
        adj = [sb(f"adj_{part}", [TP, T, TT], F32R, graph) for part in ("hi", "lo")]
        graph.close()
        raw += [sb(f"raw{n}", [128, K, D]) for n in range(2, U)]

        psum = ctx.enter_context(nc.psum_tensor("psum", [128, BANKS * BW], F32))

        def bank_at(n):
            return psum[:, (n % BANKS) * BW:(n % BANKS + 1) * BW]

        def bank(*name):
            return bank_at(BANK[JOB[name]])

        def transposed(b):
            return b[:, 0:K * TW].rearrange("p (k n) -> p k n", k=K)

        def count_psum(b):
            first = (4 + 2 * (b % 2)) * BW
            return psum[0:TP, first:first + T * OHW].rearrange("p (t n) -> p t n", t=T)

        sum_bank = bank_at

        def sum_psum(n):
            chunks, at = SUMS[n]
            width = at.stop - at.start
            return sum_bank(n)[:, 0:len(chunks) * width].rearrange("p (m n) -> p m n", m=len(chunks))

        layer_bank = bank_at
        expert_bank = bank_at
        dots_bank = bank_at(T)

        TAIL = [("aT", 0)]
        for i in range(1, T):
            TAIL += [("aT", i), ("fo", i - 1)]
        TAIL += [("fo", T - 1)]

        def tail_after(*name):
            return TAIL.index(name) + 1

        def tail_bank(*name):
            return bank_at(T + TAIL.index(name))

        groups_loaded = sem("groups_loaded")
        edges_loaded = sem("edges_loaded")
        x_loaded = sem("x_loaded")
        x_again = sem("x_again")
        rows_loaded = sem("rows_loaded")
        layer_rows_loaded = [sem(f"layer_rows_loaded{n}") for n in range(2)]
        mem_loaded = sem("mem_loaded")
        pos_loaded = sem("pos_loaded")
        raw_loaded = [sem(f"raw_loaded{n}") for n in range(U)]
        stage_hi = sem("stage_hi")
        stage_split = sem("stage_split")
        iota_ready = sem("iota_ready")
        const_ready = sem("const_ready")
        pads_ready = sem("pads_ready")
        onehots_ready = sem("onehots_ready")
        cand_ready = sem("cand_ready")
        cand_max_ready = sem("cand_max_ready")
        edges_cast = sem("edges_cast")
        edge_ready = sem("edge_ready")
        bounds_ready = sem("bounds_ready")
        slots_free = sem("slots_free")
        cnt_max_ready = sem("cnt_max_ready")
        flag_ready = sem("flag_ready")
        expert_split = sem("expert_split")
        sums_full = sem("sums_full")
        sums_hi = sem("sums_hi")
        sums_free = sem("sums_free")
        layer_full = sem("layer_full")
        layer_free = sem("layer_free")
        dots_full = sem("dots_full")
        q_sum_ready = sem("q_sum_ready")
        mo_scaled = sem("mo_scaled")
        counted = sem("counted")
        adj_hi = sem("adj_hi")
        adj_split = sem("adj_split")
        var_ready = sem("var_ready")
        std_ready = sem("std_ready")
        xn_ready = sem("xn_ready")
        xr_norm_ready = sem("xr_norm_ready")
        xr_ready = sem("xr_ready")
        xr_scale_ready = sem("xr_scale_ready")
        bank_full = sem("bank_full")
        bank_free = sem("bank_free")
        hi_ready = sem("hi_ready")
        k_max_ready = sem("k_max_ready")
        k_exp_ready = sem("k_exp_ready")
        ctx_hi_ready = sem("ctx_hi_ready")
        ctx_split = sem("ctx_split")
        q_exp_ready = sem("q_exp_ready")
        q_ready = sem("q_ready")
        mo_norm_ready = sem("mo_norm_ready")
        h_ready = sem("h_ready")
        h_hi_ready = sem("h_hi_ready")
        h_split = sem("h_split")
        h_biased = sem("h_biased")
        pos_sq_ready = sem("pos_sq_ready")
        xm_ready = sem("xm_ready")
        pos_hi_ready = sem("pos_hi_ready")
        pos_split = sem("pos_split")
        x2n_ready = sem("x2n_ready")
        x2_sq_ready = sem("x2_sq_ready")
        dist_sq_ready = sem("dist_sq_ready")
        dist_ready = sem("dist_ready")
        logits_ready = sem("logits_ready")
        exps_ready = sem("exps_ready")
        tile_full = sem("tile_full")
        tile_free = sem("tile_free")
        tail_full = sem("tail_full")
        tail_hi = sem("tail_hi")
        tail_free = sem("tail_free")
        out_ready = sem("out_ready")
        stored = sem("stored")
        dve_step = sem("dve_step")
        act_step = sem("act_step")
        pool_step = sem("pool_step")

        block = ctx.enter_context(nc.Block())

        @block.sync
        def _(sp):
            def load_stage(s):
                n = s - PRE
                if 2 <= s < PRE + 2:
                    sp.wait_ge(stage_split, s - 1)
                elif 2 <= n < U:
                    sp.wait_ge(sums_full, len(SUMS) * LAYERS)
                elif U <= n < U + 2:
                    sp.wait_ge(stage_split, s - U + 1)
                elif n >= U + 2:
                    sp.wait_ge(expert_split, n - U - 1)
                source = stage_src[s] if s in stage_src else value_w[n].rearrange(kp, k=K)
                sp.dma_start(raw[raw_slot(s)][:, :, :], source).then_inc(raw_loaded[raw_slot(s)], 16)

            sp.dma_start(groups_i[:, :], dst.rearrange("(g e) -> g e", g=EG)).then_inc(groups_loaded, 16)
            sp.dma_start(edges_i[:, 0, :], src.rearrange("(c p) -> c p", p=TP)).then_inc(edges_loaded, 16)
            sp.dma_start(edges_i[:, 1, :], dst.rearrange("(c p) -> c p", p=TP)).then_inc(edges_loaded, 16)
            sp.dma_start(h[:, :, :], x.rearrange("(t p) n -> p t n", p=TP)).then_inc(x_loaded, 16)
            load_stage(0)
            load_stage(1)
            sp.dma_start(nw_col[:, :], norm_w.rearrange("(p k) -> p k", k=K)).then_inc(mem_loaded, 16)
            sp.dma_start(memk[:, :, :], mem_k.rearrange("(j p) m -> p j m", p=128)).then_inc(mem_loaded, 16)
            sp.dma_start(memv[:, :], mem_v).then_inc(mem_loaded, 16)

            def row(dest, source, done):
                sp.dma_start(dest, source.partition_broadcast(TP)).then_inc(done, 16)

            row(b_out_row[:, :], b_out, rows_loaded)
            row(out_norm_row[:, :], out_norm_w, rows_loaded)
            row(out_b_row[:, :], out_b, rows_loaded)
            row(scales_row[:, :], scales, rows_loaded)
            sp.dma_start(a_col[:, :], a_prelu.partition_broadcast(128)).then_inc(rows_loaded, 16)
            for l in range(2):
                for n, source in enumerate(gnn_rows[l]):
                    row(layer_rows[:, l, n, :], source, layer_rows_loaded[l])
            sp.dma_start(pos[:, :, :], pos_t.rearrange(kp, k=K)).then_inc(pos_loaded, 16)
            load_stage(2)
            load_stage(3)
            sp.wait_ge(bank_full, after("qT", T - 1))
            sp.dma_start(xm, x.rearrange("(t p) n -> p t n", p=TP)).then_inc(x_again, 16)
            for s in range(4, 8):
                load_stage(s)
            for l in range(2, LAYERS):
                sp.wait_ge(h_ready, T * (l - 1))
                for n, source in enumerate(gnn_rows[l]):
                    row(layer_rows[:, l % 2, n, :], source, layer_rows_loaded[l % 2])
            for s in range(8, PRE + 2 * U):
                load_stage(s)
            with sp.Fori(2, EXPERTS // U) as i:
                for u in range(U):
                    sp.wait_ge(expert_split, i * U + (u - U - 1))
                    sp.dma_start(raw[u][:, :, :],
                                 value_w[bass.ds(i * U + u, 1)].rearrange("o (p k) n -> p (o k) n", k=K))\
                      .then_inc(raw_loaded[u], 16)
            load_stage(stage_out)
            for i in range(T):
                sp.wait_ge(out_ready, i + 1)
                sp.dma_start(out[i * TP:(i + 1) * TP, :], xm[:, i, :]).then_inc(stored, 16)
            sp.wait_ge(stored, 16 * T)

        @block.gpsimd
        def _(pool):
            steps = [0]

            def link(ins):
                steps[0] += 1
                ins.then_inc(pool_step, 1)
                pool.wait_ge(pool_step, steps[0])

            pool.iota(block_no[:, :, :], [[TP, 2], [TP, T]], base=0, channel_multiplier=0,
                      allow_small_or_imprecise_dtypes=True).then_inc(iota_ready, 1)
            pool.iota(group_no[:, 0:1], [[1, 1]], base=EG - 1, channel_multiplier=-1,
                      allow_small_or_imprecise_dtypes=True).then_inc(iota_ready, 1)
            pool.iota(group_no[:, 1:2], [[1, 1]], base=1, channel_multiplier=1,
                      allow_small_or_imprecise_dtypes=True).then_inc(iota_ready, 1)
            link(pool.memset(ident[:, :], 0.0))
            pool.affine_select(out=ident[:, :], in_=ident[:, :], compare_op=ALU.not_equal, fill=1.0,
                               base=0, pattern=[[-1, 128]], channel_multiplier=1).then_inc(const_ready, 1)
            tiles = iota[:, :].rearrange("p (t n) -> p t n", t=T)
            link(pool.iota(tiles, [[TP, T], [1, OHW]], base=0, channel_multiplier=0))
            pool.memset(tiles[:, :, TP:OHW], -1).then_inc(iota_ready, 1)
            pool.memset(zeros[:, :], 0.0).then_inc(const_ready, 1)
            pool.memset(ones[:, :], 1.0).then_inc(const_ready, 1)
            pool.memset(ones_r[:, :].bitcast(F32), 1.0).then_inc(const_ready, 1)
            for n in range(2):
                for a in R[n]:
                    pool.memset(a[:, :].bitcast(F32), 0.0).then_inc(pads_ready, 1)

            def split_stage(s):
                pool.wait_ge(stage_hi, s + 1)
                hi, lo = split_w[s % 2]
                pool.tensor_tensor(lo[:, :, :], raw[raw_slot(s)][:, :, :], hi[:, :, :].bitcast(F32),
                                   ALU.subtract).then_inc(stage_split, 1)

            def h_lo(l, i):
                pool.wait_ge(h_hi_ready, T * l + i + 1)
                pool.tensor_tensor(h_r[1][:, i, :], h[:, i, :], h_r[0][:, i, :].bitcast(F32), ALU.subtract)\
                    .then_inc(h_split, 1)

            def h_bias(l, i):
                pool.wait_ge(bank_full, after("hT", l, i))
                pool.wait_ge(h_split, T * l + i + 1)
                pool.tensor_tensor(h[:, i, :], h[:, i, :], layer_rows[:, l % 2, 0, :], ALU.add)\
                    .then_inc(h_biased, 1)

            def q_scale(i):
                pool.wait_ge(q_sum_ready, i + 1)
                q = xm[:, i, :].rearrange("p (h c) -> p h c", c=C)
                pool.tensor_tensor(q, q, q_sum[:, i, :].unsqueeze(2).to_broadcast([TP, HEADS, C]), ALU.mult)\
                    .then_inc(q_ready, 1)

            for s in (stage_k, stage_v, stage_q):
                split_stage(s)
            q_scale(0)
            q_scale(1)
            split_stage(stage_o)
            for i in range(2, T):
                q_scale(i)
            split_stage(stage_r(0))
            for i in range(T):
                h_lo(0, i)
            pool.wait_ge(x_again, 16)
            for i in range(T):
                pool.wait_ge(mo_scaled, i + 1)
                pool.tensor_tensor(xm[:, i, :], xm[:, i, :], scratch(i % 2)[0:TP, :], ALU.add)\
                    .then_inc(xm_ready, 1)
            split_stage(stage_l(0))
            for l in range(1, LAYERS):
                pool.wait_ge(layer_rows_loaded[l % 2], 48 * (l // 2 + 1))
                for step, i in LAYER_STEPS:
                    if step == "norm":
                        h_lo(l, i)
                    elif step == "hT":
                        h_bias(l, i)
                    if (step, i) == ("norm", 1):
                        split_stage(stage_r(l))
                split_stage(stage_l(l))
            pool.wait_ge(pos_hi_ready, 1)
            pool.tensor_tensor(pos_hl[1], pos[:, :, :], pos_hl[0].bitcast(F32), ALU.subtract).then_inc(pos_split, 1)
            split_stage(PRE)
            split_stage(PRE + 1)

        @block.scalar
        def _(act):
            steps = [0]

            def link(ins):
                steps[0] += 1
                ins.then_inc(act_step, 1)
                act.wait_ge(act_step, steps[0])

            def wait_stage_used(s):
                if s < PRE:
                    last = {stage_k: ("kTb", J - 1), stage_v: ("v", T - 1), stage_q: ("q", T - 1),
                            stage_o: ("mo", T - 1)}
                    last |= {stage_r(l): ("zR", l, T - 1) for l in range(LAYERS)}
                    if s in last:
                        act.wait_ge(bank_full, after(*last[s]))
                    else:
                        act.wait_ge(layer_full, T * ((s - 5) // 2 + 1))
                else:
                    act.wait_ge(tile_full, T * (s - PRE + 1))

            def split_stage(s):
                act.wait_ge(raw_loaded[raw_slot(s)], 16 * raw_loads(s))
                if s >= 2:
                    wait_stage_used(s - 2)
                act.activation(split_w[s % 2][0][:, :, :], raw[raw_slot(s)][:, :, :], ACT.Copy)\
                   .then_inc(stage_hi, 1)

            def ln_std_of(n):
                act.wait_ge(var_ready, n + 1)
                act.activation(ln_std[:, n:n + 1], mean_var[:, n, 1:2], ACT.Sqrt).then_inc(std_ready, 1)

            def hi_of(job, dest, source):
                act.wait_ge(bank_full, after(*job))
                act.activation(dest, source, ACT.Copy).then_inc(hi_ready, 1)

            def hi_of_tile(job, i, dest):
                hi_of(job, dest[0][:, :, i * TW:i * TW + TP], transposed(bank(*job))[:, :, 0:TP])

            def h_hi(l, i):
                if l == 0:
                    act.wait_ge(xn_ready, i + 1)
                else:
                    act.wait_ge(h_ready, T * (l - 1) + i + 1)
                act.activation(h_r[0][:, i, :], h[:, i, :], ACT.Copy).then_inc(h_hi_ready, 1)

            def xn_norm(i):
                ln_std_of(ln_index(0, i))
                act.wait_ge(xn_ready, i + 1)
                link(act.activation(xm[:, i, :], h[:, i, :], ACT.Square, accum_out=xr_norm[:, 0, i:i + 1]))
                act.activation(xr_norm[:, 1, i:i + 1], xr_norm[:, 0, i:i + 1], ACT.Sqrt)\
                   .then_inc(xr_norm_ready, 1)
                act.wait_ge(xr_scale_ready, i + 1)
                act.activation(xm[:, i, :], h[:, i, :], ACT.Copy, scale=xr_norm[:, 2, i:i + 1]).then_inc(xr_ready, 1)

            def adj_hi_of(b):
                act.wait_ge(counted, b + 1)
                act.activation(adj[0][:, :, b * TW:(b + 1) * TW], count_psum(b)[:, :, 0:TW], ACT.Copy)\
                   .then_inc(adj_hi, 1)

            def k_exp_of(j):
                act.wait_ge(k_max_ready, j + 1)
                for n, (name, at, width) in enumerate((("kTa", 0, SA), ("kTb", SA, SB))):
                    act.activation(k_exp[:, j, at:at + width].rearrange("p (t n) -> p t n", n=TW)[:, :, 0:TP],
                                   bank(name, j)[:, 0:width].rearrange("p (t n) -> p t n", n=TW)[:, :, 0:TP],
                                   ACT.Exp, bias=k_neg[:, j:j + 1], accum_out=k_sum[:, j, n:n + 1])
                act.activation(memk_exp[:, j, :], memk[:, j, :], ACT.Exp, bias=k_neg[:, j:j + 1],
                               accum_out=k_sum[:, j, 2:3]).then_inc(k_exp_ready, 1)

            for i in range(T):
                xn_norm(i)
            act.wait_ge(pads_ready, 4)
            act.wait_ge(mem_loaded, 48)
            split_stage(stage_k)
            for i in range(T):
                act.wait_ge(bank_full, after("xrT", i))
                for k in range(K):
                    ins = act.activation(xr_c[0][:, k, i * TW:i * TW + TP], transposed(bank("xrT", i))[:, k, 0:TP],
                                         ACT.Copy, scale=nw_col[:, k:k + 1])
                ins.then_inc(hi_ready, 1)
            split_stage(stage_v)
            adj_hi_of(0)
            adj_hi_of(1)
            k_exp_of(0)
            k_exp_of(1)
            adj_hi_of(2)
            k_exp_of(2)
            k_exp_of(3)
            split_stage(stage_q)
            adj_hi_of(3)
            for i in range(3):
                hi_of(("v", i), v_r[0][:, i, :], bank("v", i)[0:TP, :])
            adj_hi_of(4)
            for i in range(3, T):
                hi_of(("v", i), v_r[0][:, i, :], bank("v", i)[0:TP, :])
            for i in range(T):
                hi_of(("kN", i), kn_r[0][:, i, :], bank("kN", i)[0:TP, :])
            split_stage(stage_o)

            def q_exp(i):
                act.wait_ge(bank_free, after("q", i))
                act.activation(xm[:, i, :], xm[:, i, :], ACT.Exp).then_inc(q_exp_ready, 1)

            q_exp(0)
            q_exp(1)
            act.wait_ge(bank_free, after("ctx", 0))
            act.activation(ctx_hl[0][:, :, :], ctx_f, ACT.Copy).then_inc(ctx_hi_ready, 1)
            for i in range(2, T):
                q_exp(i)
            split_stage(stage_r(0))
            for i in range(T):
                hi_of_tile(("qT", i), i, q_c)
            for j in range(J):
                hi_of(("oTa", j), o_c[0][:, j, 0:SA], bank("oTa", j)[:, 0:SA])
                hi_of(("oTb", j), o_c[0][:, j, SA:TT], bank("oTb", j)[:, 0:SB])
            for i in range(T):
                h_hi(0, i)

            def mo_rms(i):
                act.wait_ge(bank_free, after("mo", i))
                link(act.activation(act_dump[0:TP, :], scratch(i % 2)[0:TP, :], ACT.Square,
                                    accum_out=mo_norm[:, 0, i:i + 1]))
                act.activation(mo_norm[:, 1, i:i + 1], mo_norm[:, 0, i:i + 1], ACT.Sqrt)\
                   .then_inc(mo_norm_ready, 1)

            mo_rms(0)
            mo_rms(1)
            for i in range(2, T):
                hi_of_tile(("hT", 0, i - 2), i - 2, h_c)
                mo_rms(i)
            hi_of_tile(("hT", 0, T - 2), T - 2, h_c)
            hi_of_tile(("hT", 0, T - 1), T - 1, h_c)
            split_stage(stage_l(0))

            for l in range(LAYERS):
                for n, (chunks, at) in enumerate(SUMS):
                    act.wait_ge(sums_full, len(SUMS) * l + n + 1)
                    act.activation(sum_part(s_c[0], n), sum_psum(n), ACT.Copy).then_inc(sums_hi, 1)
                last = l == LAYERS - 1
                for step, i in LAST_STEPS if last else LAYER_STEPS:
                    if step == "norm":
                        ln_std_of(ln_index(1 + l, i))
                        if last:
                            ln_std_of(ln_index(1 + LAYERS, i))
                            act.wait_ge(x2n_ready, i + 1)
                            act.activation(act_dump[0:TP, :], h[:, i, :], ACT.Square,
                                           accum_out=x2_sq[:, i:i + 1]).then_inc(x2_sq_ready, 1)
                        else:
                            h_hi(l + 1, i)
                    elif step == "hT":
                        hi_of_tile(("hT", l + 1, i), i, h_c)
                    elif step == "x2T":
                        hi_of_tile(("x2T", i), i, x2_c)
                    if (step, i) == ("norm", 1):
                        if last:
                            act.wait_ge(pos_loaded, 16)
                            act.wait_ge(bank_full, after("zR", l, T - 1))
                            act.activation(pos_hl[0], pos[:, :, :], ACT.Copy).then_inc(pos_hi_ready, 1)
                        split_stage(stage_r(l + 1))
                if not last:
                    split_stage(stage_l(l + 1))
            split_stage(PRE + 1)
            act.wait_ge(dist_sq_ready, 1)
            act.activation(attn_t[:, :, :], attn_t[:, :, :], ACT.Sqrt).then_inc(dist_ready, 1)
            for t in range(T):
                act.wait_ge(logits_ready, t + 1)
                act.activation(attn_t[:, t, :], attn_t[:, t, :], ACT.Exp, bias=a_max[:, t:t + 1],
                               accum_out=a_sum[:, t:t + 1]).then_inc(exps_ready, 1)
            with act.Fori(0, EXPERTS // U - 1) as i:
                for u in range(U):
                    m = u + 2
                    slot = m % U
                    act.wait_ge(raw_loaded[slot], i * 16 + 16 * raw_loads(PRE + m))
                    act.wait_ge(tile_full, i * (U * T) + (m - 1) * T)
                    act.activation(split_w[u % 2][0][:, :, :], raw[slot][:, :, :], ACT.Copy).then_inc(stage_hi, 1)
            for s in range(PRE + EXPERTS - U + 2, stage_out + 1):
                split_stage(s)
            for i in range(T):
                act.wait_ge(tail_full, tail_after("aT", i))
                act.activation(acc_c[0][:, :, i * TW:i * TW + TP], transposed(tail_bank("aT", i))[:, :, 0:TP],
                               ACT.Copy).then_inc(tail_hi, 1)

        @block.vector
        def _(dve):
            steps = [0]

            def link(ins):
                steps[0] += 1
                ins.then_inc(dve_step, 1)
                dve.wait_ge(dve_step, steps[0])

            def minus_hi(dest, source, hi):
                return dve.tensor_tensor(dest, source, hi.bitcast(F32), ALU.subtract)

            def split_expert(n):
                s = PRE + n
                dve.wait_ge(stage_hi, s + 1)
                minus_hi(split_w[s % 2][1][:, :, :], raw[raw_slot(s)][:, :, :], split_w[s % 2][0][:, :, :])\
                    .then_inc(expert_split, 1)

            def lo_of(job, pair, source, at):
                dve.wait_ge(hi_ready, hi_after(*job))
                minus_hi(at(pair[1]), source, at(pair[0])).then_inc(bank_free, 1)

            def lo_of_tile(job, i, pair):
                lo_of(job, pair, transposed(bank(*job))[:, :, 0:TP], lambda a: a[:, :, i * TW:i * TW + TP])

            def onehots(chunk, slot, tile):
                dve.tensor_scalar(onehot[0:TP, slot, 0, :], iota[0:TP, :], edge[:, 0, bass.ds(chunk, 1)], None,
                                  ALU.is_equal)
                at = slice(tile * OHW, (tile + 1) * OHW)
                dve.tensor_scalar(onehot[0:TP, slot, 1, at], iota[0:TP, at], edge[:, 1, bass.ds(chunk, 1)], None,
                                  ALU.is_equal).then_inc(onehots_ready, 1)

            def ln_stats(n, source):
                link(dve.bn_stats(bn6[:, n, :], source))
                link(dve.bn_aggr(mean_var[:, n, :], bn6[:, n, :]))
                dve.tensor_scalar(mean_var[:, n, 1:2], mean_var[:, n, 1:2], LN_EPS, None, ALU.add)\
                   .then_inc(var_ready, 1)
                dve.wait_ge(std_ready, n + 1)
                link(dve.reciprocal(ln_rstd[:, n:n + 1], ln_std[:, n:n + 1]))

            def ln_apply(n, dest, source):
                return dve.tensor_scalar(dest, source, mean_var[:, n, 0:1], ln_rstd[:, n:n + 1],
                                         ALU.subtract, ALU.mult)

            def root_d_over(norms, i, done=None):
                link(dve.tensor_scalar(norms[:, 1, i:i + 1], norms[:, 1, i:i + 1], RMS_EPS, None, ALU.max))
                link(dve.reciprocal(norms[:, 2, i:i + 1], norms[:, 1, i:i + 1]))
                ins = dve.tensor_scalar(norms[:, 2, i:i + 1], norms[:, 2, i:i + 1], ROOT_D, None, ALU.mult)
                if done is None:
                    link(ins)
                else:
                    ins.then_inc(done, 1)

            def xn_tile(i):
                n = ln_index(0, i)
                ln_stats(n, h[:, i, :])
                ln_apply(n, h[:, i, :], h[:, i, :]).then_inc(xn_ready, 1)
                dve.wait_ge(xr_norm_ready, i + 1)
                root_d_over(xr_norm, i, xr_scale_ready)

            dve.wait_ge(groups_loaded, 16)
            dve.tensor_reduce(extent[:, 0:1], groups_i[:, :], AX.X, ALU.max)
            link(dve.tensor_reduce(extent[:, 1:2], groups_i[:, :], AX.X, ALU.min))
            dve.wait_ge(iota_ready, 3)
            dve.tensor_scalar(cand[:, 0, :], block_no[:, 0, :], extent[:, 0:1], group_no[:, 0:1],
                              ALU.is_le, ALU.mult).then_inc(cand_ready, 1)
            dve.tensor_scalar(cand[:, 1, :], block_no[:, 1, :], extent[:, 1:2], group_no[:, 1:2],
                              ALU.is_gt, ALU.mult).then_inc(cand_ready, 1)
            dve.wait_ge(edges_loaded, 32)
            dve.tensor_copy(edges_f[:, :, :], edges_i[:, :, :]).then_inc(edges_cast, 1)
            dve.wait_ge(bank_full, after("range", 0))
            dve.tensor_reduce(cand_max[:, :], bank("range", 0)[0:2 * T, 0:EG], AX.X, ALU.max).then_inc(bank_free, 1)
            dve.wait_ge(bank_full, after("edgeT", 0))
            dve.tensor_copy(edge[:, :, :], bank("edgeT", 0)[0:TP, 0:2 * EC].rearrange("p (s c) -> p s c", s=2))\
               .then_inc(bank_free, 1)
            dve.wait_ge(bank_full, after("range", 1))
            link(dve.tensor_copy(bounds_f[:, :, :], bank("range", 1)[0:1, 0:2 * T].rearrange("p (s b) -> p s b", s=2)))
            link(dve.tensor_scalar(bounds_f[:, 0, :], bounds_f[:, 0, :], -1.0, float(EG - 1), ALU.mult, ALU.add))
            link(dve.scalar_tensor_tensor(out=bounds_f[:, 1, :], in0=bounds_f[:, 0, :], scalar=1.0,
                                          in1=bounds_f[:, 1, :], op0=ALU.add, op1=ALU.max))
            dve.tensor_copy(bounds[:, :, :], bounds_f[:, :, :]).then_inc(bank_free, 1)
            dve.wait_ge(bank_free, after("range", 1))
            group_range = [[dve.value_load(bounds[0:1, s, b:b + 1], min_val=s, max_val=EG - 1 + s) for s in range(2)]
                           for b in range(T)]
            built = dve.alloc_register("onehots_built")
            dve.reg_mov(built, 0)

            def onehot_loop(b):
                with dve.Fori(*group_range[b]) as g:
                    so_far = dve.snap(built)
                    for u in range(OHR):
                        dve.wait_ge(slots_free, so_far + (u + 1))
                        onehots(g * OHR + u, u, b)
                    dve.reg_add(built, built, OHR)

            def adj_lo_of(b):
                dve.wait_ge(adj_hi, b + 1)
                at = slice(b * TW, (b + 1) * TW)
                minus_hi(adj[1][:, :, at], count_psum(b)[:, :, 0:TW], adj[0][:, :, at]).then_inc(adj_split, 1)

            def k_max_of(j):
                for n, (name, width) in enumerate((("kTa", SA), ("kTb", SB))):
                    dve.wait_ge(bank_full, after(name, j))
                    dve.tensor_reduce(k_max[:, j, n:n + 1],
                                      bank(name, j)[:, 0:width].rearrange("p (t n) -> p t n", n=TW)[:, :, 0:TP],
                                      AX.XY, ALU.max)
                link(dve.tensor_reduce(k_max[:, j, 2:3], memk[:, j, :], AX.X, ALU.max))
                dve.tensor_reduce(k_neg[:, j:j + 1], k_max[:, j, :], AX.X, ALU.max, negate=True)\
                   .then_inc(k_max_ready, 1)

            def k_sum_of(j):
                dve.wait_ge(k_exp_ready, j + 1)
                link(dve.tensor_reduce(k_rsum[:, j:j + 1], k_sum[:, j, :], AX.X, ALU.add))
                dve.reciprocal(k_rsum[:, j:j + 1], k_rsum[:, j:j + 1]).then_inc(bank_free, 2)

            dve.wait_ge(iota_ready, 4)
            dve.wait_ge(x_loaded, 16)
            xn_tile(0)
            onehot_loop(0)
            for i in range(1, T):
                xn_tile(i)
            for i in range(T):
                dve.wait_ge(hi_ready, hi_after("xrT", i))
                for k in range(K):
                    at = slice(i * TW, i * TW + TP)
                    ins = dve.scalar_tensor_tensor(out=xr_c[1][:, k, at], in0=transposed(bank("xrT", i))[:, k, 0:TP],
                                                   scalar=nw_col[:, k:k + 1], in1=xr_c[0][:, k, at].bitcast(F32),
                                                   op0=ALU.mult, op1=ALU.subtract)
                ins.then_inc(bank_free, 1)
            onehot_loop(1)
            adj_lo_of(0)
            onehot_loop(2)
            adj_lo_of(1)
            k_max_of(0)
            k_max_of(1)
            k_sum_of(0)
            k_sum_of(1)
            onehot_loop(3)
            adj_lo_of(2)
            k_max_of(2)
            k_max_of(3)
            k_sum_of(2)
            k_sum_of(3)
            onehot_loop(4)
            adj_lo_of(3)
            for i in range(3):
                lo_of(("v", i), v_r, bank("v", i)[0:TP, :], lambda a: a[:, i, :])
            adj_lo_of(4)
            dve.memset(ctx_f, 0.0)
            for i in range(3, T):
                lo_of(("v", i), v_r, bank("v", i)[0:TP, :], lambda a: a[:, i, :])
            dve.wait_ge(bank_full, after("cnt", 0))
            in_degree = bank("cnt", 0)[0:TP, 0:2 * T].rearrange("p (t n) -> p t n", n=2)[:, :, 0:1]
            dve.tensor_reduce(cnt_max[:, :], in_degree, AX.XY, ALU.max).then_inc(cnt_max_ready, 1)
            link(dve.tensor_scalar(rcnt[:, :].unsqueeze(2), in_degree, 1.0, None, ALU.max))
            dve.reciprocal(rcnt[:, :], rcnt[:, :]).then_inc(bank_free, 1)
            dve.wait_ge(bank_full, after("flag", 0))
            link(dve.tensor_reduce(flag_f[:, :], bank("flag", 0)[0:1, 0:TP], AX.X, ALU.max))
            link(dve.tensor_scalar(flag[:, :], flag_f[:, :], EXACT, None, ALU.is_gt))
            dve.tensor_copy(flag_f[:, :], flag_f[:, :]).then_inc(bank_free, 1)
            for i in range(T):
                lo_of(("kN", i), kn_r, bank("kN", i)[0:TP, :], lambda a: a[:, i, :])
            dve.wait_ge(bank_full, after("kM", 0))
            dve.tensor_copy(memk_n[:, :], bank("kM", 0)[0:NMEM, :]).then_inc(bank_free, 1)

            def per_head(a):
                return a.rearrange("p (h c) -> p h c", c=C)

            def q_shift(i):
                dve.wait_ge(bank_full, after("q", i))
                link(dve.tensor_reduce(q_max[:, i, :], per_head(bank("q", i)[0:TP, :]), AX.X, ALU.max))
                dve.tensor_tensor(per_head(xm[:, i, :]), per_head(bank("q", i)[0:TP, :]),
                                  q_max[:, i, :].unsqueeze(2).to_broadcast([TP, HEADS, C]), ALU.subtract)\
                   .then_inc(bank_free, 1)

            def q_softmax(i):
                dve.wait_ge(q_exp_ready, i + 1)
                link(dve.tensor_reduce(q_sum[:, i, :], per_head(xm[:, i, :]), AX.X, ALU.add))
                link(dve.reciprocal(q_sum[:, i, :], q_sum[:, i, :]))
                dve.tensor_scalar(q_sum[:, i, :], q_sum[:, i, :], Q_SCALE, None, ALU.mult).then_inc(q_sum_ready, 1)

            q_shift(0)
            q_shift(1)
            dve.wait_ge(bank_full, after("ctx", 0))
            ctx_psum = bank("ctx", 0).rearrange("p (j e) -> p j e", j=J)
            for half in range(2):
                at = slice(C * half, C * half + C)
                ins = dve.tensor_tensor(ctx_f[at, :, at], ctx_psum[at, :, at],
                                        k_rsum[at, :].unsqueeze(2).to_broadcast([C, J, C]), ALU.mult)
                if half == 0:
                    link(ins)
            ins.then_inc(bank_free, 1)
            dve.wait_ge(ctx_hi_ready, 1)
            minus_hi(ctx_hl[1][:, :, :], ctx_f, ctx_hl[0][:, :, :]).then_inc(ctx_split, 1)
            q_softmax(0)
            q_softmax(1)
            for i in range(2, T):
                q_shift(i)
            for i in range(2, T):
                q_softmax(i)
            for i in range(T):
                lo_of_tile(("qT", i), i, q_c)
            for j in range(J):
                lo_of(("oTa", j), o_c, bank("oTa", j)[:, 0:SA], lambda a: a[:, j, 0:SA])
                lo_of(("oTb", j), o_c, bank("oTb", j)[:, 0:SB], lambda a: a[:, j, SA:TT])
            dve.wait_ge(rows_loaded, 80)
            dve.wait_ge(pos_loaded, 16)
            dve.tensor_tensor(pos_sq, pos[:, :, :], pos[:, :, :], ALU.mult).then_inc(pos_sq_ready, 1)

            def attention_out(i):
                tmp = scratch(i % 2)[0:TP, :]
                dve.wait_ge(bank_full, after("mo", i))
                if i >= 2:
                    dve.wait_ge(xm_ready, i - 1)
                dve.tensor_tensor(tmp, bank("mo", i)[0:TP, :], b_out_row[:, :], ALU.add).then_inc(bank_free, 1)
                dve.wait_ge(mo_norm_ready, i + 1)
                root_d_over(mo_norm, i)
                dve.scalar_tensor_tensor(out=tmp, in0=tmp, scalar=mo_norm[:, 2, i:i + 1],
                                         in1=out_norm_row[:, :], op0=ALU.mult, op1=ALU.mult).then_inc(mo_scaled, 1)

            attention_out(0)
            attention_out(1)
            for i in range(2, T):
                lo_of_tile(("hT", 0, i - 2), i - 2, h_c)
                attention_out(i)
            lo_of_tile(("hT", 0, T - 2), T - 2, h_c)
            dve.wait_ge(bank_full, after("p2", 0))
            dve.tensor_copy(p2_row[:, :], bank("p2", 0)[0:TP, 0:EXPERTS]).then_inc(bank_free, 1)
            lo_of_tile(("hT", 0, T - 1), T - 1, h_c)

            def root_product(l, i):
                dve.wait_ge(bank_full, after("zR", l, i))
                if l == 0:
                    dve.wait_ge(h_split, i + 1)
                    rest = layer_rows[:, 0, 0, :]
                else:
                    dve.wait_ge(h_biased, T * (l - 1) + i + 1)
                    rest = h[:, i, :]
                dve.tensor_tensor(h[:, i, :], bank("zR", l, i)[0:TP, :], rest, ALU.add).then_inc(bank_free, 1)

            dve.wait_ge(layer_rows_loaded[0], 48)
            for i in range(3):
                root_product(0, i)
            for l in range(LAYERS):
                last = l == LAYERS - 1
                for n in range(len(SUMS)):
                    dve.wait_ge(sums_hi, len(SUMS) * l + n + 1)
                    minus_hi(sum_part(s_c[1], n), sum_psum(n), sum_part(s_c[0], n)).then_inc(sums_free, 1)
                for i in range(3, T):
                    root_product(l, i)
                gain_row, shift_row = (layer_rows[:, l % 2, n, :] for n in (1, 2))
                dve.wait_ge(layer_rows_loaded[l % 2], 48 * (l // 2 + 1))
                for step, i in LAST_STEPS if last else LAYER_STEPS:
                    if step == "add":
                        dve.wait_ge(layer_full, T * l + i + 1)
                        dve.wait_ge(bank_free, after("zR", l, i))
                        dve.scalar_tensor_tensor(out=h[:, i, :], in0=layer_bank(i)[0:TP, :],
                                                 scalar=rcnt[:, i:i + 1], in1=h[:, i, :],
                                                 op0=ALU.mult, op1=ALU.add).then_inc(layer_free, 1)
                    elif step == "norm":
                        n = ln_index(1 + l, i)
                        tmp = scratch(0)[0:TP, :]
                        dve.wait_ge(layer_free, T * l + i + 1)
                        ln_stats(n, h[:, i, :])
                        link(ln_apply(n, h[:, i, :], h[:, i, :]))
                        link(dve.tensor_tensor(h[:, i, :], h[:, i, :], gain_row, ALU.mult))
                        link(dve.tensor_tensor(h[:, i, :], h[:, i, :], shift_row, ALU.add))
                        link(dve.tensor_scalar(tmp, h[:, i, :], 0.0, a_col[0:TP, 0:1], ALU.min, ALU.mult))
                        dve.scalar_tensor_tensor(out=h[:, i, :], in0=h[:, i, :], scalar=0.0, in1=tmp,
                                                 op0=ALU.max, op1=ALU.add).then_inc(h_ready, 1)
                        if last:
                            n = ln_index(1 + LAYERS, i)
                            dve.wait_ge(h_ready, T * l + i + 1)
                            dve.wait_ge(xm_ready, i + 1)
                            link(dve.tensor_tensor(xm[:, i, :], xm[:, i, :], h[:, i, :], ALU.add))
                            ln_stats(n, xm[:, i, :])
                            ln_apply(n, h[:, i, :], xm[:, i, :]).then_inc(x2n_ready, 1)
                    elif step == "hT":
                        lo_of_tile(("hT", l + 1, i), i, h_c)
                    elif step == "zR":
                        root_product(l + 1, i)
                    elif step == "x2T":
                        lo_of_tile(("x2T", i), i, x2_c)

            dve.wait_ge(x2_sq_ready, T)

            def squares(t):
                return dve.tensor_scalar(attn_t[:, t, :], p2_row[:, :], x2_sq[:, t:t + 1], None, ALU.add)

            for t in range(T):
                link(squares(t))
            dve.wait_ge(dots_full, 1)
            dots = dots_bank[0:TP, :].rearrange("p (t n) -> p t n", n=EXPERTS)
            link(dve.scalar_tensor_tensor(out=attn_t[:, 0:4, :], in0=dots, scalar=-2.0, in1=attn_t[:, 0:4, :],
                                          op0=ALU.mult, op1=ALU.add))
            dve.wait_ge(bank_full, after("d", 1))
            dve.scalar_tensor_tensor(out=attn_t[:, 4, :], in0=bank("d", 1)[0:TP, 0:EXPERTS], scalar=-2.0,
                                     in1=attn_t[:, 4, :], op0=ALU.mult, op1=ALU.add).then_inc(bank_free, 1)
            dve.wait_ge(bank_free, NJ)
            dve.tensor_scalar(attn_t[:, :, :], attn_t[:, :, :], 0.0, None, ALU.max).then_inc(dist_sq_ready, 1)
            dve.wait_ge(dist_ready, 1)
            link(dve.tensor_scalar(attn_t[:, :, :], attn_t[:, :, :], 0.1, None, ALU.add))
            link(dve.reciprocal(attn_t[:, :, :], attn_t[:, :, :]))
            link(dve.tensor_tensor(attn_t[:, :, :], attn_t[:, :, :],
                                   scales_row[:, :].unsqueeze(1).to_broadcast([TP, T, EXPERTS]), ALU.mult))
            for t in range(T):
                dve.tensor_reduce(a_max[:, t:t + 1], attn_t[:, t, :], AX.X, ALU.max, negate=True)\
                   .then_inc(logits_ready, 1)
            dve.wait_ge(exps_ready, T)
            link(dve.reciprocal(a_sum[:, :], a_sum[:, :]))
            for t in range(T):
                ins = dve.tensor_scalar(attn_t[:, t, :], attn_t[:, t, :], a_sum[:, t:t + 1], None, ALU.mult)
            link(ins)

            for t in range(T):
                dve.wait_ge(tile_full, t + 1)
                dve.tensor_scalar(h[:, t, :], expert_bank(t)[0:TP, :], attn_t[:, t, 0:1], None, ALU.mult)\
                   .then_inc(tile_free, 1)

            def gather(before, expert):
                for t in range(T):
                    dve.wait_ge(tile_full, before + (t + 1))
                    dve.wait_ge(tile_free, before + (t + 1 - T))
                    dve.scalar_tensor_tensor(out=h[:, t, :], in0=expert_bank(t)[0:TP, :],
                                             scalar=attn_t[:, t, bass.ds(expert, 1)], in1=h[:, t, :],
                                             op0=ALU.mult, op1=ALU.add).then_inc(tile_free, 1)

            split_expert(2)
            for n in range(1, U):
                gather(n * T, n)
                split_expert(n + 2)
            with dve.Fori(1, EXPERTS // U - 1) as i:
                for u in range(U):
                    gather(i * (U * T) + u * T, i * U + u)
                    m = u + 2
                    dve.wait_ge(stage_hi, i * U + (PRE + m + 1))
                    minus_hi(split_w[u % 2][1][:, :, :], raw[m % U][:, :, :], split_w[u % 2][0][:, :, :])\
                        .then_inc(expert_split, 1)
            for n in range(EXPERTS - U, EXPERTS):
                gather(n * T, n)
                if n + 2 <= EXPERTS:
                    split_expert(n + 2)

            def tail_lo(i):
                dve.wait_ge(tail_hi, i + 1)
                minus_hi(acc_c[1][:, :, i * TW:i * TW + TP], transposed(tail_bank("aT", i))[:, :, 0:TP],
                         acc_c[0][:, :, i * TW:i * TW + TP]).then_inc(tail_free, 1)

            tail_lo(0)
            for i in range(T):
                if i + 1 < T:
                    tail_lo(i + 1)
                link(dve.tensor_tensor(scratch(i % 2)[0:TP, :], xm[:, i, :], out_b_row[:, :], ALU.add))
                dve.wait_ge(tail_full, tail_after("fo", i))
                dve.tensor_tensor(xm[:, i, :], tail_bank("fo", i)[0:TP, :], scratch(i % 2)[0:TP, :], ALU.add)\
                   .then_inc(out_ready, 1)

        @block.tensor
        def _(pe):
            def start_job(name):
                n = JOB[name]
                last = [m for m in range(n) if BANK[m] == BANK[n]]
                if last:
                    pe.wait_ge(bank_free, last[-1] + 1)
                return bank(*name)

            def three_pass(dest, lhs, rhs, start, stop, **more):
                pe.matmul(dest, lhs[0], rhs[0], start=start, stop=False, **more)
                pe.matmul(dest, lhs[1], rhs[0], start=False, stop=False, **more)
                return pe.matmul(dest, lhs[0], rhs[1], start=False, stop=stop, **more)

            def pair(p, *at):
                return [a[at] for a in p]

            def weights(s):
                return split_w[s % 2]

            def tile_product(dest, lhs_cols, i, w, start=True, stop=True):
                at = slice(i * TW, i * TW + TP)
                for k in range(K):
                    ins = three_pass(dest, pair(lhs_cols, slice(None), k, at), pair(w, slice(None), k),
                                     start and k == 0, stop and k == K - 1)
                return ins

            def transposes(job, source):
                b = transposed(start_job(job))
                for k in range(K):
                    ins = pe.transpose(b[:, k, 0:TP], source(k), ident[0:TP, 0:TP])
                ins.then_inc(bank_full, 1)

            pe.wait_ge(const_ready, 1)
            pe.wait_ge(cand_ready, 2)
            pe.transpose(start_job(("range", 0))[0:2 * T, 0:EG], cand[:, :, :].rearrange("p s b -> p (s b)"),
                         ident[0:EG, 0:EG]).then_inc(bank_full, 1)
            pe.wait_ge(edges_cast, 1)
            b = start_job(("edgeT", 0))
            for n in range(2):
                ins = pe.transpose(b[0:TP, n * EC:(n + 1) * EC], edges_f[:, n, :], ident[0:EC, 0:EC])
            ins.then_inc(bank_full, 1)
            pe.wait_ge(bank_free, after("range", 0))
            pe.transpose(start_job(("range", 1))[0:1, 0:2 * T], cand_max[:, :], ident[0:2 * T, 0:2 * T])\
              .then_inc(bank_full, 1)
            pe.wait_ge(bank_free, after("range", 1))
            group_range = [[pe.value_load(bounds[0:1, s, b:b + 1], min_val=s, max_val=EG - 1 + s) for s in range(2)]
                           for b in range(T)]
            taken = pe.alloc_register("onehots_taken")
            pe.reg_mov(taken, 0)
            pe.wait_ge(const_ready, 4)

            def count_block(b):
                if b >= 2:
                    pe.wait_ge(adj_split, b - 1)
                out_b = count_psum(b)
                flat = psum[0:TP, (4 + 2 * (b % 2)) * BW:(6 + 2 * (b % 2)) * BW]
                for at in (slice(0, BW), slice(BW, BW + OHW)):
                    ins = pe.matmul(flat[:, at], zeros[:, 0:TP], zeros[:, 0:at.stop - at.start], start=True,
                                    stop=False, skip_group_check=True)
                if b == 0:
                    ins.then_inc(slots_free, OHR)
                with pe.Fori(*group_range[b]):
                    so_far = pe.snap(taken)
                    for u in range(OHR):
                        pe.wait_ge(onehots_ready, so_far + (u + 1))
                        for i in range(T):
                            ins = pe.matmul(out_b[:, i, :], onehot[0:TP, u, 0, i * OHW:i * OHW + TP],
                                            onehot[0:TP, u, 1, b * OHW:(b + 1) * OHW], start=False, stop=False,
                                            skip_group_check=True)
                        ins.then_inc(slots_free, 1)
                    pe.reg_add(taken, taken, OHR)
                for at in (slice(0, BW), slice(BW, BW + OHW)):
                    ins = pe.matmul(flat[:, at], zeros[:, 0:TP], zeros[:, 0:at.stop - at.start], start=False,
                                    stop=True, skip_group_check=True)
                ins.then_inc(counted, 1)

            def k_job(j):
                for name, at in (("kTa", slice(0, SA)), ("kTb", slice(SA, TT))):
                    b = start_job((name, j))
                    for k in range(K):
                        ins = three_pass(b[:, 0:at.stop - at.start],
                                         pair(weights(stage_k), slice(None), k, slice(128 * j, 128 * j + 128)),
                                         pair(xr_c, slice(None), k, at), k == 0, k == K - 1)
                    ins.then_inc(bank_full, 1)

            def project(job, i, s, lhs):
                ins = tile_product(start_job(job)[0:TP, :], lhs, i, weights(s))
                ins.then_inc(bank_full, 1)

            count_block(0)
            for i in range(T):
                pe.wait_ge(xr_ready, i + 1)
                transposes(("xrT", i), lambda k: xm[:, i, k::K])
            count_block(1)
            pe.wait_ge(stage_split, stage_k + 1)
            pe.wait_ge(bank_free, after("xrT", T - 1))
            k_job(0)
            k_job(1)
            count_block(2)
            k_job(2)
            k_job(3)
            count_block(3)
            pe.wait_ge(stage_split, stage_v + 1)
            for i in range(3):
                project(("v", i), i, stage_v, xr_c)
            count_block(4)
            for i in range(3, T):
                project(("v", i), i, stage_v, xr_c)
            pe.wait_ge(adj_split, T)
            b = start_job(("cnt", 0))
            for t in range(T):
                for i in range(T):
                    for part in range(2):
                        ins = pe.matmul(b[0:TP, 2 * t:2 * t + 2], adj[part][:, i, t * TW:t * TW + TP], ones_r[:, :],
                                        start=i == 0 and part == 0, stop=i == T - 1 and part == 1)
            ins.then_inc(bank_full, 1)
            pe.wait_ge(cnt_max_ready, 1)
            pe.transpose(start_job(("flag", 0))[0:1, 0:TP], cnt_max[:, :], ident[0:TP, 0:TP]).then_inc(bank_full, 1)
            for i in range(T):
                pe.wait_ge(k_exp_ready, J)
                b = start_job(("kN", i))
                for j in range(J):
                    ins = pe.transpose(b[0:TP, 128 * j:128 * j + 128], k_exp[:, j, i * TW:i * TW + TP], ident[:, :])
                ins.then_inc(bank_full, 1)
            b = start_job(("kM", 0))
            for j in range(J):
                ins = pe.transpose(b[0:NMEM, 128 * j:128 * j + 128], memk_exp[:, j, :], ident[:, :])
            ins.then_inc(bank_full, 1)
            pe.wait_ge(stage_split, stage_q + 1)
            for i in range(2):
                project(("q", i), i, stage_q, xr_c)
            pe.wait_ge(bank_free, after("kM", 0))
            pe.wait_ge(mem_loaded, 48)
            b = start_job(("ctx", 0))
            for j in range(J):
                at = slice(128 * j, 128 * j + 128)
                for i in range(T):
                    three_pass(b[:, at], pair(kn_r, slice(None), i, at), pair(v_r, slice(None), i, at), i == 0, False)
                ins = pe.matmul(b[:, at], memk_n[:, at], memv[:, at], start=False, stop=True)
            ins.then_inc(bank_full, 1)
            for i in range(2, T):
                project(("q", i), i, stage_q, xr_c)
            for i in range(T):
                pe.wait_ge(q_ready, i + 1)
                if i == 0:
                    pe.wait_ge(ctx_split, 1)
                b = transposed(start_job(("qT", i)))
                for j in range(J):
                    ins = pe.transpose(b[:, j, 0:TP], xm[:, i, 128 * j:128 * j + 128], ident[0:TP, 0:TP])
                ins.then_inc(bank_full, 1)
            pe.wait_ge(bank_free, after("qT", T - 1))
            for j in range(J):
                for name, at in (("oTa", slice(0, SA)), ("oTb", slice(SA, TT))):
                    b = start_job((name, j))
                    three_pass(b[:, 0:at.stop - at.start], pair(ctx_hl, slice(None), j), pair(q_c, slice(None), j, at),
                               True, True).then_inc(bank_full, 1)
            pe.wait_ge(bank_free, after("oTb", J - 1))
            pe.wait_ge(stage_split, stage_o + 1)
            def root_job(l, i):
                pe.wait_ge(bank_free, after("hT", l, i))
                tile_product(start_job(("zR", l, i))[0:TP, :], h_c, i, weights(stage_r(l))).then_inc(bank_full, 1)

            for i in range(T):
                project(("mo", i), i, stage_o, o_c)
                if i >= 1:
                    transposes(("hT", 0, i - 1), lambda k: h[:, i - 1, k::K])
            pe.wait_ge(pos_sq_ready, 1)
            b = start_job(("p2", 0))
            for k in range(K):
                ins = pe.matmul(b[0:TP, 0:EXPERTS], ones[:, 0:TP], pos_sq[:, k, :], start=k == 0, stop=k == K - 1)
            ins.then_inc(bank_full, 1)
            transposes(("hT", 0, T - 1), lambda k: h[:, T - 1, k::K])

            has_low = pe.value_load(flag[0:1, 0:1], min_val=0, max_val=1)

            def sum_source(l, i):
                pe.wait_ge(h_split, T * l + i + 1)
                if i == T - 1:
                    with pe.If(has_low != 0):
                        for j in range(T):
                            for n, (chunks, at) in enumerate(SUMS):
                                for c, m in enumerate(chunks):
                                    width = at.stop - at.start
                                    pe.matmul(sum_bank(n)[:, c * width:(c + 1) * width], h_r[0][:, j, m::K],
                                              adj[1][:, j, at], start=False, stop=False, skip_group_check=True)
                for n, (chunks, at) in enumerate(SUMS):
                    for c, m in enumerate(chunks):
                        width = at.stop - at.start
                        for part in range(2):
                            ins = pe.matmul(sum_bank(n)[:, c * width:(c + 1) * width], h_r[part][:, i, m::K],
                                            adj[0][:, i, at], start=i == 0 and c == 0 and part == 0,
                                            stop=i == T - 1, skip_group_check=True)
                    if i == T - 1:
                        ins.then_inc(sums_full, 1)

            pe.wait_ge(stage_split, stage_r(0) + 1)
            root_job(0, 0)
            root_job(0, 1)
            pe.wait_ge(bank_free, after("hT", 0, T - 1))
            for i in range(T):
                sum_source(0, i)
                if i == 0:
                    root_job(0, 2)
            for l in range(LAYERS):
                root_job(l, 3)
                root_job(l, 4)
                pe.wait_ge(stage_split, stage_l(l) + 1)
                pe.wait_ge(sums_free, len(SUMS) * (l + 1))
                for i in range(T):
                    tile_product(layer_bank(i)[0:TP, :], s_c, i, weights(stage_l(l))).then_inc(layer_full, 1)
                if l + 1 < LAYERS:
                    def turn(i):
                        pe.wait_ge(h_ready, T * l + i + 1)
                        transposes(("hT", l + 1, i), lambda k: h[:, i, k::K])

                    turn(0)
                    turn(1)
                    pe.wait_ge(stage_split, stage_r(l + 1) + 1)
                    root_job(l + 1, 0)
                    pe.wait_ge(layer_free, T * (l + 1))
                    sum_source(l + 1, 0)
                    root_job(l + 1, 1)
                    sum_source(l + 1, 1)
                    turn(2)
                    root_job(l + 1, 2)
                    sum_source(l + 1, 2)
                    turn(3)
                    sum_source(l + 1, 3)
                    turn(4)
                    sum_source(l + 1, 4)

            def turn_x2(i):
                pe.wait_ge(x2n_ready, i + 1)
                transposes(("x2T", i), lambda k: h[:, i, k::K])

            def dots(b, i):
                pe.wait_ge(bank_free, after("x2T", i))
                at = slice(i * TW, i * TW + TP)
                for k in range(K):
                    ins = three_pass(b, pair(x2_c, slice(None), k, at), pair(pos_hl, slice(None), k),
                                     k == 0, k == K - 1)
                return ins

            def dots_early(i):
                ins = dots(dots_bank[0:TP, i * EXPERTS:(i + 1) * EXPERTS], i)
                if i == T - 2:
                    ins.then_inc(dots_full, 1)

            def expert_tile(slot, t):
                tile_product(expert_bank(t)[0:TP, :], x2_c, t, weights(slot)).then_inc(tile_full, 1)

            turn_x2(0)
            turn_x2(1)
            pe.wait_ge(pos_split, 1)
            dots_early(0)
            dots_early(1)
            turn_x2(2)
            dots_early(2)
            pe.wait_ge(layer_free, T * LAYERS)
            pe.wait_ge(stage_split, PRE + 1)
            expert_tile(0, 0)
            turn_x2(3)
            dots_early(3)
            turn_x2(4)
            dots(start_job(("d", 1))[0:TP, 0:EXPERTS], T - 1).then_inc(bank_full, 1)
            for t in range(1, T):
                expert_tile(0, t)
            for n in range(1, U):
                if n == 1:
                    pe.wait_ge(stage_split, PRE + 2)
                else:
                    pe.wait_ge(expert_split, n - 1)
                for t in range(T):
                    pe.wait_ge(tile_free, T * (n - 1) + t + 1)
                    expert_tile(n, t)
            with pe.Fori(1, EXPERTS // U) as it:
                for u in range(U):
                    pe.wait_ge(expert_split, it * U + (u - 1))
                    for t in range(T):
                        pe.wait_ge(tile_free, it * (U * T) + ((u - 1) * T + t + 1))
                        expert_tile(u, t)

            def tail_transposes(i):
                pe.wait_ge(tile_free, T * (EXPERTS - 1) + i + 1)
                b = transposed(tail_bank("aT", i))
                for k in range(K):
                    ins = pe.transpose(b[:, k, 0:TP], h[:, i, k::K], ident[0:TP, 0:TP])
                ins.then_inc(tail_full, 1)

            tail_transposes(0)
            pe.wait_ge(expert_split, EXPERTS - 1)
            for i in range(T):
                if i + 1 < T:
                    tail_transposes(i + 1)
                pe.wait_ge(tail_free, i + 1)
                tile_product(tail_bank("fo", i)[0:TP, :], acc_c, i, weights(stage_out)).then_inc(tail_full, 1)


def kernel(**inputs):
    import numpy as np
    import concourse.bacc as bacc
    from concourse.bass_utils import run_bass_kernel_spmd

    nc = bacc.Bacc("TRN2", target_bir_lowering=False, num_devices=1)
    arrays = {}

    def dram(name, array):
        array = np.ascontiguousarray(array)
        arrays[name] = array
        return nc.dram_tensor(name, array.shape, mybir.dt.from_np(array.dtype), kind="ExternalInput").ap()

    def given(name):
        return dram(name, inputs[name])

    def turned(name):
        return dram(name + "_t", np.asarray(inputs[name]).T)

    layers = range(3)
    heads, dim, slots = inputs["L0_mix_mem_kv"].shape[1:]
    mem_kv = np.asarray(inputs["L0_mix_mem_kv"]).reshape(2, heads * dim, slots)
    nodes, features = inputs["x"].shape
    out = nc.dram_tensor("out", (nodes, features), F32, kind="ExternalOutput").ap()
    gps_kernel(
        nc, given("x"), given("src"), given("dst"),
        [(turned(f"L0_gnn_Wl{l}"), turned(f"L0_gnn_Wr{l}")) for l in layers],
        [[given(f"L0_gnn_{row}{l}") for row in ("bl", "g", "b")] for l in layers],
        given("L0_gnn_a_prelu"),
        dram("norm_w", np.asarray(inputs["L0_mix_norm_w"]).reshape(-1)),
        given("L0_mix_w_qkv"), dram("mem_k", mem_kv[0]), dram("mem_v", mem_kv[1].T),
        given("L0_mix_w_out"), given("L0_mix_b_out"),
        dram("out_norm_w", np.asarray(inputs["L0_mix_out_norm_w"]).reshape(-1)),
        turned("L0_ffn_positions"), given("L0_ffn_scales"), given("L0_ffn_value_weight"),
        turned("L0_ffn_out_W"), given("L0_ffn_out_b"), out)
    result = run_bass_kernel_spmd(nc, [arrays], core_ids=[0])
    return result.results[0]["out"]
```

```python
from contextlib import ExitStack

import concourse.bass as bass
from concourse import mybir

F32 = mybir.dt.float32
F32R = mybir.dt.float32r
BF16 = mybir.dt.bfloat16
I16 = mybir.dt.int16
I32 = mybir.dt.int32
ALU = mybir.AluOpType
ACT = mybir.ActivationFunctionType
AX = mybir.AxisListType


def gps_kernel(nc, x, src, dst, gnn_w, gnn_rows, a_prelu, norm_w, w_qkv, mem_k, mem_v, w_out, b_out,
               out_norm_w, pos_t, scales, value_w, out_wt, out_b, out):
    NODES, D = x.shape
    TP = 125
    T = NODES // TP
    TW = TP + 1
    TT = T * TW
    SA = 3 * TW
    SB = TT - SA
    K = D // 128
    EDGES = src.shape[0]
    EC = EDGES // TP
    OHW = 128
    OHR = 5
    EG = EC // OHR
    HEADS, C = 8, 64
    J = HEADS // 2
    NMEM = mem_v.shape[0]
    LAYERS = len(gnn_rows)
    EXPERTS = value_w.shape[0]
    U = 4
    LN_EPS = 1e-5
    RMS_EPS = 1e-12
    EXACT = 4096.0
    ROOT_D = float(D) ** 0.5
    Q_SCALE = float(C) ** -0.5

    stage_k, stage_v, stage_q, stage_o = range(4)

    def stage_r(l):
        return 4 + 2 * l

    def stage_l(l):
        return 5 + 2 * l

    BY_DVE = 3
    PRE = 4 + 2 * LAYERS
    stage_out = PRE + EXPERTS
    kp = "(p k) n -> p k n"
    stage_src = {
        stage_k: w_qkv[:, D:2 * D].rearrange(kp, k=K),
        stage_v: w_qkv[:, 2 * D:3 * D].rearrange(kp, k=K),
        stage_q: w_qkv[:, 0:D].rearrange(kp, k=K),
        stage_o: w_out.rearrange("(j p) n -> p j n", p=128),
        stage_out: out_wt.rearrange(kp, k=K),
    }
    for l in range(LAYERS):
        stage_l_t, stage_r_t = gnn_w[l]
        stage_src[stage_r(l)] = stage_r_t.rearrange(kp, k=K)
        stage_src[stage_l(l)] = stage_l_t.rearrange(kp, k=K)

    def raw_slot(s):
        return s % 2 if s < PRE else (s - PRE) % U

    def raw_loads(s):
        if s < PRE:
            return s // 2 + 1
        return (PRE // 2 if raw_slot(s) < 2 else 0) + (s - PRE) // U + 1

    BANKS = 8
    BW = 512
    JOBS, BANK = [], []

    def take(names, banks):
        for n, name in enumerate(names):
            JOBS.append(name)
            BANK.append(banks[n % len(banks)])

    kt = [(name, j) for j in range(J) for name in ("kTa", "kTb")]
    take([("range", 0), ("edgeT", 0), ("range", 1)] + [("xrT", i) for i in range(T)]
         + kt + [("v", i) for i in range(T)] + [("flag", 0), ("p2", 0)], range(4))
    mix = [("kN", i) for i in range(T)] + [("kM", 0)]
    mix += [("q", 0), ("q", 1), ("q", 2), ("q", 3), ("ctx", 0), ("hT", 0, 0), ("hT", 0, 1), ("qT", 0),
            ("qT", 1), ("qT", 2), ("q", 4)]
    mix += [("oTa", j) for j in range(J)] + [("hT", 0, 2), ("qT", 3), ("qT", 4), ("hT", 0, 3)]
    mix += [("oTb", j) for j in range(J)] + [("hT", 0, 4)]
    mix += [("mo", i) for i in range(T)]
    take(mix, [(n + 3) % BANKS for n in range(BANKS)])
    graph_jobs = [("zR", 0, i) for i in range(T)]
    for l in range(1, LAYERS):
        graph_jobs += [("hT", l, 0), ("hT", l, 1), ("zR", l, 0), ("zR", l, 1), ("hT", l, 2), ("zR", l, 2),
                       ("hT", l, 3), ("hT", l, 4), ("zR", l, 3), ("zR", l, 4)]
    graph_jobs += [("x2T", i) for i in range(T)] + [("d", 1)]
    take(graph_jobs, (6, 7))
    JOB = {name: n for n, name in enumerate(JOBS)}

    def after(*name):
        return JOB[name] + 1

    SPLIT = [n for n in JOBS if n[0] in ("xrT", "v", "kN", "qT", "oTa", "oTb", "hT", "x2T")]

    def hi_after(*name):
        return SPLIT.index(name) + 1

    SUMS = [((0,), slice(0, SA)), ((1,), slice(0, SA)), ((0, 1), slice(SA, TT)),
            ((2,), slice(0, SA)), ((3,), slice(0, SA)), ((2, 3), slice(SA, TT))]

    LAYER_STEPS = [("add", 0), ("stats", 0), ("add", 1), ("stats", 1), ("norm", 0), ("add", 2), ("norm", 1),
                   ("add", 3), ("add", 4), ("hT", 0), ("stats", 2), ("hT", 1), ("stats", 3), ("norm", 2),
                   ("zR", 0), ("stats", 4), ("norm", 3), ("zR", 1), ("hT", 2), ("norm", 4), ("zR", 2),
                   ("hT", 3), ("hT", 4)]
    LAST_STEPS = [("add", 0), ("stats", 0), ("add", 1), ("stats", 1), ("norm", 0), ("add", 2), ("norm", 1),
                  ("add", 3), ("add", 4), ("stats2", 0), ("stats", 2), ("norm2", 0), ("stats2", 1),
                  ("x2T", 0), ("norm2", 1), ("norm", 2), ("stats", 3), ("x2T", 1), ("stats2", 2), ("norm2", 2),
                  ("norm", 3), ("stats", 4), ("x2T", 2), ("stats2", 3), ("norm2", 3), ("norm", 4),
                  ("x2T", 3), ("stats2", 4), ("norm2", 4), ("x2T", 4)]

    def ln_index(group, i):
        if group < LAYERS:
            return group * T + i
        order = [step for step in LAST_STEPS if step[0] in ("stats", "stats2")]
        return LAYERS * T + order.index((("stats", "stats2")[group - LAYERS], i))

    NLN = (LAYERS + 2) * T

    ctx = ExitStack()
    with ctx:
        def sb(name, shape, dt=F32, stack=ctx):
            return stack.enter_context(nc.sbuf_tensor(name, shape, dt))

        def sem(name):
            return ctx.enter_context(nc.semaphore(name))

        ident = sb("ident", [128, 128])
        ones = sb("ones", [128, 128])
        iota = sb("iota", [128, T * OHW], I16)
        zeros = sb("zeros", [128, BW], BF16)
        edges_i = sb("edges_i", [EC, 2, TP], I32)
        edges_f = sb("edges_f", [EC, 2, TP])
        groups_i = sb("groups_i", [EG, OHR * TP], I32)
        edge = sb("edge", [TP, 2, EC])
        group_no = sb("group_no", [EG, 2])
        block_no = sb("block_no", [EG, 2, T])
        extent = sb("extent", [EG, 2])
        cand = sb("cand", [EG, 2, T])
        cand_max = sb("cand_max", [2 * T, 1])
        bounds_f = sb("bounds_f", [1, 2, T])
        bounds = sb("bounds", [1, 2, T], I32)
        ones_b = sb("ones_b", [TP, 2], BF16)
        in_degree = sb("in_degree", [TP, T])
        rcnt = sb("rcnt", [TP, T])
        cnt_max = sb("cnt_max", [TP, 1])
        flag_f = sb("flag_f", [1, 1])
        flag = sb("flag", [1, 1], I32)
        work = sb("work", [128, OHR * 2 * T * OHW], BF16)
        onehot = work[:, :].rearrange("p (u s n) -> p u s n", u=OHR, s=2)
        workf = work[:, :].bitcast(F32)

        def scratch(n):
            return workf[:, n * BW:(n + 1) * BW]

        ctx_f = scratch(2).rearrange("p (j e) -> p j e", j=J)
        act_dump = scratch(3)

        def mo_tmp(i):
            return scratch(i % 3)[0:TP, :]

        pos_sq = scratch(4).rearrange("p (k n) -> p k n", k=K)
        attn_t = sb("attn", [TP, T, EXPERTS])
        h = sb("h", [TP, T, D])
        xm_t = sb("xm", [128, T * BW])
        xm = xm_t[0:TP, :].rearrange("p (t n) -> p t n", t=T)
        k_exp = xm_t[:, 0:J * TT].rearrange("p (j n) -> p j n", j=J)
        R = [[sb(f"r{n}_{part}", [128, T * BW], F32R) for part in ("hi", "lo")] for n in range(3)]

        def cols(n):
            return [a[:, 0:K * TT].rearrange("p (k n) -> p k n", k=K) for a in R[n]]

        def rows(n):
            return [a[0:TP, :].rearrange("p (t n) -> p t n", t=T) for a in R[n]]

        xr_c, s_c, x2_c = cols(0), cols(0), cols(0)
        kn_r, q_c, h_r = rows(1), cols(1), rows(1)
        v_r, o_c, h_c = rows(2), cols(0), cols(2)
        acc_c = cols(1)

        def sum_part(a, n):
            chunks, at = SUMS[n]
            return a[:, chunks[0]:chunks[-1] + 1, at]

        pos_hl = [a[:, 0:K * EXPERTS].rearrange("p (k n) -> p k n", k=K) for a in R[2]]
        split_w = [[sb(f"w{n}_{part}", [128, K, D], F32R) for part in ("hi", "lo")] for n in range(2)]
        layer_rows = sb("layer_rows", [TP, 2, 3, D])
        b_out_row = sb("b_out_row", [TP, D])
        out_norm_row = sb("out_norm_row", [TP, D])
        out_b_row = sb("out_b_row", [TP, D])
        scales_row = sb("scales_row", [TP, EXPERTS])
        p2_row = sb("p2_row", [TP, EXPERTS])
        ln_eps = sb("ln_eps", [TP, 1])
        a_col = sb("a_col", [128, 1])
        nw_col = sb("nw_col", [128, K])
        memk = sb("memk", [128, J, NMEM])
        memk_exp = sb("memk_exp", [128, J, NMEM])
        memk_n = sb("memk_n", [NMEM, D])
        memv = sb("memv", [NMEM, D])
        pos = sb("pos", [128, K, EXPERTS])
        ctx_hl = [sb(f"ctx_{part}", [128, J, 128], F32R) for part in ("hi", "lo")]
        bn6 = sb("bn6", [TP, NLN, 6])
        mean_var = sb("mean_var", [TP, NLN, 2])
        ln_std = sb("ln_std", [TP, NLN])
        ln_rstd = sb("ln_rstd", [TP, NLN])
        xr_norm = sb("xr_norm", [TP, 3, T])
        mo_norm = sb("mo_norm", [TP, 3, T])
        k_max = sb("k_max", [128, J, 3])
        k_neg = sb("k_neg", [128, J])
        k_sum = sb("k_sum", [128, J, 3])
        k_rsum = sb("k_rsum", [128, J])
        q_max = sb("q_max", [TP, T, HEADS])
        q_sum = sb("q_sum", [TP, T, HEADS])
        x2_sq = sb("x2_sq", [TP, T])
        a_max = sb("a_max", [TP, T])
        a_sum = sb("a_sum", [TP, T])
        raw = [sb(f"raw{n}", [128, K, D]) for n in range(2)]
        graph = ExitStack()
        adj = [sb(f"adj_{part}", [TP, T, TT], F32R, graph) for part in ("hi", "lo")]
        graph.close()
        raw += [sb(f"raw{n}", [128, K, D]) for n in range(2, U)]
        first = sb("first", [TP, T - 1, D])

        def first_tile(t):
            return first[:, t, :] if t < T - 1 else scratch(1)[0:TP, :]


        psum = ctx.enter_context(nc.psum_tensor("psum", [128, BANKS * BW], F32))

        def bank_at(n):
            return psum[:, (n % BANKS) * BW:(n % BANKS + 1) * BW]

        def bank(*name):
            return bank_at(BANK[JOB[name]])

        def transposed(b):
            return b[:, 0:K * TW].rearrange("p (k n) -> p k n", k=K)

        def count_psum(b):
            first = (4 + 2 * (b % 2)) * BW
            return psum[0:TP, first:first + T * OHW].rearrange("p (t n) -> p t n", t=T)

        def degree_psum(b):
            first = (4 + 2 * (b % 2)) * BW + T * OHW
            return psum[0:TP, first:first + 2]

        sum_bank = bank_at

        def sum_psum(n):
            chunks, at = SUMS[n]
            width = at.stop - at.start
            return sum_bank(n)[:, 0:len(chunks) * width].rearrange("p (m n) -> p m n", m=len(chunks))

        layer_bank = bank_at
        expert_bank = bank_at
        dots_bank = bank_at(T)

        TAIL = [("aT", 0)]
        for i in range(1, T):
            TAIL += [("aT", i), ("fo", i - 1)]
        TAIL += [("fo", T - 1)]

        def tail_after(*name):
            return TAIL.index(name) + 1

        def tail_bank(*name):
            return bank_at(T + TAIL.index(name))

        groups_loaded = sem("groups_loaded")
        edges_loaded = sem("edges_loaded")
        x_loaded = [sem(f"x_loaded{i}") for i in range(T)]
        x_again = sem("x_again")
        rows_loaded = sem("rows_loaded")
        layer_rows_loaded = [sem(f"layer_rows_loaded{n}") for n in range(2)]
        mem_loaded = sem("mem_loaded")
        pos_loaded = sem("pos_loaded")
        raw_loaded = [sem(f"raw_loaded{n}") for n in range(U)]
        stage_hi = sem("stage_hi")
        stage_split = sem("stage_split")
        iota_ready = sem("iota_ready")
        const_ready = sem("const_ready")
        eps_ready = sem("eps_ready")
        pads_ready = sem("pads_ready")
        onehots_ready = sem("onehots_ready")
        cand_ready = sem("cand_ready")
        edges_cast = sem("edges_cast")
        slots_free = sem("slots_free")
        cnt_max_ready = sem("cnt_max_ready")
        expert_split = sem("expert_split")
        sums_full = sem("sums_full")
        sums_hi = sem("sums_hi")
        sums_free = sem("sums_free")
        layer_full = sem("layer_full")
        layer_free = sem("layer_free")
        dots_full = sem("dots_full")
        q_sum_ready = sem("q_sum_ready")
        mo_scaled = sem("mo_scaled")
        counted = sem("counted")
        adj_hi = sem("adj_hi")
        adj_split = sem("adj_split")
        var_ready = sem("var_ready")
        std_ready = sem("std_ready")
        xn_ready = sem("xn_ready")
        xr_norm_ready = sem("xr_norm_ready")
        xr_ready = sem("xr_ready")
        xr_scale_ready = sem("xr_scale_ready")
        bank_full = sem("bank_full")
        bank_free = sem("bank_free")
        hi_ready = sem("hi_ready")
        k_max_ready = sem("k_max_ready")
        k_exp_ready = sem("k_exp_ready")
        ctx_hi_ready = sem("ctx_hi_ready")
        ctx_split = sem("ctx_split")
        q_exp_ready = sem("q_exp_ready")
        q_ready = sem("q_ready")
        mo_norm_ready = sem("mo_norm_ready")
        h_ready = sem("h_ready")
        h_hi_ready = sem("h_hi_ready")
        h_split = sem("h_split")
        h_biased = sem("h_biased")
        pos_sq_ready = sem("pos_sq_ready")
        xm_ready = sem("xm_ready")
        pos_hi_ready = sem("pos_hi_ready")
        pos_split = sem("pos_split")
        x2n_ready = sem("x2n_ready")
        x2_ready = sem("x2_ready")
        dots_scaled = sem("dots_scaled")
        first_taken = sem("first_taken")
        x2_sq_ready = sem("x2_sq_ready")
        dist_ready = sem("dist_ready")
        logits_ready = sem("logits_ready")
        exps_ready = sem("exps_ready")
        tile_full = sem("tile_full")
        tile_free = sem("tile_free")
        tail_full = sem("tail_full")
        tail_hi = sem("tail_hi")
        tail_free = sem("tail_free")
        out_ready = sem("out_ready")
        stored = sem("stored")
        dve_step = sem("dve_step")
        act_step = sem("act_step")
        pool_step = sem("pool_step")

        def group_range(engine, b):
            return [engine.value_load(bounds[0:1, s, b:b + 1], min_val=s, max_val=EG - 1 + s) for s in range(2)]

        block = ctx.enter_context(nc.Block())

        @block.sync
        def _(sp):
            def load_stage(s):
                n = s - PRE
                if 2 <= s < PRE + 2:
                    sp.wait_ge(stage_split, s - 1)
                elif 2 <= n < U:
                    sp.wait_ge(sums_full, len(SUMS) * LAYERS)
                elif U <= n < U + BY_DVE:
                    sp.wait_ge(stage_split, s - U + 1)
                elif n >= U + BY_DVE:
                    sp.wait_ge(expert_split, n - U - BY_DVE + 1)
                source = stage_src[s] if s in stage_src else value_w[n].rearrange(kp, k=K)
                sp.dma_start(raw[raw_slot(s)][:, :, :], source).then_inc(raw_loaded[raw_slot(s)], 16)

            sp.dma_start(groups_i[:, :], dst.rearrange("(g e) -> g e", g=EG)).then_inc(groups_loaded, 16)
            sp.dma_start(edges_i[:, 0, :], src.rearrange("(c p) -> c p", p=TP)).then_inc(edges_loaded, 16)
            sp.dma_start(edges_i[:, 1, :], dst.rearrange("(c p) -> c p", p=TP)).then_inc(edges_loaded, 16)
            for i in range(T):
                sp.dma_start(h[:, i, :], x[i * TP:(i + 1) * TP, :]).then_inc(x_loaded[i], 16)
            load_stage(0)
            load_stage(1)
            sp.dma_start(nw_col[:, :], norm_w.rearrange("(p k) -> p k", k=K)).then_inc(mem_loaded, 16)
            sp.dma_start(memk[:, :, :], mem_k.rearrange("(j p) m -> p j m", p=128)).then_inc(mem_loaded, 16)
            sp.dma_start(memv[:, :], mem_v).then_inc(mem_loaded, 16)

            def row(dest, source, done):
                sp.dma_start(dest, source.partition_broadcast(TP)).then_inc(done, 16)

            row(b_out_row[:, :], b_out, rows_loaded)
            row(out_norm_row[:, :], out_norm_w, rows_loaded)
            row(out_b_row[:, :], out_b, rows_loaded)
            row(scales_row[:, :], scales, rows_loaded)
            sp.dma_start(a_col[:, :], a_prelu.partition_broadcast(128)).then_inc(rows_loaded, 16)
            for l in range(2):
                for n, source in enumerate(gnn_rows[l]):
                    row(layer_rows[:, l, n, :], source, layer_rows_loaded[l])
            sp.dma_start(pos[:, :, :], pos_t.rearrange(kp, k=K)).then_inc(pos_loaded, 16)
            load_stage(2)
            load_stage(3)
            load_stage(4)
            sp.wait_ge(bank_full, after("qT", T - 1))
            sp.dma_start(xm, x.rearrange("(t p) n -> p t n", p=TP)).then_inc(x_again, 16)
            for s in range(5, 8):
                load_stage(s)
            for l in range(2, LAYERS):
                sp.wait_ge(h_ready, T * (l - 1))
                for n, source in enumerate(gnn_rows[l]):
                    row(layer_rows[:, l % 2, n, :], source, layer_rows_loaded[l % 2])
            for s in range(8, PRE + 2 * U):
                load_stage(s)
            with sp.Fori(2, EXPERTS // U) as i:
                for u in range(U):
                    sp.wait_ge(expert_split, i * U + (u - U - BY_DVE + 1))
                    sp.dma_start(raw[u][:, :, :],
                                 value_w[bass.ds(i * U + u, 1)].rearrange("o (p k) n -> p (o k) n", k=K))\
                      .then_inc(raw_loaded[u], 16)
            load_stage(stage_out)
            for i in range(T):
                sp.wait_ge(out_ready, i + 1)
                sp.dma_start(out[i * TP:(i + 1) * TP, :], xm[:, i, :]).then_inc(stored, 16)
            sp.wait_ge(stored, 16 * T)

        @block.gpsimd
        def _(pool):
            steps = [0]

            def link(ins):
                steps[0] += 1
                ins.then_inc(pool_step, 1)
                pool.wait_ge(pool_step, steps[0])

            pool.iota(block_no[:, :, :], [[TP, 2], [TP, T]], base=0, channel_multiplier=0,
                      allow_small_or_imprecise_dtypes=True).then_inc(iota_ready, 1)
            pool.iota(group_no[:, 0:1], [[1, 1]], base=EG - 1, channel_multiplier=-1,
                      allow_small_or_imprecise_dtypes=True).then_inc(iota_ready, 1)
            pool.iota(group_no[:, 1:2], [[1, 1]], base=1, channel_multiplier=1,
                      allow_small_or_imprecise_dtypes=True).then_inc(iota_ready, 1)
            link(pool.memset(ident[:, :], 0.0))
            pool.affine_select(out=ident[:, :], in_=ident[:, :], compare_op=ALU.not_equal, fill=1.0,
                               base=0, pattern=[[-1, 128]], channel_multiplier=1).then_inc(const_ready, 1)
            tiles = iota[:, :].rearrange("p (t n) -> p t n", t=T)
            link(pool.iota(tiles, [[TP, T], [1, OHW]], base=0, channel_multiplier=0))
            pool.memset(tiles[:, :, TP:OHW], -1).then_inc(iota_ready, 1)
            pool.memset(ln_eps[:, :], LN_EPS).then_inc(eps_ready, 1)
            pool.memset(zeros[:, :], 0.0).then_inc(const_ready, 1)
            pool.memset(ones[:, :], 1.0).then_inc(const_ready, 1)
            pool.memset(ones_b[:, :], 1.0).then_inc(const_ready, 1)
            for n in range(2):
                for a in R[n]:
                    pool.memset(a[:, :].bitcast(F32), 0.0).then_inc(pads_ready, 1)

            def split_stage(s):
                pool.wait_ge(stage_hi, s + 1)
                hi, lo = split_w[s % 2]
                pool.tensor_tensor(lo[:, :, :], raw[raw_slot(s)][:, :, :], hi[:, :, :].bitcast(F32),
                                   ALU.subtract).then_inc(stage_split, 1)

            def h_lo(l, i):
                pool.wait_ge(h_hi_ready, T * l + i + 1)
                pool.tensor_tensor(h_r[1][:, i, :], h[:, i, :], h_r[0][:, i, :].bitcast(F32), ALU.subtract)\
                    .then_inc(h_split, 1)

            def h_bias(l, i):
                pool.wait_ge(bank_full, after("hT", l, i))
                pool.wait_ge(h_split, T * l + i + 1)
                pool.tensor_tensor(h[:, i, :], h[:, i, :], layer_rows[:, l % 2, 0, :], ALU.add)\
                    .then_inc(h_biased, 1)

            def q_scale(i):
                pool.wait_ge(q_sum_ready, i + 1)
                q = xm[:, i, :].rearrange("p (h c) -> p h c", c=C)
                pool.tensor_tensor(q, q, q_sum[:, i, :].unsqueeze(2).to_broadcast([TP, HEADS, C]), ALU.mult)\
                    .then_inc(q_ready, 1)

            for s in (stage_k, stage_v, stage_q, stage_o):
                split_stage(s)
            for i in range(T):
                q_scale(i)
            split_stage(stage_r(0))
            for i in range(T + 2):
                if i < T:
                    h_lo(0, i)
                if i == 2:
                    pool.wait_ge(x_again, 16)
                if i >= 2:
                    pool.wait_ge(mo_scaled, i - 1)
                    pool.tensor_tensor(xm[:, i - 2, :], xm[:, i - 2, :], mo_tmp(i - 2), ALU.add)\
                        .then_inc(xm_ready, 1)
            split_stage(stage_l(0))
            for l in range(1, LAYERS):
                pool.wait_ge(layer_rows_loaded[l % 2], 48 * (l // 2 + 1))
                split_stage(stage_r(l))
                for step, i in LAYER_STEPS:
                    if step == "norm":
                        h_lo(l, i)
                    elif step == "hT":
                        h_bias(l, i)
                split_stage(stage_l(l))
            pool.wait_ge(pos_hi_ready, 1)
            pool.tensor_tensor(pos_hl[1], pos[:, :, :], pos_hl[0].bitcast(F32), ALU.subtract).then_inc(pos_split, 1)
            split_stage(PRE)
            for i in range(T):
                pool.wait_ge(h_ready, T * (LAYERS - 1) + i + 1)
                pool.tensor_tensor(xm[:, i, :], xm[:, i, :], h[:, i, :], ALU.add).then_inc(x2_ready, 1)
                if i == 3:
                    split_stage(PRE + 1)
            split_stage(PRE + 2)

        @block.scalar
        def _(act):
            steps = [0]

            def link(ins):
                steps[0] += 1
                ins.then_inc(act_step, 1)
                act.wait_ge(act_step, steps[0])

            def wait_stage_used(s):
                if s < PRE:
                    last = {stage_k: ("kTb", J - 1), stage_v: ("v", T - 1), stage_q: ("q", T - 1),
                            stage_o: ("mo", T - 1)}
                    last |= {stage_r(l): ("zR", l, T - 1) for l in range(LAYERS)}
                    if s in last:
                        act.wait_ge(bank_full, after(*last[s]))
                    else:
                        act.wait_ge(layer_full, T * ((s - 5) // 2 + 1))
                else:
                    act.wait_ge(tile_full, T * (s - PRE + 1))

            def split_stage(s):
                act.wait_ge(raw_loaded[raw_slot(s)], 16 * raw_loads(s))
                if s >= 2:
                    wait_stage_used(s - 2)
                act.activation(split_w[s % 2][0][:, :, :], raw[raw_slot(s)][:, :, :], ACT.Copy)\
                   .then_inc(stage_hi, 1)

            def ln_std_of(n):
                act.wait_ge(var_ready, n + 1)
                act.activation(ln_std[:, n:n + 1], mean_var[:, n, 1:2], ACT.Sqrt, bias=ln_eps[:, :])\
                   .then_inc(std_ready, 1)

            def hi_of(job, dest, source):
                act.wait_ge(bank_full, after(*job))
                act.activation(dest, source, ACT.Copy).then_inc(hi_ready, 1)

            def hi_of_tile(job, i, dest):
                hi_of(job, dest[0][:, :, i * TW:i * TW + TP], transposed(bank(*job))[:, :, 0:TP])

            def h_hi(l, i):
                if l == 0:
                    act.wait_ge(xn_ready, i + 1)
                else:
                    act.wait_ge(h_ready, T * (l - 1) + i + 1)
                act.activation(h_r[0][:, i, :], h[:, i, :], ACT.Copy).then_inc(h_hi_ready, 1)

            def adj_hi_of(b):
                act.wait_ge(counted, b + 1)
                act.activation(adj[0][:, :, b * TW:(b + 1) * TW], count_psum(b)[:, :, 0:TW], ACT.Copy)\
                   .then_inc(adj_hi, 1)

            def k_exp_of(j):
                act.wait_ge(k_max_ready, j + 1)
                for n, (name, at, width) in enumerate((("kTa", 0, SA), ("kTb", SA, SB))):
                    act.activation(k_exp[:, j, at:at + width].rearrange("p (t n) -> p t n", n=TW)[:, :, 0:TP],
                                   bank(name, j)[:, 0:width].rearrange("p (t n) -> p t n", n=TW)[:, :, 0:TP],
                                   ACT.Exp, bias=k_neg[:, j:j + 1], accum_out=k_sum[:, j, n:n + 1])
                act.activation(memk_exp[:, j, :], memk[:, j, :], ACT.Exp, bias=k_neg[:, j:j + 1],
                               accum_out=k_sum[:, j, 2:3]).then_inc(k_exp_ready, 1)

            def xr_hi(i):
                act.wait_ge(bank_full, after("xrT", i))
                for k in range(K):
                    ins = act.activation(xr_c[0][:, k, i * TW:i * TW + TP], transposed(bank("xrT", i))[:, k, 0:TP],
                                         ACT.Copy, scale=nw_col[:, k:k + 1])
                ins.then_inc(hi_ready, 1)

            act.wait_ge(eps_ready, 1)
            for i in range(T):
                ln_std_of(ln_index(0, i))
            for i in range(T):
                act.wait_ge(xn_ready, i + 1)
                ins = act.activation(xm[:, i, :], h[:, i, :], ACT.Square, accum_out=xr_norm[:, 0, i:i + 1])
            link(ins)
            act.activation(xr_norm[:, 1, :], xr_norm[:, 0, :], ACT.Sqrt).then_inc(xr_norm_ready, 1)
            act.wait_ge(xr_scale_ready, 1)
            for i in range(T):
                act.activation(xm[:, i, :], h[:, i, :], ACT.Copy, scale=xr_norm[:, 2, i:i + 1]).then_inc(xr_ready, 1)
            adj_hi_of(0)
            act.wait_ge(pads_ready, 4)
            act.wait_ge(mem_loaded, 48)
            for i in range(T - 1):
                xr_hi(i)
            split_stage(stage_k)
            adj_hi_of(1)
            xr_hi(T - 1)
            split_stage(stage_v)
            adj_hi_of(2)
            k_exp_of(0)
            adj_hi_of(3)
            k_exp_of(1)
            adj_hi_of(4)
            k_exp_of(2)
            k_exp_of(3)
            split_stage(stage_q)
            for i in range(T):
                hi_of(("v", i), v_r[0][:, i, :], bank("v", i)[0:TP, :])
            for i in range(T):
                hi_of(("kN", i), kn_r[0][:, i, :], bank("kN", i)[0:TP, :])
            split_stage(stage_o)

            def q_exp(i):
                act.wait_ge(bank_free, after("q", i))
                act.activation(xm[:, i, :], xm[:, i, :], ACT.Exp).then_inc(q_exp_ready, 1)

            def h_turned_hi(i):
                hi_of_tile(("hT", 0, i), i, h_c)

            def q_turned_hi(i):
                hi_of_tile(("qT", i), i, q_c)

            for i in range(4):
                q_exp(i)
            act.wait_ge(bank_free, after("ctx", 0))
            act.activation(ctx_hl[0][:, :, :], ctx_f, ACT.Copy).then_inc(ctx_hi_ready, 1)
            h_turned_hi(0)
            h_turned_hi(1)
            q_turned_hi(0)
            q_turned_hi(1)
            q_turned_hi(2)
            q_exp(4)
            for j in range(J):
                hi_of(("oTa", j), o_c[0][:, j, 0:SA], bank("oTa", j)[:, 0:SA])
            h_turned_hi(2)
            q_turned_hi(3)
            q_turned_hi(4)
            h_turned_hi(3)
            for j in range(J):
                hi_of(("oTb", j), o_c[0][:, j, SA:TT], bank("oTb", j)[:, 0:SB])
            h_turned_hi(4)
            split_stage(stage_r(0))
            for i in range(T):
                h_hi(0, i)

            def mo_rms(i):
                act.wait_ge(bank_free, after("mo", i))
                link(act.activation(act_dump[0:TP, :], mo_tmp(i), ACT.Square,
                                    accum_out=mo_norm[:, 0, i:i + 1]))
                act.activation(mo_norm[:, 1, i:i + 1], mo_norm[:, 0, i:i + 1], ACT.Sqrt)\
                   .then_inc(mo_norm_ready, 1)

            for i in range(T):
                mo_rms(i)
            split_stage(stage_l(0))

            def take_first(t):
                act.wait_ge(tile_full, t + 1)
                act.activation(first_tile(t), expert_bank(t)[0:TP, :], ACT.Copy).then_inc(first_taken, 1)

            for l in range(LAYERS):
                for n, (chunks, at) in enumerate(SUMS):
                    act.wait_ge(sums_full, len(SUMS) * l + n + 1)
                    act.activation(sum_part(s_c[0], n), sum_psum(n), ACT.Copy).then_inc(sums_hi, 1)
                last = l == LAYERS - 1
                if last:
                    act.wait_ge(pos_loaded, 16)
                    act.wait_ge(bank_full, after("zR", l, T - 1))
                    act.activation(pos_hl[0], pos[:, :, :], ACT.Copy).then_inc(pos_hi_ready, 1)
                split_stage(stage_r(l + 1))
                for step, i in LAST_STEPS if last else LAYER_STEPS:
                    if step == "stats":
                        ln_std_of(ln_index(1 + l, i))
                    elif step == "stats2":
                        ln_std_of(ln_index(1 + LAYERS, i))
                    elif step == "norm" and not last:
                        h_hi(l + 1, i)
                    elif step == "norm2":
                        act.wait_ge(x2n_ready, i + 1)
                        act.activation(act_dump[0:TP, :], h[:, i, :], ACT.Square,
                                       accum_out=x2_sq[:, i:i + 1]).then_inc(x2_sq_ready, 1)
                    elif step == "hT":
                        hi_of_tile(("hT", l + 1, i), i, h_c)
                    elif step == "x2T":
                        hi_of_tile(("x2T", i), i, x2_c)
                    if step == "x2T" and i >= 2:
                        take_first(i - 2)
                    if (step, i) == ("norm2", 2):
                        split_stage(PRE + 1)
                if not last:
                    split_stage(stage_l(l + 1))
            take_first(T - 2)
            act.wait_ge(x2_sq_ready, T)
            for t in range(T):
                act.wait_ge(dots_scaled, 1 if t < T - 1 else 2)
                ins = act.activation(attn_t[:, t, :], attn_t[:, t, :], ACT.Relu, bias=x2_sq[:, t:t + 1])
            link(ins)
            act.activation(attn_t[:, :, :], attn_t[:, :, :], ACT.Sqrt).then_inc(dist_ready, 1)
            take_first(T - 1)
            split_stage(PRE + 2)
            for t in range(T):
                act.wait_ge(logits_ready, t + 1)
                act.activation(attn_t[:, t, :], attn_t[:, t, :], ACT.Exp, bias=a_max[:, t:t + 1],
                               accum_out=a_sum[:, t:t + 1]).then_inc(exps_ready, 1)
            with act.Fori(0, EXPERTS // U - 1) as i:
                for u in range(U):
                    m = u + BY_DVE
                    slot = m % U
                    act.wait_ge(raw_loaded[slot], i * 16 + 16 * raw_loads(PRE + m))
                    act.wait_ge(tile_full, i * (U * T) + (m - 1) * T)
                    act.activation(split_w[m % 2][0][:, :, :], raw[slot][:, :, :], ACT.Copy).then_inc(stage_hi, 1)
            for s in range(PRE + EXPERTS - U + BY_DVE, stage_out + 1):
                split_stage(s)
            for i in range(T):
                act.wait_ge(tail_full, tail_after("aT", i))
                act.activation(acc_c[0][:, :, i * TW:i * TW + TP], transposed(tail_bank("aT", i))[:, :, 0:TP],
                               ACT.Copy).then_inc(tail_hi, 1)

        @block.vector
        def _(dve):
            steps = [0]

            def link(ins):
                steps[0] += 1
                ins.then_inc(dve_step, 1)
                dve.wait_ge(dve_step, steps[0])

            def minus_hi(dest, source, hi):
                return dve.tensor_tensor(dest, source, hi.bitcast(F32), ALU.subtract)

            def split_expert(n):
                s = PRE + n
                dve.wait_ge(stage_hi, s + 1)
                minus_hi(split_w[s % 2][1][:, :, :], raw[raw_slot(s)][:, :, :], split_w[s % 2][0][:, :, :])\
                    .then_inc(expert_split, 1)

            def lo_of(job, pair, source, at):
                dve.wait_ge(hi_ready, hi_after(*job))
                minus_hi(at(pair[1]), source, at(pair[0])).then_inc(bank_free, 1)

            def lo_of_tile(job, i, pair):
                lo_of(job, pair, transposed(bank(*job))[:, :, 0:TP], lambda a: a[:, :, i * TW:i * TW + TP])

            def onehots(chunk, slot, tile):
                dve.tensor_scalar(onehot[0:TP, slot, 0, :], iota[0:TP, :], edge[:, 0, bass.ds(chunk, 1)], None,
                                  ALU.is_equal)
                at = slice(tile * OHW, (tile + 1) * OHW)
                dve.tensor_scalar(onehot[0:TP, slot, 1, at], iota[0:TP, at], edge[:, 1, bass.ds(chunk, 1)], None,
                                  ALU.is_equal).then_inc(onehots_ready, 1)

            def ln_stats(n, source):
                link(dve.bn_stats(bn6[:, n, :], source))
                dve.bn_aggr(mean_var[:, n, :], bn6[:, n, :]).then_inc(var_ready, 1)

            def ln_rstd_of(n, last=None):
                last = n if last is None else last
                dve.wait_ge(std_ready, last + 1)
                link(dve.reciprocal(ln_rstd[:, n:last + 1], ln_std[:, n:last + 1]))

            def ln_apply(n, dest, source):
                return dve.tensor_scalar(dest, source, mean_var[:, n, 0:1], ln_rstd[:, n:n + 1],
                                         ALU.subtract, ALU.mult)

            def root_d_over(norms, at, done=None):
                link(dve.tensor_scalar(norms[:, 1, at], norms[:, 1, at], RMS_EPS, None, ALU.max))
                link(dve.reciprocal(norms[:, 2, at], norms[:, 1, at]))
                ins = dve.tensor_scalar(norms[:, 2, at], norms[:, 2, at], ROOT_D, None, ALU.mult)
                if done is None:
                    link(ins)
                else:
                    ins.then_inc(done, 1)

            dve.wait_ge(groups_loaded, 16)
            dve.tensor_reduce(extent[:, 0:1], groups_i[:, :], AX.X, ALU.max)
            link(dve.tensor_reduce(extent[:, 1:2], groups_i[:, :], AX.X, ALU.min))
            dve.wait_ge(iota_ready, 3)
            dve.tensor_scalar(cand[:, 0, :], block_no[:, 0, :], extent[:, 0:1], group_no[:, 0:1],
                              ALU.is_le, ALU.mult).then_inc(cand_ready, 1)
            dve.tensor_scalar(cand[:, 1, :], block_no[:, 1, :], extent[:, 1:2], group_no[:, 1:2],
                              ALU.is_gt, ALU.mult).then_inc(cand_ready, 1)
            dve.wait_ge(edges_loaded, 32)
            dve.tensor_copy(edges_f[:, :, :], edges_i[:, :, :]).then_inc(edges_cast, 1)
            dve.wait_ge(bank_full, after("range", 0))
            dve.tensor_reduce(cand_max[:, :], bank("range", 0)[0:2 * T, 0:EG], AX.X, ALU.max).then_inc(bank_free, 1)
            dve.wait_ge(bank_full, after("edgeT", 0))
            dve.tensor_copy(edge[:, :, :], bank("edgeT", 0)[0:TP, 0:2 * EC].rearrange("p (s c) -> p s c", s=2))\
               .then_inc(bank_free, 1)
            dve.wait_ge(bank_full, after("range", 1))
            link(dve.tensor_copy(bounds_f[:, :, :],
                                 bank("range", 1)[0:1, 0:2 * T].rearrange("p (s b) -> p s b", s=2)))
            link(dve.tensor_scalar(bounds_f[:, 0, :], bounds_f[:, 0, :], -1.0, float(EG - 1), ALU.mult, ALU.add))
            link(dve.scalar_tensor_tensor(out=bounds_f[:, 1, :], in0=bounds_f[:, 0, :], scalar=1.0,
                                          in1=bounds_f[:, 1, :], op0=ALU.add, op1=ALU.max))
            dve.tensor_copy(bounds[:, :, :], bounds_f[:, :, :]).then_inc(bank_free, 1)
            for i in range(T):
                dve.wait_ge(x_loaded[i], 16)
                ln_stats(ln_index(0, i), h[:, i, :])
            ln_rstd_of(ln_index(0, 0), ln_index(0, T - 1))
            for i in range(T):
                ln_apply(ln_index(0, i), h[:, i, :], h[:, i, :]).then_inc(xn_ready, 1)
            dve.wait_ge(bank_free, after("range", 1))
            built = dve.alloc_register("onehots_built")
            dve.reg_mov(built, 0)

            def onehot_loop(b):
                with dve.Fori(*group_range(dve, b)) as g:
                    so_far = dve.snap(built)
                    for u in range(OHR):
                        dve.wait_ge(slots_free, so_far + (u + 1))
                        onehots(g * OHR + u, u, b)
                    dve.reg_add(built, built, OHR)

            def adj_lo_of(b):
                dve.wait_ge(adj_hi, b + 1)
                at = slice(b * TW, (b + 1) * TW)
                dve.tensor_copy(in_degree[:, b:b + 1], degree_psum(b)[:, 0:1])
                minus_hi(adj[1][:, :, at], count_psum(b)[:, :, 0:TW], adj[0][:, :, at]).then_inc(adj_split, 1)

            def k_max_of(j):
                for n, (name, width) in enumerate((("kTa", SA), ("kTb", SB))):
                    dve.wait_ge(bank_full, after(name, j))
                    dve.tensor_reduce(k_max[:, j, n:n + 1],
                                      bank(name, j)[:, 0:width].rearrange("p (t n) -> p t n", n=TW)[:, :, 0:TP],
                                      AX.XY, ALU.max)
                link(dve.tensor_reduce(k_max[:, j, 2:3], memk[:, j, :], AX.X, ALU.max))
                dve.tensor_reduce(k_neg[:, j:j + 1], k_max[:, j, :], AX.X, ALU.max, negate=True)\
                   .then_inc(k_max_ready, 1)

            def k_sum_of(j):
                dve.wait_ge(k_exp_ready, j + 1)
                link(dve.tensor_reduce(k_rsum[:, j:j + 1], k_sum[:, j, :], AX.X, ALU.add))
                dve.reciprocal(k_rsum[:, j:j + 1], k_rsum[:, j:j + 1]).then_inc(bank_free, 2)

            dve.wait_ge(iota_ready, 4)
            dve.wait_ge(xr_norm_ready, 1)
            root_d_over(xr_norm, slice(0, T), xr_scale_ready)
            onehot_loop(0)
            adj_lo_of(0)
            onehot_loop(1)
            for i in range(T):
                dve.wait_ge(hi_ready, hi_after("xrT", i))
                for k in range(K):
                    at = slice(i * TW, i * TW + TP)
                    ins = dve.scalar_tensor_tensor(out=xr_c[1][:, k, at], in0=transposed(bank("xrT", i))[:, k, 0:TP],
                                                   scalar=nw_col[:, k:k + 1], in1=xr_c[0][:, k, at].bitcast(F32),
                                                   op0=ALU.mult, op1=ALU.subtract)
                ins.then_inc(bank_free, 1)
            onehot_loop(2)
            adj_lo_of(1)
            k_max_of(0)
            onehot_loop(3)
            adj_lo_of(2)
            k_sum_of(0)
            k_max_of(1)
            onehot_loop(4)
            adj_lo_of(3)
            k_sum_of(1)
            k_max_of(2)
            adj_lo_of(4)
            dve.wait_ge(adj_split, T)
            dve.tensor_reduce(cnt_max[:, :], in_degree[:, :], AX.X, ALU.max).then_inc(cnt_max_ready, 1)
            link(dve.tensor_scalar(rcnt[:, :], in_degree[:, :], 1.0, None, ALU.max))
            dve.reciprocal(rcnt[:, :], rcnt[:, :])
            k_sum_of(2)
            k_max_of(3)
            dve.memset(ctx_f, 0.0)
            dve.wait_ge(pos_loaded, 16)
            dve.tensor_tensor(pos_sq, pos[:, :, :], pos[:, :, :], ALU.mult).then_inc(pos_sq_ready, 1)
            k_sum_of(3)
            for i in range(T):
                lo_of(("v", i), v_r, bank("v", i)[0:TP, :], lambda a: a[:, i, :])
            dve.wait_ge(bank_full, after("flag", 0))
            link(dve.tensor_reduce(flag_f[:, :], bank("flag", 0)[0:1, 0:TP], AX.X, ALU.max))
            dve.tensor_scalar(flag[:, :], flag_f[:, :], EXACT, None, ALU.is_gt).then_inc(bank_free, 1)
            dve.wait_ge(bank_full, after("p2", 0))
            dve.tensor_copy(p2_row[:, :], bank("p2", 0)[0:TP, 0:EXPERTS]).then_inc(bank_free, 1)
            for i in range(T):
                lo_of(("kN", i), kn_r, bank("kN", i)[0:TP, :], lambda a: a[:, i, :])
            dve.wait_ge(bank_full, after("kM", 0))
            dve.tensor_copy(memk_n[:, :], bank("kM", 0)[0:NMEM, :]).then_inc(bank_free, 1)

            def per_head(a):
                return a.rearrange("p (h c) -> p h c", c=C)

            def q_shift(i):
                dve.wait_ge(bank_full, after("q", i))
                link(dve.tensor_reduce(q_max[:, i, :], per_head(bank("q", i)[0:TP, :]), AX.X, ALU.max))
                dve.tensor_tensor(per_head(xm[:, i, :]), per_head(bank("q", i)[0:TP, :]),
                                  q_max[:, i, :].unsqueeze(2).to_broadcast([TP, HEADS, C]), ALU.subtract)\
                   .then_inc(bank_free, 1)

            def q_softmax(i):
                dve.wait_ge(q_exp_ready, i + 1)
                link(dve.tensor_reduce(q_sum[:, i, :], per_head(xm[:, i, :]), AX.X, ALU.add))
                link(dve.reciprocal(q_sum[:, i, :], q_sum[:, i, :]))
                dve.tensor_scalar(q_sum[:, i, :], q_sum[:, i, :], Q_SCALE, None, ALU.mult).then_inc(q_sum_ready, 1)

            def h_turned_lo(i):
                lo_of_tile(("hT", 0, i), i, h_c)

            def q_turned_lo(i):
                lo_of_tile(("qT", i), i, q_c)

            q_shift(0)
            q_shift(1)
            q_softmax(0)
            q_shift(2)
            q_softmax(1)
            q_shift(3)
            q_softmax(2)
            q_softmax(3)
            dve.wait_ge(bank_full, after("ctx", 0))
            ctx_psum = bank("ctx", 0).rearrange("p (j e) -> p j e", j=J)
            for half in range(2):
                at = slice(C * half, C * half + C)
                ins = dve.tensor_tensor(ctx_f[at, :, at], ctx_psum[at, :, at],
                                        k_rsum[at, :].unsqueeze(2).to_broadcast([C, J, C]), ALU.mult)
                if half == 0:
                    link(ins)
            ins.then_inc(bank_free, 1)
            dve.wait_ge(ctx_hi_ready, 1)
            minus_hi(ctx_hl[1][:, :, :], ctx_f, ctx_hl[0][:, :, :]).then_inc(ctx_split, 1)
            h_turned_lo(0)
            h_turned_lo(1)
            q_turned_lo(0)
            q_turned_lo(1)
            q_turned_lo(2)
            q_shift(4)
            for j in range(J):
                lo_of(("oTa", j), o_c, bank("oTa", j)[:, 0:SA], lambda a: a[:, j, 0:SA])
                if j == 0:
                    q_softmax(4)
            h_turned_lo(2)
            q_turned_lo(3)
            q_turned_lo(4)
            h_turned_lo(3)
            for j in range(J):
                lo_of(("oTb", j), o_c, bank("oTb", j)[:, 0:SB], lambda a: a[:, j, SA:TT])
            h_turned_lo(4)
            dve.wait_ge(rows_loaded, 80)
            def biased(i):
                dve.wait_ge(bank_full, after("mo", i))
                if i >= 3:
                    dve.wait_ge(xm_ready, i - 2)
                dve.tensor_tensor(mo_tmp(i), bank("mo", i)[0:TP, :], b_out_row[:, :], ALU.add).then_inc(bank_free, 1)

            def rms_scaled(i):
                dve.wait_ge(mo_norm_ready, i + 1)
                root_d_over(mo_norm, slice(i, i + 1))
                dve.scalar_tensor_tensor(out=mo_tmp(i), in0=mo_tmp(i), scalar=mo_norm[:, 2, i:i + 1],
                                         in1=out_norm_row[:, :], op0=ALU.mult, op1=ALU.mult).then_inc(mo_scaled, 1)

            biased(0)
            for i in range(1, T):
                biased(i)
                rms_scaled(i - 1)
            rms_scaled(T - 1)

            def root_product(l, i):
                dve.wait_ge(bank_full, after("zR", l, i))
                if l == 0:
                    dve.wait_ge(h_split, i + 1)
                    rest = layer_rows[:, 0, 0, :]
                else:
                    dve.wait_ge(h_biased, T * (l - 1) + i + 1)
                    rest = h[:, i, :]
                dve.tensor_tensor(h[:, i, :], bank("zR", l, i)[0:TP, :], rest, ALU.add).then_inc(bank_free, 1)

            dve.wait_ge(layer_rows_loaded[0], 48)
            for i in range(3):
                root_product(0, i)
            for l in range(LAYERS):
                last = l == LAYERS - 1
                for n in range(len(SUMS)):
                    dve.wait_ge(sums_hi, len(SUMS) * l + n + 1)
                    minus_hi(sum_part(s_c[1], n), sum_psum(n), sum_part(s_c[0], n)).then_inc(sums_free, 1)
                for i in range(3, T):
                    root_product(l, i)
                gain_row, shift_row = (layer_rows[:, l % 2, n, :] for n in (1, 2))
                dve.wait_ge(layer_rows_loaded[l % 2], 48 * (l // 2 + 1))
                for step, i in LAST_STEPS if last else LAYER_STEPS:
                    if step == "add":
                        dve.wait_ge(layer_full, T * l + i + 1)
                        dve.wait_ge(bank_free, after("zR", l, i))
                        dve.scalar_tensor_tensor(out=h[:, i, :], in0=layer_bank(i)[0:TP, :],
                                                 scalar=rcnt[:, i:i + 1], in1=h[:, i, :],
                                                 op0=ALU.mult, op1=ALU.add).then_inc(layer_free, 1)
                    elif step == "stats":
                        dve.wait_ge(layer_free, T * l + i + 1)
                        ln_stats(ln_index(1 + l, i), h[:, i, :])
                    elif step == "norm":
                        n = ln_index(1 + l, i)
                        tmp = scratch(0)[0:TP, :]
                        dve.wait_ge(var_ready, n + 1)
                        dve.scalar_tensor_tensor(out=h[:, i, :], in0=h[:, i, :], scalar=mean_var[:, n, 0:1],
                                                 in1=gain_row, op0=ALU.subtract, op1=ALU.mult)
                        ln_rstd_of(n)
                        link(dve.scalar_tensor_tensor(out=h[:, i, :], in0=h[:, i, :], scalar=ln_rstd[:, n:n + 1],
                                                      in1=shift_row, op0=ALU.mult, op1=ALU.add))
                        link(dve.tensor_scalar(tmp, h[:, i, :], 0.0, a_col[0:TP, 0:1], ALU.min, ALU.mult))
                        dve.scalar_tensor_tensor(out=h[:, i, :], in0=h[:, i, :], scalar=0.0, in1=tmp,
                                                 op0=ALU.max, op1=ALU.add).then_inc(h_ready, 1)
                    elif step == "stats2":
                        dve.wait_ge(x2_ready, i + 1)
                        ln_stats(ln_index(1 + LAYERS, i), xm[:, i, :])
                    elif step == "norm2":
                        n = ln_index(1 + LAYERS, i)
                        dve.wait_ge(var_ready, n + 1)
                        ln_rstd_of(n)
                        ln_apply(n, h[:, i, :], xm[:, i, :]).then_inc(x2n_ready, 1)
                    elif step == "hT":
                        lo_of_tile(("hT", l + 1, i), i, h_c)
                    elif step == "zR":
                        root_product(l + 1, i)
                    elif step == "x2T":
                        lo_of_tile(("x2T", i), i, x2_c)

            dve.wait_ge(dots_full, 1)
            dve.scalar_tensor_tensor(out=attn_t[:, 0:T - 1, :], in0=dots_bank[0:TP, :].rearrange(
                "p (t n) -> p t n", n=EXPERTS), scalar=-2.0,
                in1=p2_row[:, :].unsqueeze(1).to_broadcast([TP, T - 1, EXPERTS]),
                op0=ALU.mult, op1=ALU.add).then_inc(dots_scaled, 1)
            dve.wait_ge(bank_full, after("d", 1))
            dve.scalar_tensor_tensor(out=attn_t[:, T - 1, :], in0=bank("d", 1)[0:TP, 0:EXPERTS], scalar=-2.0,
                                     in1=p2_row[:, :], op0=ALU.mult, op1=ALU.add).then_inc(dots_scaled, 1)
            dve.wait_ge(dist_ready, 1)
            link(dve.tensor_scalar(attn_t[:, :, :], attn_t[:, :, :], 0.1, None, ALU.add))
            link(dve.reciprocal(attn_t[:, :, :], attn_t[:, :, :]))
            link(dve.tensor_tensor(attn_t[:, :, :], attn_t[:, :, :],
                                   scales_row[:, :].unsqueeze(1).to_broadcast([TP, T, EXPERTS]), ALU.mult))
            for t in range(T):
                dve.tensor_reduce(a_max[:, t:t + 1], attn_t[:, t, :], AX.X, ALU.max, negate=True)\
                   .then_inc(logits_ready, 1)
            dve.wait_ge(exps_ready, T)
            link(dve.reciprocal(a_sum[:, :], a_sum[:, :]))
            for t in range(T):
                ins = dve.tensor_scalar(attn_t[:, t, :], attn_t[:, t, :], a_sum[:, t:t + 1], None, ALU.mult)
            link(ins)

            for t in range(T):
                dve.wait_ge(first_taken, t + 1)
                dve.tensor_scalar(h[:, t, :], first_tile(t), attn_t[:, t, 0:1], None, ALU.mult)\
                   .then_inc(tile_free, 1)

            def gather(before, expert):
                for t in range(T):
                    dve.wait_ge(tile_full, before + (t + 1))
                    dve.wait_ge(tile_free, before + (t + 1 - T))
                    dve.scalar_tensor_tensor(out=h[:, t, :], in0=expert_bank(t)[0:TP, :],
                                             scalar=attn_t[:, t, bass.ds(expert, 1)], in1=h[:, t, :],
                                             op0=ALU.mult, op1=ALU.add).then_inc(tile_free, 1)

            for n in range(1, U):
                gather(n * T, n)
                split_expert(n + 2)
            with dve.Fori(1, EXPERTS // U - 1) as i:
                for u in range(U):
                    gather(i * (U * T) + u * T, i * U + u)
                    m = u + 2
                    dve.wait_ge(stage_hi, i * U + (PRE + m + 1))
                    minus_hi(split_w[u % 2][1][:, :, :], raw[m % U][:, :, :], split_w[u % 2][0][:, :, :])\
                        .then_inc(expert_split, 1)
            for n in range(EXPERTS - U, EXPERTS):
                gather(n * T, n)
                if n + 2 <= EXPERTS:
                    split_expert(n + 2)

            def tail_lo(i):
                dve.wait_ge(tail_hi, i + 1)
                minus_hi(acc_c[1][:, :, i * TW:i * TW + TP], transposed(tail_bank("aT", i))[:, :, 0:TP],
                         acc_c[0][:, :, i * TW:i * TW + TP]).then_inc(tail_free, 1)

            tail_lo(0)
            for i in range(T):
                if i + 1 < T:
                    tail_lo(i + 1)
                link(dve.tensor_tensor(scratch(i % 2)[0:TP, :], xm[:, i, :], out_b_row[:, :], ALU.add))
                dve.wait_ge(tail_full, tail_after("fo", i))
                dve.tensor_tensor(xm[:, i, :], tail_bank("fo", i)[0:TP, :], scratch(i % 2)[0:TP, :], ALU.add)\
                   .then_inc(out_ready, 1)

        @block.tensor
        def _(pe):
            def start_job(name):
                n = JOB[name]
                last = [m for m in range(n) if BANK[m] == BANK[n]]
                if last:
                    pe.wait_ge(bank_free, last[-1] + 1)
                return bank(*name)

            def three_pass(dest, lhs, rhs, start, stop, **more):
                pe.matmul(dest, lhs[0], rhs[0], start=start, stop=False, **more)
                pe.matmul(dest, lhs[1], rhs[0], start=False, stop=False, **more)
                return pe.matmul(dest, lhs[0], rhs[1], start=False, stop=stop, **more)

            def pair(p, *at):
                return [a[at] for a in p]

            def weights(s):
                return split_w[s % 2]

            def tile_product(dest, lhs_cols, i, w, start=True, stop=True):
                at = slice(i * TW, i * TW + TP)
                for k in range(K):
                    ins = three_pass(dest, pair(lhs_cols, slice(None), k, at), pair(w, slice(None), k),
                                     start and k == 0, stop and k == K - 1)
                return ins

            def transposes(job, source):
                b = transposed(start_job(job))
                for k in range(K):
                    ins = pe.transpose(b[:, k, 0:TP], source(k), ident[0:TP, 0:TP])
                ins.then_inc(bank_full, 1)

            pe.wait_ge(const_ready, 1)
            pe.wait_ge(cand_ready, 2)
            pe.transpose(start_job(("range", 0))[0:2 * T, 0:EG], cand[:, :, :].rearrange("p s b -> p (s b)"),
                         ident[0:EG, 0:EG]).then_inc(bank_full, 1)
            pe.wait_ge(edges_cast, 1)
            b = start_job(("edgeT", 0))
            for n in range(2):
                ins = pe.transpose(b[0:TP, n * EC:(n + 1) * EC], edges_f[:, n, :], ident[0:EC, 0:EC])
            ins.then_inc(bank_full, 1)
            pe.wait_ge(bank_free, after("range", 0))
            pe.transpose(start_job(("range", 1))[0:1, 0:2 * T], cand_max[:, :], ident[0:2 * T, 0:2 * T])\
              .then_inc(bank_full, 1)
            pe.wait_ge(bank_free, after("range", 1))
            taken = pe.alloc_register("onehots_taken")
            pe.reg_mov(taken, 0)
            pe.wait_ge(const_ready, 4)

            def count_block(b):
                groups = group_range(pe, b)
                if b >= 2:
                    pe.wait_ge(adj_split, b - 1)
                out_b = count_psum(b)
                flat = psum[0:TP, (4 + 2 * (b % 2)) * BW:(6 + 2 * (b % 2)) * BW]
                for at in (slice(0, BW), slice(BW, BW + OHW + 2)):
                    ins = pe.matmul(flat[:, at], zeros[:, 0:TP], zeros[:, 0:at.stop - at.start], start=True,
                                    stop=False, skip_group_check=True)
                if b == 0:
                    ins.then_inc(slots_free, OHR)
                with pe.Fori(*groups):
                    so_far = pe.snap(taken)
                    for u in range(OHR):
                        pe.wait_ge(onehots_ready, so_far + (u + 1))
                        for i in range(T):
                            ins = pe.matmul(out_b[:, i, :], onehot[0:TP, u, 0, i * OHW:i * OHW + TP],
                                            onehot[0:TP, u, 1, b * OHW:(b + 1) * OHW], start=False, stop=False,
                                            skip_group_check=True)
                        ins = pe.matmul(degree_psum(b), onehot[0:TP, u, 1, b * OHW:b * OHW + TP], ones_b[:, :],
                                        start=False, stop=False, skip_group_check=True)
                        ins.then_inc(slots_free, 1)
                    pe.reg_add(taken, taken, OHR)
                for at in (slice(0, BW), slice(BW, BW + OHW + 2)):
                    ins = pe.matmul(flat[:, at], zeros[:, 0:TP], zeros[:, 0:at.stop - at.start], start=False,
                                    stop=True, skip_group_check=True)
                ins.then_inc(counted, 1)

            def k_job(j):
                for name, at, last in (("kTa", slice(0, SA), 2), ("kTb", slice(SA, TT), T - 1)):
                    pe.wait_ge(bank_free, after("xrT", last))
                    b = start_job((name, j))
                    for k in range(K):
                        ins = three_pass(b[:, 0:at.stop - at.start],
                                         pair(weights(stage_k), slice(None), k, slice(128 * j, 128 * j + 128)),
                                         pair(xr_c, slice(None), k, at), k == 0, k == K - 1)
                    ins.then_inc(bank_full, 1)

            def project(job, i, s, lhs):
                ins = tile_product(start_job(job)[0:TP, :], lhs, i, weights(s))
                ins.then_inc(bank_full, 1)

            def turn_xr(i):
                pe.wait_ge(xr_ready, i + 1)
                transposes(("xrT", i), lambda k: xm[:, i, k::K])

            count_block(0)
            for i in range(T - 1):
                turn_xr(i)
            count_block(1)
            turn_xr(T - 1)
            pe.wait_ge(stage_split, stage_k + 1)
            k_job(0)
            count_block(2)
            k_job(1)
            count_block(3)
            k_job(2)
            count_block(4)
            k_job(3)
            pe.wait_ge(stage_split, stage_v + 1)
            for i in range(T):
                project(("v", i), i, stage_v, xr_c)
            pe.wait_ge(cnt_max_ready, 1)
            pe.transpose(start_job(("flag", 0))[0:1, 0:TP], cnt_max[:, :], ident[0:TP, 0:TP]).then_inc(bank_full, 1)
            pe.wait_ge(pos_sq_ready, 1)
            b = start_job(("p2", 0))
            for k in range(K):
                ins = pe.matmul(b[0:TP, 0:EXPERTS], ones[:, 0:TP], pos_sq[:, k, :], start=k == 0, stop=k == K - 1)
            ins.then_inc(bank_full, 1)
            for i in range(T):
                pe.wait_ge(k_exp_ready, J)
                b = start_job(("kN", i))
                for j in range(J):
                    ins = pe.transpose(b[0:TP, 128 * j:128 * j + 128], k_exp[:, j, i * TW:i * TW + TP], ident[:, :])
                ins.then_inc(bank_full, 1)
            b = start_job(("kM", 0))
            for j in range(J):
                ins = pe.transpose(b[0:NMEM, 128 * j:128 * j + 128], memk_exp[:, j, :], ident[:, :])
            ins.then_inc(bank_full, 1)
            pe.wait_ge(stage_split, stage_q + 1)
            for i in range(4):
                project(("q", i), i, stage_q, xr_c)
            pe.wait_ge(bank_free, after("kM", 0))
            pe.wait_ge(mem_loaded, 48)
            b = start_job(("ctx", 0))
            for j in range(J):
                at = slice(128 * j, 128 * j + 128)
                for i in range(T):
                    three_pass(b[:, at], pair(kn_r, slice(None), i, at), pair(v_r, slice(None), i, at), i == 0, False)
                ins = pe.matmul(b[:, at], memk_n[:, at], memv[:, at], start=False, stop=True)
            ins.then_inc(bank_full, 1)

            def turn_h(i):
                transposes(("hT", 0, i), lambda k: h[:, i, k::K])

            def turn_q(i):
                pe.wait_ge(q_ready, i + 1)
                transposes(("qT", i), lambda j: xm[:, i, 128 * j:128 * j + 128])

            def attend(name, at, last):
                pe.wait_ge(bank_free, after("qT", last))
                for j in range(J):
                    b = start_job((name, j))
                    three_pass(b[:, 0:at.stop - at.start], pair(ctx_hl, slice(None), j),
                               pair(q_c, slice(None), j, at), True, True).then_inc(bank_full, 1)

            turn_h(0)
            turn_h(1)
            turn_q(0)
            turn_q(1)
            turn_q(2)
            project(("q", 4), 4, stage_q, xr_c)
            pe.wait_ge(ctx_split, 1)
            attend("oTa", slice(0, SA), 2)
            turn_h(2)
            turn_q(3)
            turn_q(4)
            turn_h(3)
            attend("oTb", slice(SA, TT), T - 1)
            turn_h(4)
            pe.wait_ge(stage_split, stage_o + 1)
            def root_job(l, i):
                pe.wait_ge(bank_free, after("hT", l, i))
                tile_product(start_job(("zR", l, i))[0:TP, :], h_c, i, weights(stage_r(l))).then_inc(bank_full, 1)

            for i in range(T):
                pe.wait_ge(bank_free, after("oTa" if i < 3 else "oTb", J - 1))
                project(("mo", i), i, stage_o, o_c)
            def turn_x2(i):
                pe.wait_ge(x2n_ready, i + 1)
                transposes(("x2T", i), lambda k: h[:, i, k::K])

            pe.wait_ge(bank_free, after("flag", 0))
            has_low = pe.value_load(flag[0:1, 0:1], min_val=0, max_val=1)

            def sum_source(l, i):
                pe.wait_ge(h_split, T * l + i + 1)
                if i == T - 1:
                    with pe.If(has_low != 0):
                        for j in range(T):
                            for n, (chunks, at) in enumerate(SUMS):
                                for c, m in enumerate(chunks):
                                    width = at.stop - at.start
                                    pe.matmul(sum_bank(n)[:, c * width:(c + 1) * width], h_r[0][:, j, m::K],
                                              adj[1][:, j, at], start=False, stop=False, skip_group_check=True)
                for n, (chunks, at) in enumerate(SUMS):
                    for c, m in enumerate(chunks):
                        width = at.stop - at.start
                        for part in range(2):
                            ins = pe.matmul(sum_bank(n)[:, c * width:(c + 1) * width], h_r[part][:, i, m::K],
                                            adj[0][:, i, at], start=i == 0 and c == 0 and part == 0,
                                            stop=i == T - 1, skip_group_check=True)
                    if i == T - 1:
                        ins.then_inc(sums_full, 1)

            pe.wait_ge(stage_split, stage_r(0) + 1)
            root_job(0, 0)
            root_job(0, 1)
            pe.wait_ge(bank_free, after("mo", T - 1))
            for i in range(T):
                sum_source(0, i)
                if i == 0:
                    root_job(0, 2)
            for l in range(LAYERS):
                root_job(l, 3)
                root_job(l, 4)
                pe.wait_ge(stage_split, stage_l(l) + 1)
                pe.wait_ge(sums_free, len(SUMS) * (l + 1))

                def layer_tile(i):
                    tile_product(layer_bank(i)[0:TP, :], s_c, i, weights(stage_l(l))).then_inc(layer_full, 1)

                for i in range(T - 1):
                    layer_tile(i)
                if l + 1 == LAYERS:
                    layer_tile(T - 1)
                    turn_x2(0)
                else:
                    def turn(i):
                        pe.wait_ge(h_ready, T * l + i + 1)
                        transposes(("hT", l + 1, i), lambda k: h[:, i, k::K])

                    turn(0)
                    layer_tile(T - 1)
                    turn(1)
                    pe.wait_ge(stage_split, stage_r(l + 1) + 1)
                    pe.wait_ge(layer_free, T * (l + 1))
                    sum_source(l + 1, 0)
                    root_job(l + 1, 0)
                    root_job(l + 1, 1)
                    sum_source(l + 1, 1)
                    turn(2)
                    sum_source(l + 1, 2)
                    root_job(l + 1, 2)
                    turn(3)
                    sum_source(l + 1, 3)
                    turn(4)
                    sum_source(l + 1, 4)

            def dots(b, i):
                pe.wait_ge(bank_free, after("x2T", i))
                at = slice(i * TW, i * TW + TP)
                for k in range(K):
                    ins = three_pass(b, pair(x2_c, slice(None), k, at), pair(pos_hl, slice(None), k),
                                     k == 0, k == K - 1)
                return ins

            def dots_early(i):
                ins = dots(dots_bank[0:TP, i * EXPERTS:(i + 1) * EXPERTS], i)
                if i == T - 2:
                    ins.then_inc(dots_full, 1)

            def expert_tile(slot, t):
                tile_product(expert_bank(t)[0:TP, :], x2_c, t, weights(slot)).then_inc(tile_full, 1)

            pe.wait_ge(pos_split, 1)
            dots_early(0)
            pe.wait_ge(layer_free, T * LAYERS)
            pe.wait_ge(stage_split, PRE + 1)
            for i in range(1, T):
                turn_x2(i)
                expert_tile(0, i - 1)
                if i < T - 1:
                    dots_early(i)
            dots(start_job(("d", 1))[0:TP, 0:EXPERTS], T - 1).then_inc(bank_full, 1)
            expert_tile(0, T - 1)
            for n in range(1, U):
                if n < BY_DVE:
                    pe.wait_ge(stage_split, PRE + n + 1)
                else:
                    pe.wait_ge(expert_split, n - BY_DVE + 1)
                for t in range(T):
                    if n == 1:
                        pe.wait_ge(first_taken, t + 1)
                    else:
                        pe.wait_ge(tile_free, T * (n - 1) + t + 1)
                    expert_tile(n, t)
            with pe.Fori(1, EXPERTS // U) as it:
                for u in range(U):
                    pe.wait_ge(expert_split, it * U + (u - BY_DVE + 1))
                    for t in range(T):
                        pe.wait_ge(tile_free, it * (U * T) + ((u - 1) * T + t + 1))
                        expert_tile(u, t)

            def tail_transposes(i):
                pe.wait_ge(tile_free, T * (EXPERTS - 1) + i + 1)
                b = transposed(tail_bank("aT", i))
                for k in range(K):
                    ins = pe.transpose(b[:, k, 0:TP], h[:, i, k::K], ident[0:TP, 0:TP])
                ins.then_inc(tail_full, 1)

            tail_transposes(0)
            pe.wait_ge(expert_split, EXPERTS - BY_DVE + 1)
            for i in range(T):
                if i + 1 < T:
                    tail_transposes(i + 1)
                pe.wait_ge(tail_free, i + 1)
                tile_product(tail_bank("fo", i)[0:TP, :], acc_c, i, weights(stage_out)).then_inc(tail_full, 1)


def kernel(**inputs):
    import numpy as np
    import concourse.bacc as bacc
    from concourse.bass_utils import run_bass_kernel_spmd

    nc = bacc.Bacc("TRN2", target_bir_lowering=False, num_devices=1)
    arrays = {}

    def dram(name, array):
        array = np.ascontiguousarray(array)
        arrays[name] = array
        return nc.dram_tensor(name, array.shape, mybir.dt.from_np(array.dtype), kind="ExternalInput").ap()

    def given(name):
        return dram(name, inputs[name])

    def turned(name):
        return dram(name + "_t", np.asarray(inputs[name]).T)

    layers = range(3)
    heads, dim, slots = inputs["L0_mix_mem_kv"].shape[1:]
    mem_kv = np.asarray(inputs["L0_mix_mem_kv"]).reshape(2, heads * dim, slots)
    nodes, features = inputs["x"].shape
    out = nc.dram_tensor("out", (nodes, features), F32, kind="ExternalOutput").ap()
    gps_kernel(
        nc, given("x"), given("src"), given("dst"),
        [(turned(f"L0_gnn_Wl{l}"), turned(f"L0_gnn_Wr{l}")) for l in layers],
        [[given(f"L0_gnn_{row}{l}") for row in ("bl", "g", "b")] for l in layers],
        given("L0_gnn_a_prelu"),
        dram("norm_w", np.asarray(inputs["L0_mix_norm_w"]).reshape(-1)),
        given("L0_mix_w_qkv"), dram("mem_k", mem_kv[0]), dram("mem_v", mem_kv[1].T),
        given("L0_mix_w_out"), given("L0_mix_b_out"),
        dram("out_norm_w", np.asarray(inputs["L0_mix_out_norm_w"]).reshape(-1)),
        turned("L0_ffn_positions"), given("L0_ffn_scales"), given("L0_ffn_value_weight"),
        turned("L0_ffn_out_W"), given("L0_ffn_out_b"), out)
    result = run_bass_kernel_spmd(nc, [arrays], core_ids=[0])
    return result.results[0]["out"]
```
